# Optimizing a Trainium2 kernel written in Bass

```python
import numpy as np
import jax
import jax.numpy as jnp

def _softmax(x, axis=-1):
    return jax.nn.softmax(x, axis=axis)

def _gelu(x):
    return jax.nn.gelu(x, approximate=True)

def _silu(x):
    return jax.nn.silu(x)

def _sigmoid(x):
    return jax.nn.sigmoid(x)

def _layernorm(x, axis=-1, eps=1e-05):
    m = jnp.mean(x, axis=axis, keepdims=True)
    v = jnp.var(x, axis=axis, keepdims=True)
    return (x - m) / jnp.sqrt(v + eps)

def _scatter_add(tgt, idx, src, axis=0):
    return tgt.at[idx].add(src)

def _segment_sum(src, seg, n):
    return jax.ops.segment_sum(src, seg, n)
kernel_name = 'mk_vit_tower_cls_d2_tok_img512_r4_4c1adf'

def setup_inputs(seed: int=0):
    np.random.seed(seed)
    _w = jnp.asarray

    def _rec_inputs():
        import jax
        import jax.numpy as jnp
        _rk = jax.random.key(seed)
        x = -0.000356955 + 1 * jax.random.normal(jax.random.fold_in(_rk, 1), (64, 3, 224, 224), jnp.float32)
        cls_tok = 0.02 * jax.random.normal(jax.random.fold_in(_rk, 5), (1, 1, 128), jnp.float32)
        return (x, cls_tok)
    x, cls_tok = _rec_inputs()

    def _L0_tok_setup():
        import jax, jax.numpy as jnp
        import numpy as np
        P = 16
        SHIFT = P // 2
        EPS = 1e-05

        def _shift2d(img, dy, dx):
            H, W = (img.shape[2], img.shape[3])
            pad = ((0, 0), (0, 0), (max(dy, 0), max(-dy, 0)), (max(dx, 0), max(-dx, 0)))
            z = jnp.pad(img, pad)
            return z[:, :, max(-dy, 0):max(-dy, 0) + H, max(-dx, 0):max(-dx, 0) + W]

        def _patchify(img):
            B, C, H, W = img.shape
            nH, nW = (H // P, W // P)
            t = img.reshape(B, C, nH, P, nW, P).transpose(0, 2, 4, 1, 3, 5)
            return t.reshape(B, nH * nW, C * P * P)
        key = jax.random.key(seed)
        ks = jax.random.split(key, 8)
        B, C, H, Wd = (128, 3, 224, 224)
        embed_dim = 128
        d_main = embed_dim // 2
        d_shift = embed_dim // 8
        fan_in = C * P * P
        std = 0.02
        x = jax.random.normal(ks[0], (B, C, H, Wd), dtype=jnp.float32)
        W_main = jax.random.normal(ks[1], (d_main, fan_in), dtype=jnp.float32) * std
        b_main = jnp.zeros((d_main,), dtype=jnp.float32)
        W_sx = jax.random.normal(ks[2], (d_shift, fan_in), dtype=jnp.float32) * std
        b_sx = jnp.zeros((d_shift,), dtype=jnp.float32)
        W_sy = jax.random.normal(ks[3], (d_shift, fan_in), dtype=jnp.float32) * std
        b_sy = jnp.zeros((d_shift,), dtype=jnp.float32)
        ln_g = jnp.ones((embed_dim,), dtype=jnp.float32)
        ln_b = jnp.zeros((embed_dim,), dtype=jnp.float32)
        return {'x': x, 'W_main': W_main, 'b_main': b_main, 'W_sx': W_sx, 'b_sx': b_sx, 'W_sy': W_sy, 'b_sy': b_sy, 'ln_g': ln_g, 'ln_b': ln_b}
    _L0_tok_all = _L0_tok_setup()
    _L0_tok_in = {k: v for k, v in _L0_tok_all.items() if k in ('W_main', 'b_main', 'W_sx', 'b_sx', 'W_sy', 'b_sy', 'ln_g', 'ln_b')}
    del _L0_tok_all

    def _L0_attn_setup():
        import jax, jax.numpy as jnp
        import numpy as np
        D_MODEL = 128
        D_FF = 512
        D_STATE = 16
        D_CONV = 4
        EXPAND = 2
        D_INNER = EXPAND * D_MODEL
        DT_RANK = (D_MODEL + 15) // 16
        EPS = 1e-05

        def silu(x):
            return x * jax.nn.sigmoid(x)

        def layernorm(x, g, b):
            mu = jnp.mean(x, axis=-1, keepdims=True)
            var = jnp.mean(jnp.square(x - mu), axis=-1, keepdims=True)
            return (x - mu) * jax.lax.rsqrt(var + EPS) * g + b

        def mamba_block(x, in_w, conv_w, conv_b, xproj_w, dt_w, dt_b, A_log, Dp, out_w):
            Bsz, L, _ = x.shape
            di = conv_w.shape[0]
            k = conv_w.shape[1]
            n = A_log.shape[1]
            r = dt_w.shape[1]
            xz = x @ in_w.T
            xi, z = jnp.split(xz, 2, axis=-1)
            xt = jnp.transpose(xi, (0, 2, 1))
            xt = jnp.pad(xt, ((0, 0), (0, 0), (k - 1, 0)))
            xc = jax.lax.conv_general_dilated(xt, conv_w[:, None, :], (1,), 'VALID', feature_group_count=di, dimension_numbers=('NCH', 'OIH', 'NCH'))
            xc = silu(xc + conv_b[None, :, None])
            xc = jnp.transpose(xc, (0, 2, 1))
            dbc = xc @ xproj_w.T
            dt = jax.nn.softplus(dbc[..., :r] @ dt_w.T + dt_b)
            Bm = dbc[..., r:r + n]
            Cm = dbc[..., r + n:]
            A = -jnp.exp(A_log)

            def step(h, inp):
                dt_t, B_t, C_t, x_t = inp
                dA = jnp.exp(dt_t[..., None] * A)
                h = dA * h + (dt_t * x_t)[..., None] * B_t[:, None, :]
                y = jnp.einsum('bdn,bn->bd', h, C_t)
                return (h, y)
            xs = (jnp.moveaxis(dt, 1, 0), jnp.moveaxis(Bm, 1, 0), jnp.moveaxis(Cm, 1, 0), jnp.moveaxis(xc, 1, 0))
            h0 = jnp.zeros((Bsz, di, n), x.dtype)
            _, ys = jax.lax.scan(step, h0, xs)
            y = jnp.moveaxis(ys, 0, 1) + xc * Dp
            y = y * silu(z)
            return y @ out_w.T
        key = jax.random.key(seed)
        ks = iter(jax.random.split(key, 40))
        s = 0.02

        def mamba_params():
            return dict(in_w=jax.random.normal(next(ks), (2 * D_INNER, D_MODEL), jnp.float32) * s, conv_w=jax.random.normal(next(ks), (D_INNER, D_CONV), jnp.float32) * 0.3, conv_b=jnp.zeros((D_INNER,), jnp.float32), xproj_w=jax.random.normal(next(ks), (DT_RANK + 2 * D_STATE, D_INNER), jnp.float32) * s, dt_w=jax.random.normal(next(ks), (D_INNER, DT_RANK), jnp.float32) * 0.1, dt_b=jax.random.uniform(next(ks), (D_INNER,), jnp.float32, -4.0, -2.0), A_log=jnp.tile(jnp.log(jnp.arange(1, D_STATE + 1, dtype=jnp.float32)), (D_INNER, 1)), D=jnp.ones((D_INNER,), jnp.float32), out_w=jax.random.normal(next(ks), (D_MODEL, D_INNER), jnp.float32) * s)
        pf = mamba_params()
        pb = mamba_params()
        inp = dict(x=jax.random.normal(next(ks), (8, 1024, D_MODEL), jnp.float32), f_in_w=pf['in_w'], f_conv_w=pf['conv_w'], f_conv_b=pf['conv_b'], f_xproj_w=pf['xproj_w'], f_dt_w=pf['dt_w'], f_dt_b=pf['dt_b'], f_A_log=pf['A_log'], f_D=pf['D'], f_out_w=pf['out_w'], b_in_w=pb['in_w'], b_conv_w=pb['conv_w'], b_conv_b=pb['conv_b'], b_xproj_w=pb['xproj_w'], b_dt_w=pb['dt_w'], b_dt_b=pb['dt_b'], b_A_log=pb['A_log'], b_D=pb['D'], b_out_w=pb['out_w'], ln_f_g=jnp.ones((D_MODEL,), jnp.float32), ln_f_b=jnp.zeros((D_MODEL,), jnp.float32), ln_b_g=jnp.ones((D_MODEL,), jnp.float32), ln_b_b=jnp.zeros((D_MODEL,), jnp.float32), ln_ff_g=jnp.ones((D_MODEL,), jnp.float32), ln_ff_b=jnp.zeros((D_MODEL,), jnp.float32), ffn_w1=jax.random.normal(next(ks), (D_FF, D_MODEL), jnp.float32) * s, ffn_b1=jnp.zeros((D_FF,), jnp.float32), ffn_w2=jax.random.normal(next(ks), (D_MODEL, D_FF), jnp.float32) * s, ffn_b2=jnp.zeros((D_MODEL,), jnp.float32))
        return inp
    _L0_attn_all = _L0_attn_setup()
    _L0_attn_in = {k: v for k, v in _L0_attn_all.items() if k in ('f_in_w', 'f_conv_w', 'f_conv_b', 'f_xproj_w', 'f_dt_w', 'f_dt_b', 'f_A_log', 'f_D', 'f_out_w', 'b_in_w', 'b_conv_w', 'b_conv_b', 'b_xproj_w', 'b_dt_w', 'b_dt_b', 'b_A_log', 'b_D', 'b_out_w', 'ln_f_g', 'ln_f_b', 'ln_b_g', 'ln_b_b', 'ln_ff_g', 'ln_ff_b', 'ffn_w1', 'ffn_b1', 'ffn_w2', 'ffn_b2')}
    del _L0_attn_all

    def _L0_ffn_setup():
        import jax, jax.numpy as jnp
        import numpy as np
        N_CONST = 6
        PARTITIONS_OF_6 = [(6,), (5, 1), (4, 2), (4, 1, 1), (3, 3), (3, 2, 1), (3, 1, 1, 1), (2, 2, 2), (2, 2, 1, 1), (2, 1, 1, 1, 1), (1, 1, 1, 1, 1, 1)]
        N_EXPERTS = 6
        TOP_K = 2

        def _partition_weights():
            w = np.zeros((len(PARTITIONS_OF_6), N_EXPERTS), dtype=np.float32)
            for i, partition in enumerate(PARTITIONS_OF_6):
                for j, part in enumerate(partition):
                    if j < N_EXPERTS:
                        w[i, j] = part / N_CONST
            return jnp.asarray(w)
        key = jax.random.key(seed)
        ks = jax.random.split(key, 6)
        B, S, D, F, E, P = (32, 512, 128, 341, 6, 11)
        scale_in = 1.0 / np.sqrt(D)
        scale_hid = 1.0 / np.sqrt(F)
        return {'x': jax.random.normal(ks[0], (B, S, D), dtype=jnp.float32), 'router_w': jax.random.normal(ks[1], (P, D), dtype=jnp.float32) * scale_in, 'W1': jax.random.normal(ks[2], (E, D, F), dtype=jnp.float32) * scale_in, 'b1': jax.random.normal(ks[3], (E, F), dtype=jnp.float32) * 0.01, 'W2': jax.random.normal(ks[4], (E, F, D), dtype=jnp.float32) * scale_hid, 'b2': jax.random.normal(ks[5], (E, D), dtype=jnp.float32) * 0.01}
    _L0_ffn_all = _L0_ffn_setup()
    _L0_ffn_in = {k: v for k, v in _L0_ffn_all.items() if k in ('router_w', 'W1', 'b1', 'W2', 'b2')}
    del _L0_ffn_all

    def _L1_attn_setup():
        import jax, jax.numpy as jnp
        import numpy as np
        B, L, D, MODES = (32, 1024, 128, 64)
        key = jax.random.key(seed)
        k_q, k_wr, k_wi = jax.random.split(key, 3)
        scale = 1.0 / (D * D)
        q = jax.random.normal(k_q, (B, L, D), dtype=jnp.float32)
        weights_real = scale * jax.random.normal(k_wr, (D, D, MODES), dtype=jnp.float32)
        weights_imag = scale * jax.random.normal(k_wi, (D, D, MODES), dtype=jnp.float32)
        return {'q': q, 'weights_real': weights_real, 'weights_imag': weights_imag}
    _L1_attn_all = _L1_attn_setup()
    _L1_attn_in = {k: v for k, v in _L1_attn_all.items() if k in ('weights_real', 'weights_imag')}
    del _L1_attn_all

    def _L1_ffn_setup():
        import jax, jax.numpy as jnp
        import numpy as np
        MARK_AX, OP_ADD, OP_SUB = (0, 1, 2)
        ALU_LO, ALU_HI = (16, 32)
        AX_CARRY_LO, AX_CARRY_HI = (48, 64)
        OPCODE_BASE = 80
        OUTPUT_LO, OUTPUT_HI, CARRY = (128, 144, 160)
        NIB_A, NIB_B, OP_START = (0, 1, 10)
        RESULT, CARRY_OUT = (100, 101)
        GE_POS, GE_DIM = (8, 160)
        OPC_ADD, OPC_SUB = (25, 26)
        B, S, D = (8, 1024, 128)

        def _decode_nibble(x, base):
            return jnp.argmax(x[..., base:base + 16] > 0.5, axis=-1).astype(x.dtype)

        def _pipeline(h, W, b):
            for i in range(3):
                h = jnp.einsum('bspd,od->bspo', h, W[i]) + b[i]
                if i < 2:
                    h = jax.nn.relu(h)
            return h
        key = jax.random.key(seed)
        kx, k1, k2, k3, k4 = jax.random.split(key, 5)
        x_bd = jax.random.uniform(kx, (B, S, D), dtype=jnp.float32)
        Wa = jax.random.normal(k1, (3, GE_DIM, GE_DIM), dtype=jnp.float32) * 0.05
        ba = jax.random.normal(k2, (3, GE_DIM), dtype=jnp.float32) * 0.05
        Ws = jax.random.normal(k3, (3, GE_DIM, GE_DIM), dtype=jnp.float32) * 0.05
        bs = jax.random.normal(k4, (3, GE_DIM), dtype=jnp.float32) * 0.05
        return {'x_bd': x_bd, 'Wa': Wa, 'ba': ba, 'Ws': Ws, 'bs': bs}
    _L1_ffn_all = _L1_ffn_setup()
    _L1_ffn_in = {k: v for k, v in _L1_ffn_all.items() if k in ('Wa', 'ba', 'Ws', 'bs')}
    del _L1_ffn_all
    return {'x': x, 'cls_tok': cls_tok, 'L0_tok_W_main': _L0_tok_in['W_main'], 'L0_tok_b_main': _L0_tok_in['b_main'], 'L0_tok_W_sx': _L0_tok_in['W_sx'], 'L0_tok_b_sx': _L0_tok_in['b_sx'], 'L0_tok_W_sy': _L0_tok_in['W_sy'], 'L0_tok_b_sy': _L0_tok_in['b_sy'], 'L0_tok_ln_g': _L0_tok_in['ln_g'], 'L0_tok_ln_b': _L0_tok_in['ln_b'], 'L0_attn_f_in_w': _L0_attn_in['f_in_w'], 'L0_attn_f_conv_w': _L0_attn_in['f_conv_w'], 'L0_attn_f_conv_b': _L0_attn_in['f_conv_b'], 'L0_attn_f_xproj_w': _L0_attn_in['f_xproj_w'], 'L0_attn_f_dt_w': _L0_attn_in['f_dt_w'], 'L0_attn_f_dt_b': _L0_attn_in['f_dt_b'], 'L0_attn_f_A_log': _L0_attn_in['f_A_log'], 'L0_attn_f_D': _L0_attn_in['f_D'], 'L0_attn_f_out_w': _L0_attn_in['f_out_w'], 'L0_attn_b_in_w': _L0_attn_in['b_in_w'], 'L0_attn_b_conv_w': _L0_attn_in['b_conv_w'], 'L0_attn_b_conv_b': _L0_attn_in['b_conv_b'], 'L0_attn_b_xproj_w': _L0_attn_in['b_xproj_w'], 'L0_attn_b_dt_w': _L0_attn_in['b_dt_w'], 'L0_attn_b_dt_b': _L0_attn_in['b_dt_b'], 'L0_attn_b_A_log': _L0_attn_in['b_A_log'], 'L0_attn_b_D': _L0_attn_in['b_D'], 'L0_attn_b_out_w': _L0_attn_in['b_out_w'], 'L0_attn_ln_f_g': _L0_attn_in['ln_f_g'], 'L0_attn_ln_f_b': _L0_attn_in['ln_f_b'], 'L0_attn_ln_b_g': _L0_attn_in['ln_b_g'], 'L0_attn_ln_b_b': _L0_attn_in['ln_b_b'], 'L0_attn_ln_ff_g': _L0_attn_in['ln_ff_g'], 'L0_attn_ln_ff_b': _L0_attn_in['ln_ff_b'], 'L0_attn_ffn_w1': _L0_attn_in['ffn_w1'], 'L0_attn_ffn_b1': _L0_attn_in['ffn_b1'], 'L0_attn_ffn_w2': _L0_attn_in['ffn_w2'], 'L0_attn_ffn_b2': _L0_attn_in['ffn_b2'], 'L0_ffn_router_w': _L0_ffn_in['router_w'], 'L0_ffn_W1': _L0_ffn_in['W1'], 'L0_ffn_b1': _L0_ffn_in['b1'], 'L0_ffn_W2': _L0_ffn_in['W2'], 'L0_ffn_b2': _L0_ffn_in['b2'], 'L1_attn_weights_real': _L1_attn_in['weights_real'], 'L1_attn_weights_imag': _L1_attn_in['weights_imag'], 'L1_ffn_Wa': _L1_ffn_in['Wa'], 'L1_ffn_ba': _L1_ffn_in['ba'], 'L1_ffn_Ws': _L1_ffn_in['Ws'], 'L1_ffn_bs': _L1_ffn_in['bs']}

def reference(x, cls_tok, L0_tok_W_main, L0_tok_b_main, L0_tok_W_sx, L0_tok_b_sx, L0_tok_W_sy, L0_tok_b_sy, L0_tok_ln_g, L0_tok_ln_b, L0_attn_f_in_w, L0_attn_f_conv_w, L0_attn_f_conv_b, L0_attn_f_xproj_w, L0_attn_f_dt_w, L0_attn_f_dt_b, L0_attn_f_A_log, L0_attn_f_D, L0_attn_f_out_w, L0_attn_b_in_w, L0_attn_b_conv_w, L0_attn_b_conv_b, L0_attn_b_xproj_w, L0_attn_b_dt_w, L0_attn_b_dt_b, L0_attn_b_A_log, L0_attn_b_D, L0_attn_b_out_w, L0_attn_ln_f_g, L0_attn_ln_f_b, L0_attn_ln_b_g, L0_attn_ln_b_b, L0_attn_ln_ff_g, L0_attn_ln_ff_b, L0_attn_ffn_w1, L0_attn_ffn_b1, L0_attn_ffn_w2, L0_attn_ffn_b2, L0_ffn_router_w, L0_ffn_W1, L0_ffn_b1, L0_ffn_W2, L0_ffn_b2, L1_attn_weights_real, L1_attn_weights_imag, L1_ffn_Wa, L1_ffn_ba, L1_ffn_Ws, L1_ffn_bs):
    import jax
    import jax.numpy as jnp

    def _L0_tok_ref(x, W_main, b_main, W_sx, b_sx, W_sy, b_sy, ln_g, ln_b):
        import jax, jax.numpy as jnp
        import numpy as np
        P = 16
        SHIFT = P // 2
        EPS = 1e-05

        def _shift2d(img, dy, dx):
            H, W = (img.shape[2], img.shape[3])
            pad = ((0, 0), (0, 0), (max(dy, 0), max(-dy, 0)), (max(dx, 0), max(-dx, 0)))
            z = jnp.pad(img, pad)
            return z[:, :, max(-dy, 0):max(-dy, 0) + H, max(-dx, 0):max(-dx, 0) + W]

        def _patchify(img):
            B, C, H, W = img.shape
            nH, nW = (H // P, W // P)
            t = img.reshape(B, C, nH, P, nW, P).transpose(0, 2, 4, 1, 3, 5)
            return t.reshape(B, nH * nW, C * P * P)

        def proj(img, W, b):
            return jnp.einsum('bnf,of->bno', _patchify(img), W) + b
        main = proj(x, W_main, b_main)
        xl = proj(_shift2d(x, 0, -SHIFT), W_sx, b_sx)
        xr = proj(_shift2d(x, 0, SHIFT), W_sx, b_sx)
        yu = proj(_shift2d(x, -SHIFT, 0), W_sy, b_sy)
        yd = proj(_shift2d(x, SHIFT, 0), W_sy, b_sy)
        tok = jnp.concatenate([main, xl, xr, yu, yd], axis=-1)
        mu = jnp.mean(tok, axis=-1, keepdims=True)
        var = jnp.mean(jnp.square(tok - mu), axis=-1, keepdims=True)
        return (tok - mu) * jax.lax.rsqrt(var + EPS) * ln_g + ln_b

    def _L0_attn_ref(x, f_in_w, f_conv_w, f_conv_b, f_xproj_w, f_dt_w, f_dt_b, f_A_log, f_D, f_out_w, b_in_w, b_conv_w, b_conv_b, b_xproj_w, b_dt_w, b_dt_b, b_A_log, b_D, b_out_w, ln_f_g, ln_f_b, ln_b_g, ln_b_b, ln_ff_g, ln_ff_b, ffn_w1, ffn_b1, ffn_w2, ffn_b2):
        import jax, jax.numpy as jnp
        import numpy as np
        D_MODEL = 128
        D_FF = 512
        D_STATE = 16
        D_CONV = 4
        EXPAND = 2
        D_INNER = EXPAND * D_MODEL
        DT_RANK = (D_MODEL + 15) // 16
        EPS = 1e-05

        def silu(x):
            return x * jax.nn.sigmoid(x)

        def layernorm(x, g, b):
            mu = jnp.mean(x, axis=-1, keepdims=True)
            var = jnp.mean(jnp.square(x - mu), axis=-1, keepdims=True)
            return (x - mu) * jax.lax.rsqrt(var + EPS) * g + b

        def mamba_block(x, in_w, conv_w, conv_b, xproj_w, dt_w, dt_b, A_log, Dp, out_w):
            Bsz, L, _ = x.shape
            di = conv_w.shape[0]
            k = conv_w.shape[1]
            n = A_log.shape[1]
            r = dt_w.shape[1]
            xz = x @ in_w.T
            xi, z = jnp.split(xz, 2, axis=-1)
            xt = jnp.transpose(xi, (0, 2, 1))
            xt = jnp.pad(xt, ((0, 0), (0, 0), (k - 1, 0)))
            xc = jax.lax.conv_general_dilated(xt, conv_w[:, None, :], (1,), 'VALID', feature_group_count=di, dimension_numbers=('NCH', 'OIH', 'NCH'))
            xc = silu(xc + conv_b[None, :, None])
            xc = jnp.transpose(xc, (0, 2, 1))
            dbc = xc @ xproj_w.T
            dt = jax.nn.softplus(dbc[..., :r] @ dt_w.T + dt_b)
            Bm = dbc[..., r:r + n]
            Cm = dbc[..., r + n:]
            A = -jnp.exp(A_log)

            def step(h, inp):
                dt_t, B_t, C_t, x_t = inp
                dA = jnp.exp(dt_t[..., None] * A)
                h = dA * h + (dt_t * x_t)[..., None] * B_t[:, None, :]
                y = jnp.einsum('bdn,bn->bd', h, C_t)
                return (h, y)
            xs = (jnp.moveaxis(dt, 1, 0), jnp.moveaxis(Bm, 1, 0), jnp.moveaxis(Cm, 1, 0), jnp.moveaxis(xc, 1, 0))
            h0 = jnp.zeros((Bsz, di, n), x.dtype)
            _, ys = jax.lax.scan(step, h0, xs)
            y = jnp.moveaxis(ys, 0, 1) + xc * Dp
            y = y * silu(z)
            return y @ out_w.T
        mf = mamba_block(x, f_in_w, f_conv_w, f_conv_b, f_xproj_w, f_dt_w, f_dt_b, f_A_log, f_D, f_out_w)
        out_f = layernorm(x + mf, ln_f_g, ln_f_b)
        mb = mamba_block(jnp.flip(x, axis=1), b_in_w, b_conv_w, b_conv_b, b_xproj_w, b_dt_w, b_dt_b, b_A_log, b_D, b_out_w)
        out_b = jnp.flip(mb, axis=1)
        h = 0.5 * (out_f + layernorm(x + out_b, ln_b_g, ln_b_b))
        ff = jax.nn.gelu(h @ ffn_w1.T + ffn_b1) @ ffn_w2.T + ffn_b2
        return layernorm(h + ff, ln_ff_g, ln_ff_b)

    def _L0_ffn_ref(x, router_w, W1, b1, W2, b2):
        import jax, jax.numpy as jnp
        import numpy as np
        N_CONST = 6
        PARTITIONS_OF_6 = [(6,), (5, 1), (4, 2), (4, 1, 1), (3, 3), (3, 2, 1), (3, 1, 1, 1), (2, 2, 2), (2, 2, 1, 1), (2, 1, 1, 1, 1), (1, 1, 1, 1, 1, 1)]
        N_EXPERTS = 6
        TOP_K = 2

        def _partition_weights():
            w = np.zeros((len(PARTITIONS_OF_6), N_EXPERTS), dtype=np.float32)
            for i, partition in enumerate(PARTITIONS_OF_6):
                for j, part in enumerate(partition):
                    if j < N_EXPERTS:
                        w[i, j] = part / N_CONST
            return jnp.asarray(w)
        pw = _partition_weights()
        token_repr = x.mean(axis=1)
        logits = token_repr @ router_w.T
        probs = jax.nn.softmax(logits, axis=-1)
        topk_vals, topk_idx = jax.lax.top_k(probs, TOP_K)
        topk_vals = topk_vals / topk_vals.sum(axis=-1, keepdims=True)
        expert_weights = jnp.einsum('bk,bke->be', topk_vals, pw[topk_idx])
        expert_weights = jnp.where(expert_weights > 1e-06, expert_weights, 0.0)
        h = jax.nn.gelu(jnp.einsum('bsd,edf->ebsf', x, W1) + b1[:, None, None, :], approximate=False)
        out_e = jnp.einsum('ebsf,efd->ebsd', h, W2) + b2[:, None, None, :]
        return jnp.einsum('be,ebsd->bsd', expert_weights, out_e)

    def _L1_attn_ref(q, weights_real, weights_imag):
        import jax, jax.numpy as jnp
        import numpy as np
        B, L, D, MODES = (32, 1024, 128, 64)
        Bq, Lq, Dq = q.shape
        n_freq = Lq // 2 + 1
        q_ft = jnp.fft.rfft(q, axis=1)
        modes = min(weights_real.shape[-1], n_freq)
        w = weights_real[:, :, :modes] + 1j * weights_imag[:, :, :modes]
        out_modes = jnp.einsum('bmd,dem->bme', q_ft[:, :modes, :], w)
        out_ft = jnp.zeros((Bq, n_freq, Dq), dtype=out_modes.dtype).at[:, :modes, :].set(out_modes)
        out = jnp.fft.irfft(out_ft, n=Lq, axis=1)
        return out

    def _L1_ffn_ref(x_bd, Wa, ba, Ws, bs):
        import jax, jax.numpy as jnp
        import numpy as np
        MARK_AX, OP_ADD, OP_SUB = (0, 1, 2)
        ALU_LO, ALU_HI = (16, 32)
        AX_CARRY_LO, AX_CARRY_HI = (48, 64)
        OPCODE_BASE = 80
        OUTPUT_LO, OUTPUT_HI, CARRY = (128, 144, 160)
        NIB_A, NIB_B, OP_START = (0, 1, 10)
        RESULT, CARRY_OUT = (100, 101)
        GE_POS, GE_DIM = (8, 160)
        OPC_ADD, OPC_SUB = (25, 26)
        B, S, D = (8, 1024, 128)

        def _decode_nibble(x, base):
            return jnp.argmax(x[..., base:base + 16] > 0.5, axis=-1).astype(x.dtype)

        def _pipeline(h, W, b):
            for i in range(3):
                h = jnp.einsum('bspd,od->bspo', h, W[i]) + b[i]
                if i < 2:
                    h = jax.nn.relu(h)
            return h
        x = x_bd
        Bsz, seq, _ = x.shape
        x_ge = jnp.zeros((Bsz, seq, GE_POS, GE_DIM), dtype=x.dtype)
        x_ge = x_ge.at[..., 0, NIB_A].set(_decode_nibble(x, ALU_LO))
        x_ge = x_ge.at[..., 1, NIB_A].set(_decode_nibble(x, ALU_HI))
        x_ge = x_ge.at[..., 0, NIB_B].set(_decode_nibble(x, AX_CARRY_LO))
        x_ge = x_ge.at[..., 1, NIB_B].set(_decode_nibble(x, AX_CARRY_HI))
        x_ge = x_ge.at[..., :, OP_START + OPC_ADD].set(x[..., OPCODE_BASE + OPC_ADD][..., None])
        x_ge = x_ge.at[..., :, OP_START + OPC_SUB].set(x[..., OPCODE_BASE + OPC_SUB][..., None])
        mark = x[..., MARK_AX] > 0.5
        m_add = mark & (x[..., OP_ADD] > 0.5)
        m_sub = mark & ~(x[..., OP_ADD] > 0.5) & (x[..., OP_SUB] > 0.5)
        active = (m_add | m_sub).astype(x.dtype)
        y_add = _pipeline(x_ge, Wa, ba)
        y_sub = _pipeline(x_ge, Ws, bs)
        y = jnp.where(m_add[..., None, None], y_add, jnp.where(m_sub[..., None, None], y_sub, x_ge))
        res_lo = jnp.clip(jnp.round(y[..., 0, RESULT]), 0, 15).astype(jnp.int32)
        res_hi = jnp.clip(jnp.round(y[..., 1, RESULT]), 0, 15).astype(jnp.int32)
        oh_lo = jax.nn.one_hot(res_lo, 16, dtype=x.dtype) * active[..., None]
        oh_hi = jax.nn.one_hot(res_hi, 16, dtype=x.dtype) * active[..., None]
        carry = (jnp.round(y[..., 1, CARRY_OUT]) > 0.5).astype(x.dtype) * active
        out = x
        out = out.at[..., OUTPUT_LO:OUTPUT_LO + 16].add(2.0 * oh_lo)
        out = out.at[..., OUTPUT_HI:OUTPUT_HI + 16].add(2.0 * oh_hi)
        out = out.at[..., CARRY].add(carry)
        return out
    h = _L0_tok_ref(x, L0_tok_W_main, L0_tok_b_main, L0_tok_W_sx, L0_tok_b_sx, L0_tok_W_sy, L0_tok_b_sy, L0_tok_ln_g, L0_tok_ln_b)
    h = jnp.concatenate([jnp.broadcast_to(cls_tok, (h.shape[0], 1, h.shape[2])), h], axis=1)
    h = h + _L0_attn_ref(_layernorm(h, axis=-1), L0_attn_f_in_w, L0_attn_f_conv_w, L0_attn_f_conv_b, L0_attn_f_xproj_w, L0_attn_f_dt_w, L0_attn_f_dt_b, L0_attn_f_A_log, L0_attn_f_D, L0_attn_f_out_w, L0_attn_b_in_w, L0_attn_b_conv_w, L0_attn_b_conv_b, L0_attn_b_xproj_w, L0_attn_b_dt_w, L0_attn_b_dt_b, L0_attn_b_A_log, L0_attn_b_D, L0_attn_b_out_w, L0_attn_ln_f_g, L0_attn_ln_f_b, L0_attn_ln_b_g, L0_attn_ln_b_b, L0_attn_ln_ff_g, L0_attn_ln_ff_b, L0_attn_ffn_w1, L0_attn_ffn_b1, L0_attn_ffn_w2, L0_attn_ffn_b2)
    h = h + _L0_ffn_ref(_layernorm(h, axis=-1), L0_ffn_router_w, L0_ffn_W1, L0_ffn_b1, L0_ffn_W2, L0_ffn_b2)
    h = h + _L1_attn_ref(_layernorm(h, axis=-1), L1_attn_weights_real, L1_attn_weights_imag)
    h = h + _L1_ffn_ref(_layernorm(h, axis=-1), L1_ffn_Wa, L1_ffn_ba, L1_ffn_Ws, L1_ffn_bs)
    return h

_drawn_inputs = setup_inputs


def setup_inputs(seed=0):
    import zlib

    import numpy as np

    out = dict(_drawn_inputs(seed))
    spreads = {'L0_tok_b_main': (0.0, 0.1),
     'L0_tok_b_sx': (0.0, 0.1),
     'L0_tok_b_sy': (0.0, 0.1),
     'L0_tok_ln_g': (1.0, 0.2),
     'L0_tok_ln_b': (0.0, 0.1),
     'L0_attn_f_conv_b': (0.0, 0.8),
     'L0_attn_f_D': (1.0, 0.6),
     'L0_attn_b_conv_b': (0.0, 0.8),
     'L0_attn_b_D': (1.0, 0.6),
     'L0_attn_ln_f_g': (1.0, 0.2),
     'L0_attn_ln_f_b': (0.0, 0.291),
     'L0_attn_ln_b_g': (1.0, 0.2),
     'L0_attn_ln_b_b': (0.0, 0.314),
     'L0_attn_ln_ff_g': (1.0, 0.2),
     'L0_attn_ln_ff_b': (0.0, 0.1),
     'L0_attn_ffn_b1': (0.0, 0.63),
     'L0_attn_ffn_b2': (0.0, 0.1)}
    factors = {'L0_attn_f_in_w': 8.0,
     'L0_attn_f_conv_w': 8.0,
     'L0_attn_f_xproj_w': 8.0,
     'L0_attn_f_dt_w': 8.0,
     'L0_attn_f_dt_b': 8.0,
     'L0_attn_f_A_log': 8.0,
     'L0_attn_f_out_w': 8.0,
     'L0_attn_b_in_w': 8.0,
     'L0_attn_b_conv_w': 8.0,
     'L0_attn_b_xproj_w': 8.0,
     'L0_attn_b_dt_w': 8.0,
     'L0_attn_b_dt_b': 8.0,
     'L0_attn_b_A_log': 8.0,
     'L0_attn_b_out_w': 8.0,
     'L0_ffn_b1': 26.207,
     'L0_ffn_b2': 8.0,
     'L1_attn_weights_real': 64.0,
     'L1_attn_weights_imag': 64.0}
    for name, (base, spread) in spreads.items():
        noise = np.random.default_rng([zlib.crc32(name.encode()), seed]).standard_normal(out[name].shape)
        drawn = base * np.exp(spread * noise) if base else spread * noise
        out[name] = jnp.asarray(drawn.astype(out[name].dtype))
    for name, factor in factors.items():
        out[name] = (out[name] * factor).astype(out[name].dtype)
    return out
```

```python
from collections import namedtuple
from contextlib import ExitStack

import concourse.bass as bass
from concourse import mybir
import numpy as np

F32 = mybir.dt.float32
BF16 = mybir.dt.bfloat16
ALU = mybir.AluOpType
ACT = mybir.ActivationFunctionType
AXX = mybir.AxisListType.X

P = 128
D = 128
GRID = 14
NPATCH = GRID * GRID
L = NPATCH + 1
PAIR = 2
T = PAIR * L
TP = PAIR * NPATCH
PADL = L + 3
XP = PAIR * PADL
CH = 6
NS = 16
TAPS = 4
R = 8
FF = 4
EXP = 6
EC = 3
NPART = 11
MODES = 64
MB = 4
RING = 4
EPS = 1e-5
EDGE = 1.0 / 31.0
LOG_EXP = "natural_log_exp_and_others"

COLS = {}
for _name, _width in [("tok_bias", 1), ("tok_g", 1), ("tok_b", 1), ("cls", 1)] + [
        (f"{_v}{_d}", _w) for _d in range(2)
        for _v, _w in (("conv_b", 2), ("skip", 2), ("dt_b", 2), ("a_log", 2 * NS), ("ln_g", 1), ("ln_b", 1))] + [
        ("ff_g", 1), ("ff_b", 1), ("ffn_b1", FF), ("ffn_b2", 1), ("moe_b1", EXP * EC), ("moe_b2", EXP)]:
    COLS[_name] = (sum(w for _, w in COLS.values()), _width)
NCOLS = sum(w for _, w in COLS.values())


class Signal:

    def __init__(self, ctx, nc, name, per=1, unit=1):
        self.sem = ctx.enter_context(nc.semaphore(name))
        self.per, self.unit = per, unit

    def seed(self, eng):
        eng.sem_inc(self.sem, 2 * self.per * self.unit)

    def at(self, n, j=None):
        return (n * self.per + 2 * self.per + (self.per if j is None else j)) * self.unit


class Shared:
    pass


def signals(ctx, nc, prefix, **per):
    made = [Signal(ctx, nc, f"{prefix}_{k}", v) for k, v in per.items()]
    return namedtuple("Signals", list(per))(*made)


def col(S, name, i=0):
    a = COLS[name][0] + i
    return S.cols[:, a:a + 1]


def setup(nc, S, I):
    with ExitStack() as ctx:
        loaded = ctx.enter_context(nc.semaphore("su_loaded"))
        cleared = ctx.enter_context(nc.semaphore("su_cleared"))
        folded_pe = ctx.enter_context(nc.semaphore("su_folded_pe"))
        folded = ctx.enter_context(nc.semaphore("su_folded"))
        a_exp = ctx.enter_context(nc.semaphore("su_a_exp"))
        dve_step = ctx.enter_context(nc.semaphore("su_dve_step"))
        out_w = ctx.enter_context(nc.sbuf_tensor("su_out_w", [P, 2, 2 * D], F32))
        w2 = ctx.enter_context(nc.sbuf_tensor("su_w2", [P, FF * D], F32))
        in_w = ctx.enter_context(nc.sbuf_tensor("su_in_w", [P, 2, 2 * D], F32))
        taps = ctx.enter_context(nc.sbuf_tensor("su_taps", [P, 2, TAPS, 2 * D], F32))
        sel = ctx.enter_context(nc.sbuf_tensor("su_sel", [96, 2 * NS], F32))
        ps = ctx.enter_context(nc.psum_tensor("su_ps", [P, 8, 512], F32))
        block = ctx.enter_context(nc.Block())
        loads = [(S.center[:], I.center), (S.mean[:], I.mean), (S.ident[:], I.ident), (sel[:], I.sel),
                 (S.cols[:], I.cols), (out_w[:], I.out_w), (w2[:], I.ffn_w2), (in_w[:], I.in_w_x), (taps[:], I.taps),
                 (S.zw[:], I.in_w_z), (S.xpw[:], I.xproj), (S.dtw[96:96 + R], I.dt_w), (S.w1[:], I.ffn_w1)]

        @block.sync
        def _(sp):
            for dst, src in loads:
                sp.dma_start(dst, src).then_inc(loaded, 16)

        @block.tensor
        def _(pe):
            pe.wait_ge(loaded, 16 * len(loads))
            for d in range(2):
                for half in range(2):
                    nc.tensor.matmul(ps[:, 0, (2 * d + half) * D:(2 * d + half + 1) * D],
                                     out_w[:, d, half * D:(half + 1) * D], S.center[:], start=True, stop=True)
            for k in range(FF):
                nc.tensor.matmul(ps[:, 1, k * D:(k + 1) * D], w2[:, k * D:(k + 1) * D], S.center[:],
                                 start=True, stop=True)
            nc.tensor.matmul(ps[:, 2, 0:1], S.center[:], col(S, "tok_bias"), start=True, stop=True)
            nc.tensor.matmul(ps[:, 2, 1:2], S.center[:], col(S, "ffn_b2"), start=True, stop=True)\
                .then_inc(folded_pe, 1)

        @block.scalar
        def _(act):
            act.wait_ge(loaded, 16 * len(loads))
            nc.scalar.activation(S.sel[:], sel[:], ACT.Copy)
            for d in range(2):
                a = COLS[f"a_log{d}"][0]
                nc.scalar.activation(S.neg_a[:, d], S.cols[:, a:a + 2 * NS].rearrange("p (h s) -> p h s", h=2),
                                     ACT.Exp).then_inc(a_exp, 1)

        @block.gpsimd
        def _(pool):
            nc.gpsimd.memset(S.X[:], 0.0).then_inc(cleared, 1)
            pool.wait_ge(loaded, 16 * len(loads))
            for d in range(2):
                for k in range(TAPS):
                    nc.gpsimd.tensor_tensor(S.convw[:, d, k, :], in_w[:, d, :], taps[:, d, k, :], ALU.mult)

        @block.vector
        def _(dve):
            nc.vector.memset(S.eps[:], EPS)
            nc.vector.memset(S.past_edge[:], 1.0 / (1.0 + EDGE))
            dve.wait_ge(loaded, 16 * len(loads))
            nc.vector.tensor_copy(S.h[:].rearrange("p (b t) -> p b t", t=L)[:, :, 0:1],
                                  col(S, "cls").unsqueeze(1).to_broadcast([P, S.B, 1]))
            for d in range(2):
                nc.vector.tensor_scalar(S.g_half[:, d:d + 1], col(S, f"ln_g{d}"), 0.5, None, ALU.mult)
            nc.vector.tensor_tensor(S.b_half[:], col(S, "ln_b0"), col(S, "ln_b1"), ALU.add).then_inc(dve_step, 1)
            dve.wait_ge(dve_step, 1)
            nc.vector.tensor_scalar(S.b_half[:], S.b_half[:], 0.5, None, ALU.mult)
            nc.vector.tensor_scalar(S.xpw[:], S.xpw[:], 0.5, None, ALU.mult).then_inc(dve_step, 1)
            dve.wait_ge(dve_step, 2)
            parts = S.xpw[:, :, :, 0:96].rearrange("p d h (part bc s) -> p (d h) part bc s", part=3, bc=2)
            for d in range(2):
                for half in range(2):
                    c = parts[:, 2 * d + half, :, 1]
                    nc.vector.tensor_scalar(c, c, 0.5, None, ALU.mult)
                    nc.vector.tensor_scalar(S.conv_b_half[:, d, half:half + 1], col(S, f"conv_b{d}", half), 0.5, None,
                                            ALU.mult)
                    nc.vector.tensor_scalar(S.skip_half[:, d, half:half + 1], col(S, f"skip{d}", half), 0.5, None,
                                            ALU.mult)
            dve.wait_ge(a_exp, 2)
            nc.vector.tensor_scalar(S.neg_a[:], S.neg_a[:], -1.0, None, ALU.mult)
            dve.wait_ge(folded_pe, 1)
            nc.vector.tensor_scalar(S.woc[:], ps[:, 0, :], 0.5, None, ALU.mult)
            nc.vector.tensor_copy(S.w2c[:], ps[:, 1, :])
            nc.vector.tensor_copy(S.tok_bias_c[:], ps[:, 2, 0:1])
            nc.vector.tensor_copy(S.ffn_b2_c[:], ps[:, 2, 1:2]).then_inc(dve_step, 1)
            dve.wait_ge(dve_step, 3)
            nc.vector.tensor_tensor(S.ffn_b2_cg[:], S.ffn_b2_c[:], col(S, "ff_g"), ALU.mult)


def tokens(nc, S, I):
    G = S.G
    with ExitStack() as ctx:
        w_nat = ctx.enter_context(nc.sbuf_tensor("tk_w_nat", [P, 3 * CH, D], F32))
        w = ctx.enter_context(nc.sbuf_tensor("tk_w", [P, 3 * CH, D], F32))
        pix = ctx.enter_context(nc.sbuf_tensor("tk_pix", [P, 2, CH, TP], F32))
        shifted = ctx.enter_context(nc.sbuf_tensor("tk_shifted", [P, 2, CH, TP], F32))
        sq = ctx.enter_context(nc.sbuf_tensor("tk_sq", [P, 2, T], F32))
        rec = ctx.enter_context(nc.sbuf_tensor("tk_rec", [P, 2, T], F32))
        nrm = ctx.enter_context(nc.sbuf_tensor("tk_nrm", [P, 2, T], F32))
        tok_ps = ctx.enter_context(nc.psum_tensor("tk_tok_ps", [P, 2, 512], F32))
        var_ps = ctx.enter_context(nc.psum_tensor("tk_var_ps", [P, 2, 512], F32))
        cen_ps = ctx.enter_context(nc.psum_tensor("tk_cen_ps", [P, 2, 512], F32))
        wload = ctx.enter_context(nc.semaphore("tk_wload"))
        wfold_pe = ctx.enter_context(nc.semaphore("tk_wfold_pe"))
        wfold = ctx.enter_context(nc.semaphore("tk_wfold"))
        cleared = ctx.enter_context(nc.semaphore("tk_cleared"))
        s = signals(ctx, nc, "tk", shifted=2, tok=1, sq=1, var=1, log=1, rec=1, nrm=1, h=1,
                    cen=1, sq2=1, var2=1, log2=1, rec2=1, x=1)
        pix_in = [Signal(ctx, nc, f"tk_pix_in{p}", 1, 16) for p in range(2)]
        block = ctx.enter_context(nc.Block())

        @block.sync
        def _(sp):
            for p in range(2):
                pix_in[p].seed(sp)
            sp.dma_start(w_nat[:], I.tok_w).then_inc(wload, 16)
            with sp.Fori(0, G // 2) as i:
                for p in range(2):
                    sp.wait_ge(s.tok.sem, s.tok.at(2 * i + p - 2))
                    sp.dma_start(pix[:, p].rearrange("q c t -> q (c t)"),
                                 I.pixels[bass.ds(2 * i + p, 1)].rearrange("o q t -> (o q) t"))\
                        .then_inc(pix_in[p].sem, 16)

        @block.tensor
        def _(pe):
            for sig in (s.tok, s.var, s.cen, s.var2):
                sig.seed(pe)
            pe.wait_ge(wload, 16)
            for k in range(3 * CH):
                bank = (tok_ps, var_ps, cen_ps)[(k % 6) // 2][:, k % 2]
                if k >= 6:
                    pe.wait_ge(wfold, k - 5)
                nc.tensor.matmul(bank[:, 0:D], w_nat[:, k], S.center[:], start=True, stop=True).then_inc(wfold_pe, 1)
            pe.wait_ge(wfold, 3 * CH)
            with pe.Fori(0, G // 2) as i:
                for p in range(2):
                    n = 2 * i + p
                    acc = tok_ps[:, p, 0:TP]
                    rows = acc.rearrange("q (b t) -> q b t", b=PAIR)
                    pe.wait_ge(pix_in[p].sem, pix_in[p].at(i))
                    pe.wait_ge(s.nrm.sem, s.nrm.at(n - 2))
                    for c in range(CH):
                        nc.tensor.matmul(acc, w[:, c], pix[:, p, c], start=(c == 0), stop=False, skip_group_check=True)
                    for c in range(CH):
                        src = pix[:, p, c].rearrange("q (b t) -> q b t", b=PAIR)
                        up = c % 2 == 0
                        a, b = (0, GRID) if up else (GRID, 0)
                        m = NPATCH - GRID
                        nc.tensor.matmul(rows[:, :, a:a + m], w[:, 2 * CH + c], src[:, :, b:b + m],
                                         start=False, stop=False, skip_group_check=True)
                    pe.wait_ge(s.shifted.sem, s.shifted.at(n))
                    for c in range(CH):
                        mm = nc.tensor.matmul(acc, w[:, CH + c], shifted[:, p, c], start=False, stop=(c == CH - 1),
                                              skip_group_check=True)
                    mm.then_inc(s.tok.sem, 1)
                    pe.wait_ge(s.sq.sem, s.sq.at(n))
                    pe.wait_ge(s.log2.sem, s.log2.at(n - 2))
                    nc.tensor.matmul(var_ps[:, p, 0:TP], S.mean[:], sq[:, p, 0:TP], start=True, stop=True)\
                        .then_inc(s.var.sem, 1)
                    pe.wait_ge(s.h.sem, s.h.at(n))
                    pe.wait_ge(s.x.sem, s.x.at(n - 2))
                    nc.tensor.matmul(cen_ps[:, p, 0:T], S.center[:], S.h[:, bass.ds(n * T, T)], start=True, stop=True)\
                        .then_inc(s.cen.sem, 1)
                    pe.wait_ge(s.sq2.sem, s.sq2.at(n))
                    nc.tensor.matmul(var_ps[:, p, 0:T], S.mean[:], sq[:, p], start=True, stop=True)\
                        .then_inc(s.var2.sem, 1)

        @block.scalar
        def _(act):
            for sig in (s.sq, s.log, s.rec, s.sq2, s.log2, s.rec2):
                sig.seed(act)
            act.preload_act_table_set(LOG_EXP)
            with act.Fori(0, G // 2) as i:
                for p in range(2):
                    n = 2 * i + p
                    act.wait_ge(s.tok.sem, s.tok.at(n))
                    act.wait_ge(s.var2.sem, s.var2.at(n - 2))
                    nc.scalar.activation(sq[:, p, 0:TP], tok_ps[:, p, 0:TP], ACT.Square, bias=S.tok_bias_c[:])\
                        .then_inc(s.sq.sem, 1)
                    act.wait_ge(s.var.sem, s.var.at(n))
                    act.wait_ge(s.x.sem, s.x.at(n - 2))
                    nc.scalar.activation(rec[:, p, 0:TP], var_ps[:, p, 0:TP], ACT.Ln, bias=S.eps[:])\
                        .then_inc(s.log.sem, 1)
                    act.wait_ge(s.log.sem, s.log.at(n))
                    nc.scalar.activation(rec[:, p, 0:TP], rec[:, p, 0:TP], ACT.Exp, scale=-0.5).then_inc(s.rec.sem, 1)
                    act.wait_ge(s.cen.sem, s.cen.at(n))
                    nc.scalar.activation(sq[:, p], cen_ps[:, p, 0:T], ACT.Square).then_inc(s.sq2.sem, 1)
                    act.wait_ge(s.var2.sem, s.var2.at(n))
                    act.wait_ge(s.nrm.sem, s.nrm.at(n))
                    nc.scalar.activation(rec[:, p], var_ps[:, p, 0:T], ACT.Ln, bias=S.eps[:]).then_inc(s.log2.sem, 1)
                    act.wait_ge(s.log2.sem, s.log2.at(n))
                    nc.scalar.activation(rec[:, p], rec[:, p], ACT.Exp, scale=-0.5).then_inc(s.rec2.sem, 1)

        @block.vector
        def _(dve):
            for sig in (s.shifted, s.nrm, s.h, s.x):
                sig.seed(dve)
            nc.vector.memset(shifted[:], 0.0).then_inc(cleared, 1)
            for k in range(3 * CH):
                bank = (tok_ps, var_ps, cen_ps)[(k % 6) // 2][:, k % 2]
                dve.wait_ge(wfold_pe, k + 1)
                nc.vector.tensor_copy(w[:, k], bank[:, 0:D]).then_inc(wfold, 1)
            dve.wait_ge(cleared, 1)
            with dve.Fori(0, G // 2) as i:
                for p in range(2):
                    n = 2 * i + p
                    dve.wait_ge(pix_in[p].sem, pix_in[p].at(i))
                    dve.wait_ge(s.tok.sem, s.tok.at(n - 2))
                    src = pix[:, p].rearrange("q c (r j) -> q (c r) j", j=GRID)
                    dst = shifted[:, p].rearrange("q c (r j) -> q (c r) j", j=GRID)
                    nc.vector.tensor_copy(dst[0:64, :, 0:GRID - 1], src[0:64, :, 1:GRID]).then_inc(s.shifted.sem, 1)
                    nc.vector.tensor_copy(dst[64:P, :, 1:GRID], src[64:P, :, 0:GRID - 1]).then_inc(s.shifted.sem, 1)
                    dve.wait_ge(s.rec.sem, s.rec.at(n))
                    nc.vector.scalar_tensor_tensor(out=nrm[:, p, 0:TP], in0=tok_ps[:, p, 0:TP], scalar=S.tok_bias_c[:],
                                                   in1=rec[:, p, 0:TP], op0=ALU.add, op1=ALU.mult)\
                        .then_inc(s.nrm.sem, 1)
                    dve.wait_ge(s.nrm.sem, s.nrm.at(n))
                    hn = S.h[:, bass.ds(n * T, T)].rearrange("q (b t) -> q b t", b=PAIR)
                    nc.vector.tensor_scalar(hn[:, :, 1:L], nrm[:, p, 0:TP].rearrange("q (b t) -> q b t", b=PAIR),
                                            col(S, "tok_g"), col(S, "tok_b"), ALU.mult, ALU.add).then_inc(s.h.sem, 1)
                    dve.wait_ge(s.rec2.sem, s.rec2.at(n))
                    xn = S.X[:, bass.ds(n * XP, XP)].rearrange("q (b t) -> q b t", b=PAIR)
                    nc.vector.tensor_tensor(xn[:, :, 3:PADL], cen_ps[:, p, 0:T].rearrange("q (b t) -> q b t", b=PAIR),
                                            rec[:, p].rearrange("q (b t) -> q b t", b=PAIR), ALU.mult)\
                        .then_inc(s.x.sem, 1)


def mamba(nc, S, I):
    G = S.G
    with ExitStack() as ctx:
        def sb(name, shape, dt=F32):
            return ctx.enter_context(nc.sbuf_tensor(f"mb_{name}", shape, dt))

        xflip = sb("xflip", [P, XP])
        xc = sb("xc", [P, 2, 2, T])
        zs = sb("zs", [P, 2, 2, T])
        bc = sb("bc", [96, 2, T], BF16)
        rest = sb("rest", [P, 2, T])
        res1, res2, dtr = rest[0:96, 0], rest[0:96, 1], rest[96:96 + R, 0]
        part2 = sb("part2", [96, T], BF16)
        mag = sb("mag", [P, 2, T])
        v = sb("v", [P, 2, T])
        dt = sb("dt", [P, 2, 2, T])
        dtx = sb("dtx", [P, 2, 2, T])
        bs = sb("bs", [P, RING, T])
        db = sb("db", [P, 2, 2, T])
        da = sb("da", [P, RING, 2, T])
        hst = sb("hst", [P, 2, 2, T])
        hc = sb("hc", [P, 2, 2, T])
        yd = sb("yd", [P, 2, T])
        cg = sb("cg", [P, 2, T])
        sq = sb("sq", [P, T])
        h2 = sb("h2", [P, T])
        gl3 = sb("gl3", [P, T])
        ps = ctx.enter_context(nc.psum_tensor("mb_ps", [P, 8, 512], F32))
        b_ps, c_ps, y_ps, proj_ps, post_ps = ps[:, 0:2], ps[:, 2:4], ps[:, 4:6], ps[:, 6], ps[:, 7]

        cleared = ctx.enter_context(nc.semaphore("mb_cleared"))
        s = signals(
            ctx, nc, "mb", flip=1, conv=4, th=4, xb=4, xc=2, z=4, zt=4, zr=4, zs=2, xp=2, bc1=2, res1=2, part2=2,
            res2=2, bc=4, dtr=2, dtp=4, dx=4, relu=2, mag=2, u=2, logw=2, poly=12, dt=2, dtx=2,
            bb=2 * NS, bs=2 * NS, db=2 * NS, da=4 * NS, st=4 * NS, cb=2 * NS, hc=2 * NS, ys=2 * NS,
            yd=4, yz=2, h2=1, up=4, gl=4, hn=1, sums=1)
        LN_F, LN_B, LN_FF, LN_X = range(4)
        cen, cgd, sqd, var, log, rec, nrm = (
            [Signal(ctx, nc, f"mb_{x}{w}") for w in ("f", "b", "ff", "x")]
            for x in ("cen", "cg", "sq", "var", "log", "rec", "nrm"))
        block = ctx.enter_context(nc.Block())

        def images(ap):
            return ap.rearrange("q (b t) -> q b t", b=PAIR)

        gl = [rest[:, 0], rest[:, 1], images(xflip[:])[:, :, 3:PADL], gl3[:]]

        def x_of(n):
            return images(S.X[:, bass.ds(n * XP, XP)])

        def h_of(n):
            return S.h[:, bass.ds(n * T, T)]

        def before(which, n, last):
            if which == LN_X:
                return (LN_FF, n) if last else (LN_F, n + 1)
            return {LN_F: (LN_FF, n - 1), LN_B: (LN_X, n - 1), LN_FF: (LN_B, n)}[which]

        def following(n, d):
            return (n, 1) if d == 0 else (n + 1, 0)

        def preceding(n, d):
            return (n - 1, 1) if d == 0 else (n, 0)

        def later(n, d, k, steps, ahead):
            if k + steps < NS:
                return [(n, d, k + steps)]
            return [(*following(n, d), k + steps - NS)] if ahead else []

        @block.tensor
        def _(pe):
            for sig in (s.conv, s.z, s.xp, s.dtp, s.bb, s.cb, s.ys, s.up, *cen, *var):
                sig.seed(pe)

            def conv(n, d, half, taps):
                xin = x_of(n) if d == 0 else images(xflip[:])
                bank = post_ps if half else proj_ps
                if 0 in taps:
                    if half:
                        w = LN_X if d else LN_FF
                        pe.wait_ge(log[w].sem, log[w].at(n - 2))
                    elif d:
                        pe.wait_ge(s.dx.sem, s.dx.at(n, 2))
                        pe.wait_ge(s.flip.sem, s.flip.at(n))
                    else:
                        pe.wait_ge(s.gl.sem, s.gl.at(n - 2))
                for k in taps:
                    mm = nc.tensor.matmul(bank[:, 0:T], S.convw[:, d, k, half * D:(half + 1) * D],
                                          xin[:, :, k:k + L], start=(k == 0), stop=(k == TAPS - 1))
                if TAPS - 1 in taps:
                    mm.then_inc(s.conv.sem, 1)

            def gate(n, d, half, ahead):
                if half:
                    pe.wait_ge(s.zr.sem, s.zr.at(n, 2 * d + 1))
                elif ahead:
                    a, e = following(n, d)
                    pe.wait_ge(s.xb.sem, s.xb.at(a, 2 * e + 1))
                else:
                    pe.wait_ge(s.gl.sem, s.gl.at(n - 1))
                nc.tensor.matmul(proj_ps[:, 0:T], S.zw[:, d, half * D:(half + 1) * D], x_of(n)[:, :, 3:PADL],
                                 start=True, stop=True).then_inc(s.z.sem, 1)

            def project(n, d, k, gated=None):
                if k < 4:
                    conv(n, d, k // 2, [2 * (k % 2), 2 * (k % 2) + 1])
                elif k == 6:
                    if gated:
                        pe.wait_ge(s.zr.sem, s.zr.at(gated[0], 2 * gated[1] + 2))
                    pe.wait_ge(s.xc.sem, s.xc.at(n, d + 1))
                    for half in range(2):
                        mm = nc.tensor.matmul(proj_ps[0:96 + R, 0:T], S.xpw[:, d, half, :], xc[:, d, half],
                                              start=(half == 0), stop=(half == 1))
                    mm.then_inc(s.xp.sem, 1)
                elif k in (7, 9):
                    half = (k - 7) // 2
                    if half == 0:
                        pe.wait_ge(s.dtr.sem, s.dtr.at(n, d + 1))
                        pe.wait_ge(s.res1.sem, s.res1.at(n, d + 1))
                    else:
                        pe.wait_ge(s.dx.sem, s.dx.at(n, 2 * d + 1))
                    nc.tensor.matmul(proj_ps[:, 0:T], S.dtw[96:96 + R, d, half * D:(half + 1) * D], dtr,
                                     start=True, stop=True).then_inc(s.dtp.sem, 1)

            def spread_b(n, d, k):
                if k == 0:
                    pe.wait_ge(s.bc.sem, s.bc.at(n, 2 * d + 2))
                pe.wait_ge(s.bs.sem, s.bs.at(n, NS * d + k - 1))
                nc.tensor.matmul(b_ps[:, k % 2, 0:T], S.sel[:, k:k + 1].to_broadcast([96, D]), bc[:, d], start=True, stop=True)\
                    .then_inc(s.bb.sem, 1)

            def spread_c(n, d, k):
                pe.wait_ge(s.hc.sem, s.hc.at(n, NS * d + k - 1))
                nc.tensor.matmul(c_ps[:, k % 2, 0:T], S.sel[:, NS + k:NS + k + 1].to_broadcast([96, D]), bc[:, d], start=True, stop=True)\
                    .then_inc(s.cb.sem, 1)

            def add(n, d, k):
                if k == 0:
                    pe.wait_ge(s.yd.sem, s.yd.at(n, 2 * d))
                pe.wait_ge(s.hc.sem, s.hc.at(n, NS * d + k + 1))
                for half in range(2):
                    mm = nc.tensor.matmul(y_ps[:, half, 0:T], S.ident[:], hc[:, k % 2, half], start=(k == 0),
                                          stop=(k == NS - 1))
                mm.then_inc(s.ys.sem, 1)

            def variance(which, n):
                pe.wait_ge(sqd[which].sem, sqd[which].at(n))
                nc.tensor.matmul(post_ps[:, 0:T], S.mean[:], sq[:], start=True, stop=True).then_inc(var[which].sem, 1)

            def free_bank(which, n, last=False):
                w, m = before(which, n, last)
                pe.wait_ge(log[w].sem, log[w].at(m))

            def out_project(n, d, ahead):
                if ahead:
                    a, e = (n + 1, 0) if d == 0 else (n + 1, 1)
                    pe.wait_ge(s.xb.sem, s.xb.at(a, 2 * e + 2))
                else:
                    free_bank(LN_F + d, n)
                pe.wait_ge(s.yz.sem, s.yz.at(n, d + 1))
                for half in range(2):
                    nc.tensor.matmul(post_ps[:, 0:T], S.woc[:, (2 * d + half) * D:(2 * d + half + 1) * D], zs[:, d, half],
                                     start=(half == 0), stop=False)
                nc.tensor.matmul(post_ps[:, 0:T], S.ident[:], x_of(n)[:, :, 3:PADL], start=False, stop=True)\
                    .then_inc(cen[LN_F + d].sem, 1)

            def up(n, k, last):
                if k == 0:
                    free_bank(LN_FF, n)
                    pe.wait_ge(s.h2.sem, s.h2.at(n))
                elif k > 1:
                    pe.wait_ge(s.gl.sem, s.gl.at(n, k - 1))
                elif last:
                    pe.wait_ge(s.zr.sem, s.zr.at(n, 4))
                else:
                    pe.wait_ge(s.dx.sem, s.dx.at(n + 1, 4))
                bank = proj_ps if k % 2 else post_ps
                nc.tensor.matmul(bank[:, 0:T], S.w1[:, k * D:(k + 1) * D], h2[:], start=True, stop=True)\
                    .then_inc(s.up.sem, 1)

            def down(n, chunks):
                if 0 in chunks:
                    pe.wait_ge(s.gl.sem, s.gl.at(n, FF - 1))
                    nc.tensor.matmul(post_ps[:, 0:T], S.center[:], h2[:], start=True, stop=False)
                for k in chunks:
                    pe.wait_ge(s.gl.sem, s.gl.at(n, k + 1))
                    mm = nc.tensor.matmul(post_ps[:, 0:T], S.w2c[:, k * D:(k + 1) * D], gl[k], start=False,
                                          stop=(k == FF - 1))
                if FF - 1 in chunks:
                    mm.then_inc(cen[LN_FF].sem, 1)

            def center(n, last=False):
                free_bank(LN_X, n, last)
                pe.wait_ge(s.hn.sem, s.hn.at(n))
                nc.tensor.matmul(post_ps[:, 0:T], S.center[:], h_of(n), start=True, stop=True).then_inc(cen[LN_X].sem, 1)

            def forward_norm(n, k, ahead):
                if k == 5:
                    out_project(n, 0, ahead)
                elif k == 7:
                    variance(LN_F, n)

            def feed_forward(n, k, last=False):
                if k == 5:
                    out_project(n, 1, ahead=not last)
                elif k == 7:
                    variance(LN_B, n)
                elif k == 11:
                    for j in range(FF):
                        up(n, j, last)
                elif k == 12:
                    down(n, [0, 1])
                elif k == 13:
                    down(n, [2, 3])
                elif k == 15 and last:
                    variance(LN_FF, n)

            def expert_norm(n, k, last=False):
                if k == 0 and not last:
                    variance(LN_FF, n)
                elif k == 9:
                    center(n, last)
                elif k == 11:
                    variance(LN_X, n)

            def unit(n, d, first=False, ahead=True, late=True):
                for k in range(NS):
                    if k == 0 and not first:
                        add(*preceding(n, d), NS - 1)
                    for state in later(n, d, k, 3, ahead):
                        spread_b(*state)
                    for state in later(n, d, k, 1, ahead):
                        spread_c(*state)
                    if ahead:
                        project(*following(n, d), k, gated=(n, d))
                    if k in (3, 5):
                        gate(n, d, (k - 3) // 2, ahead)
                    if d == 0 and not first:
                        feed_forward(n - 1, k)
                    elif d == 1:
                        if late:
                            expert_norm(n - 1, k)
                        forward_norm(n, k, ahead)
                    if k > 0:
                        add(n, d, k - 1)

            for k in range(NS):
                project(0, 0, k)
            spread_b(0, 0, 0)
            spread_b(0, 0, 1)
            spread_b(0, 0, 2)
            spread_c(0, 0, 0)
            unit(0, 0, first=True)
            unit(0, 1, late=False)
            with pe.Fori(1, G - 1) as n:
                unit(n, 0)
                unit(n, 1)
            unit(G - 1, 0)
            unit(G - 1, 1, ahead=False)
            add(G - 1, 1, NS - 1)
            for k in range(NS):
                feed_forward(G - 1, k, last=True)
            for k in range(NS):
                expert_norm(G - 1, k, last=True)

        @block.scalar
        def _(act):
            for sig in (s.th, s.xb, s.zt, s.zr, s.part2, s.bc, s.dtr, s.dx, s.mag, s.u, s.logw, s.bs, s.da, s.gl, s.flip,
                        *cgd, *sqd, *log, *rec):
                sig.seed(act)

            def flip(n):
                act.wait_ge(s.conv.sem, s.conv.at(n - 1))
                act.wait_ge(cen[LN_FF].sem, cen[LN_FF].at(n - 2))
                nc.scalar.activation(images(xflip[:])[:, :, PADL - 1:2:-1], x_of(n)[:, :, 3:PADL], ACT.Copy)\
                    .then_inc(s.flip.sem, 1)

            def silu_parts(n, d, half, kind):
                i = 2 * d + half + 1
                bank = post_ps if half and kind == "conv" else proj_ps
                if kind == "conv":
                    act.wait_ge(s.conv.sem, s.conv.at(n, i))
                    act.wait_ge(s.poly.sem, s.poly.at(n, 6 * d))
                    nc.scalar.activation(v[:, half], bank[:, 0:T], ACT.Tanh, bias=S.conv_b_half[:, d, half:half + 1],
                                         scale=0.5).then_inc(s.th.sem, 1)
                    act.wait_ge(s.yd.sem, s.yd.at(n - 1, 2 * d + 2))
                    act.wait_ge(s.dtx.sem, s.dtx.at(n - 1, d + 1))
                    nc.scalar.activation(xc[:, d, half], bank[:, 0:T], ACT.Identity, bias=col(S, f"conv_b{d}", half))\
                        .then_inc(s.xb.sem, 1)
                else:
                    act.wait_ge(s.z.sem, s.z.at(n, i))
                    act.wait_ge(s.dt.sem, s.dt.at(n, d + 1))
                    nc.scalar.activation(mag[:, half], bank[:, 0:T], ACT.Tanh, scale=0.5).then_inc(s.zt.sem, 1)
                    act.wait_ge(cen[LN_F + d].sem, cen[LN_F + d].at(n - 1))
                    nc.scalar.activation(zs[:, d, half], bank[:, 0:T], ACT.Copy).then_inc(s.zr.sem, 1)

            def project(n, d, k, gated=None):
                if k in (2, 4):
                    silu_parts(n, d, k // 2 - 1, "conv")
                elif k == 6:
                    act.wait_ge(s.xp.sem, s.xp.at(n, d + 1))
                    act.wait_ge(s.dtp.sem, s.dtp.at(n, 2 * d))
                    act.wait_ge(cen[LN_FF].sem, cen[LN_FF].at(n - 2))
                    nc.scalar.activation(dtr, proj_ps[96:96 + R, 0:T], ACT.Copy).then_inc(s.dtr.sem, 1)
                elif k == 7:
                    act.wait_ge(s.res1.sem, s.res1.at(n, d + 1))
                    act.wait_ge(s.res2.sem, s.res2.at(n, d))
                    act.wait_ge(s.bc.sem, s.bc.at(n, 2 * d))
                    nc.scalar.activation(part2[:], res1, ACT.Copy).then_inc(s.part2.sem, 1)
                    act.wait_ge(s.part2.sem, s.part2.at(n, d + 1))
                    nc.scalar.activation(bc[32:64, d], part2[32:64], ACT.Copy).then_inc(s.bc.sem, 1)
                elif k == 8:
                    dt_in(n, d, 0)
                    act.wait_ge(s.res2.sem, s.res2.at(n, d + 1))
                    nc.scalar.activation(bc[64:96, d], res2[64:96], ACT.Copy).then_inc(s.bc.sem, 1)
                elif k == 10:
                    dt_in(n, d, 1)
                    act.wait_ge(s.dx.sem, s.dx.at(n, 2 * d + 2))
                    if gated:
                        act.wait_ge(s.zs.sem, s.zs.at(gated[0], gated[1] + 1))
                    nc.scalar.activation(mag[:], dt[:, d], ACT.Abs).then_inc(s.mag.sem, 1)
                    act.wait_ge(s.mag.sem, s.mag.at(n, d + 1))
                    act.wait_ge(s.db.sem, s.db.at(n - 1, NS * (d + 1)))
                    nc.scalar.activation(dtx[:, d], mag[:], ACT.Exp, scale=-1.0).then_inc(s.u.sem, 1)
                    act.wait_ge(s.u.sem, s.u.at(n, d + 1))
                    nc.scalar.activation(mag[:], dtx[:, d], ACT.Ln, bias=S.past_edge[:], scale=1.0 / (1.0 + EDGE))\
                        .then_inc(s.logw.sem, 1)

            def dt_in(n, d, half):
                act.wait_ge(s.dtp.sem, s.dtp.at(n, 2 * d + half + 1))
                act.wait_ge(s.da.sem, s.da.at(n - 1, 2 * NS * (d + 1)))
                nc.scalar.activation(dt[:, d, half], proj_ps[:, 0:T], ACT.Identity, bias=col(S, f"dt_b{d}", half))\
                    .then_inc(s.dx.sem, 1)

            def copy_b(n, d, k):
                j = NS * d + k + 1
                act.wait_ge(s.bb.sem, s.bb.at(n, j))
                act.wait_ge(s.db.sem, s.db.at(n, j - RING))
                nc.scalar.activation(bs[:, k % RING], b_ps[:, k % 2, 0:T], ACT.Copy).then_inc(s.bs.sem, 1)

            def decay(n, d, k):
                if k == 0:
                    act.wait_ge(s.dt.sem, s.dt.at(n, d + 1))
                act.wait_ge(s.st.sem, s.st.at(n, 2 * (NS * d + k + 1 - RING)))
                for half in range(2):
                    nc.scalar.activation(images(da[:, k % RING, half])[:, :, 1:L], images(dt[:, d, half])[:, :, 1:L],
                                         ACT.Exp, scale=S.neg_a[:, d, half, k:k + 1]).then_inc(s.da.sem, 1)

            def squares(which, n, last=False):
                act.wait_ge(cen[which].sem, cen[which].at(n))
                w, m = before(which, n, last)
                act.wait_ge(nrm[w].sem, nrm[w].at(m))
                if which == LN_F:
                    act.wait_ge(s.hn.sem, s.hn.at(n - 1))
                elif which == LN_B:
                    act.wait_ge(nrm[LN_X].sem, nrm[LN_X].at(n - 1))
                else:
                    act.wait_ge(s.h2.sem, s.h2.at(n))
                g = cg[:, which % 2]
                if which in (LN_F, LN_B):
                    nc.scalar.activation(g, post_ps[:, 0:T], ACT.Copy,
                                         scale=S.g_half[:, which:which + 1]).then_inc(cgd[which].sem, 1)
                elif which == LN_FF:
                    nc.scalar.activation(g, post_ps[:, 0:T], ACT.Identity, bias=S.ffn_b2_cg[:],
                                         scale=col(S, "ff_g")).then_inc(cgd[which].sem, 1)
                else:
                    nc.scalar.activation(g, post_ps[:, 0:T], ACT.Copy).then_inc(cgd[which].sem, 1)
                if which == LN_FF:
                    nc.scalar.activation(sq[:], post_ps[:, 0:T], ACT.Square, bias=S.ffn_b2_c[:])\
                        .then_inc(sqd[which].sem, 1)
                else:
                    nc.scalar.activation(sq[:], post_ps[:, 0:T], ACT.Square).then_inc(sqd[which].sem, 1)

            def inverse_root(which, n):
                act.wait_ge(var[which].sem, var[which].at(n))
                nc.scalar.activation(sq[:], post_ps[:, 0:T], ACT.Ln, bias=S.eps[:]).then_inc(log[which].sem, 1)
                act.wait_ge(log[which].sem, log[which].at(n))
                nc.scalar.activation(sq[:], sq[:], ACT.Exp, scale=-0.5).then_inc(rec[which].sem, 1)

            def forward_norm(n, k):
                if k == 6:
                    squares(LN_F, n)
                elif k == 8:
                    inverse_root(LN_F, n)

            def feed_forward(n, k, last=False):
                if k == 6:
                    squares(LN_B, n)
                elif k == 8:
                    inverse_root(LN_B, n)
                elif k == 11:
                    act.wait_ge(cen[LN_FF].sem, cen[LN_FF].at(n - 1))
                    if not last:
                        act.wait_ge(s.res2.sem, s.res2.at(n + 1, 2))
                        act.wait_ge(s.dtp.sem, s.dtp.at(n + 1, 4))
                        act.wait_ge(s.conv.sem, s.conv.at(n + 1, 4))
                    for j in range(FF):
                        bank = proj_ps if j % 2 else post_ps
                        act.wait_ge(s.up.sem, s.up.at(n, j + 1))
                        src = images(bank[:, 0:T]) if j == 2 else bank[:, 0:T]
                        nc.scalar.activation(gl[j], src, ACT.Gelu_apprx_tanh, bias=col(S, "ffn_b1", j))\
                            .then_inc(s.gl.sem, 1)
                    act.preload_act_table_set(LOG_EXP)
                elif k == 15:
                    squares(LN_FF, n)
                    if last:
                        inverse_root(LN_FF, n)

            def expert_norm(n, k, last=False):
                if k == 1 and not last:
                    inverse_root(LN_FF, n)
                elif k == 10:
                    squares(LN_X, n, last)
                elif k == 12:
                    inverse_root(LN_X, n)

            def unit(n, d, first=False, ahead=True, late=True):
                for k in range(NS):
                    for state in later(n, d, k, 2, ahead):
                        copy_b(*state)
                        if k < NS - 2:
                            decay(*state)
                    if ahead:
                        project(*following(n, d), k, gated=(n, d))
                    if k in (4, 5):
                        silu_parts(n, d, k - 4, "gate")
                    if k == 5:
                        act.preload_act_table_set(LOG_EXP)
                    if d == 0 and not first:
                        feed_forward(n - 1, k)
                    elif d == 1:
                        forward_norm(n, k)
                        if late:
                            expert_norm(n - 1, k)
                    if d == 1 and ahead and k == 13:
                        flip(n + 1)
                    if k >= NS - 2 and ahead:
                        decay(*following(n, d), k + 2 - NS)

            act.wait_ge(cleared, 2)
            flip(0)
            for k in range(NS):
                if k == 6:
                    act.preload_act_table_set(LOG_EXP)
                project(0, 0, k)
            for k in range(2):
                copy_b(0, 0, k)
                decay(0, 0, k)
            unit(0, 0, first=True)
            unit(0, 1, late=False)
            with act.Fori(1, G - 1) as n:
                unit(n, 0)
                unit(n, 1)
            unit(G - 1, 0)
            unit(G - 1, 1, ahead=False)
            for k in range(NS):
                feed_forward(G - 1, k, last=True)
            for k in range(NS):
                expert_norm(G - 1, k, last=True)

        @block.gpsimd
        def _(pool):
            for sig in (s.res2, s.dt, s.dtx, s.db, s.yz, *nrm):
                sig.seed(pool)

            def project(n, d, k):
                if k == 7:
                    pool.wait_ge(s.part2.sem, s.part2.at(n, d + 1))
                    pool.wait_ge(s.bc.sem, s.bc.at(n, 2 * d))
                    pool.wait_ge(cen[LN_FF].sem, cen[LN_FF].at(n - 2))
                    nc.gpsimd.tensor_tensor(res2, res1, part2[:], ALU.subtract).then_inc(s.res2.sem, 1)
                elif k == 13:
                    pool.wait_ge(s.poly.sem, s.poly.at(n, 6 * d + 6))
                    nc.gpsimd.tensor_tensor(dt[:, d], mag[:], dt[:, d], ALU.add).then_inc(s.dt.sem, 1)
                elif k == 14:
                    pool.wait_ge(s.dt.sem, s.dt.at(n, d + 1))
                    nc.gpsimd.tensor_tensor(dtx[:, d], dt[:, d], xc[:, d], ALU.mult).then_inc(s.dtx.sem, 1)

            def drive(n, d, k):
                j = NS * d + k + 1
                if k == 0:
                    pool.wait_ge(s.dtx.sem, s.dtx.at(n, d + 1))
                pool.wait_ge(s.bs.sem, s.bs.at(n, j))
                pool.wait_ge(s.st.sem, s.st.at(n, 2 * (j - 2)))
                nc.gpsimd.tensor_tensor(db[:, k % 2], dtx[:, d], bs[:, k % RING].unsqueeze(1).to_broadcast([P, 2, T]),
                                        ALU.mult).then_inc(s.db.sem, 1)

            def gate(n, d):
                pool.wait_ge(s.yd.sem, s.yd.at(n, 2 * d + 2))
                pool.wait_ge(s.zs.sem, s.zs.at(n, d + 1))
                nc.gpsimd.tensor_tensor(zs[:, d], yd[:], zs[:, d], ALU.mult).then_inc(s.yz.sem, 1)

            def norm(which, n):
                g = cg[:, which % 2]
                pool.wait_ge(rec[which].sem, rec[which].at(n))
                if which == LN_X:
                    nc.gpsimd.tensor_tensor(x_of(n)[:, :, 3:PADL], images(g), images(sq[:]), ALU.mult)\
                        .then_inc(nrm[which].sem, 1)
                else:
                    nc.gpsimd.tensor_tensor(g, g, sq[:], ALU.mult).then_inc(nrm[which].sem, 1)

            def unit(n, d, first=False, ahead=True, late=True):
                for k in range(NS):
                    for state in later(n, d, k, 1, ahead):
                        drive(*state)
                    if ahead:
                        project(*following(n, d), k)
                    if k == 2 and d == 1 and late:
                        norm(LN_FF, n - 1)
                    if k == 2 and not first:
                        gate(*preceding(n, d))
                    if k == 9 and not first:
                        norm(LN_F, n) if d else norm(LN_B, n - 1)
                    if k == 13 and d == 1 and late:
                        norm(LN_X, n - 1)

            for k in range(NS):
                project(0, 0, k)
            drive(0, 0, 0)
            unit(0, 0, first=True)
            unit(0, 1, late=False)
            with pool.Fori(1, G - 1) as n:
                unit(n, 0)
                unit(n, 1)
            unit(G - 1, 0)
            unit(G - 1, 1, ahead=False)
            gate(G - 1, 1)
            for which in (LN_B, LN_FF, LN_X):
                norm(which, G - 1)

        @block.vector
        def _(dve):
            for sig in (s.bc1, s.res1, s.relu, s.poly, s.xc, s.zs, s.st, s.hc, s.yd, s.h2, s.hn, s.sums):
                sig.seed(dve)

            def project(n, d, k):
                step = lambda i: s.poly.at(n, 6 * d + i)
                if k == 5:
                    dve.wait_ge(s.xb.sem, s.xb.at(n, 2 * d + 2))
                    dve.wait_ge(s.th.sem, s.th.at(n, 2 * d + 2))
                    nc.vector.scalar_tensor_tensor(out=xc[:, d], in0=v[:], scalar=1.0, in1=xc[:, d], op0=ALU.add,
                                                   op1=ALU.mult).then_inc(s.xc.sem, 1)
                elif k == 6:
                    dve.wait_ge(s.xp.sem, s.xp.at(n, d + 1))
                    dve.wait_ge(s.cb.sem, s.cb.at(n - 1, NS * (d + 1)))
                    dve.wait_ge(s.bb.sem, s.bb.at(n - 1, NS * (d + 1)))
                    nc.vector.tensor_copy(bc[:, d], proj_ps[0:96, 0:T]).then_inc(s.bc1.sem, 1)
                    dve.wait_ge(s.bc1.sem, s.bc1.at(n, d + 1))
                    dve.wait_ge(s.part2.sem, s.part2.at(n, d))
                    dve.wait_ge(s.res2.sem, s.res2.at(n, d))
                    dve.wait_ge(cen[LN_FF].sem, cen[LN_FF].at(n - 2))
                    nc.vector.tensor_tensor(res1, proj_ps[0:96, 0:T], bc[:, d], ALU.subtract).then_inc(s.res1.sem, 1)
                elif k == 10:
                    dve.wait_ge(s.mag.sem, s.mag.at(n, d + 1))
                    nc.vector.tensor_scalar(dt[:, d], dt[:, d], 0.0, None, ALU.max).then_inc(s.relu.sem, 1)
                elif k == 11:
                    dve.wait_ge(s.u.sem, s.u.at(n, d + 1))
                    nc.vector.tensor_scalar(v[:], dtx[:, d], EDGE, None, ALU.min).then_inc(s.poly.sem, 1)
                    dve.wait_ge(s.poly.sem, step(1))
                    dve.wait_ge(s.logw.sem, s.logw.at(n, d + 1))
                    nc.vector.scalar_tensor_tensor(out=dtx[:, d], in0=v[:], scalar=-4.0 / 3.0, in1=v[:],
                                                   op0=ALU.add, op1=ALU.mult).then_inc(s.poly.sem, 1)
                    nc.vector.scalar_tensor_tensor(out=mag[:], in0=v[:], scalar=EDGE, in1=mag[:], op0=ALU.is_ge,
                                                   op1=ALU.mult).then_inc(s.poly.sem, 1)
                elif k == 12:
                    dve.wait_ge(s.poly.sem, step(2))
                    nc.vector.scalar_tensor_tensor(out=dtx[:, d], in0=dtx[:, d], scalar=2.0, in1=v[:],
                                                   op0=ALU.add, op1=ALU.mult).then_inc(s.poly.sem, 1)
                    dve.wait_ge(s.poly.sem, step(4))
                    nc.vector.scalar_tensor_tensor(out=dtx[:, d], in0=dtx[:, d], scalar=-4.0, in1=v[:],
                                                   op0=ALU.add, op1=ALU.mult).then_inc(s.poly.sem, 1)
                elif k == 13:
                    dve.wait_ge(s.poly.sem, step(5))
                    nc.vector.scalar_tensor_tensor(out=mag[:], in0=dtx[:, d], scalar=-0.25, in1=mag[:],
                                                   op0=ALU.mult, op1=ALU.add).then_inc(s.poly.sem, 1)

            def scan(n, d, k):
                j = NS * d + k + 1
                dve.wait_ge(s.db.sem, s.db.at(n, j))
                dve.wait_ge(s.hc.sem, s.hc.at(n, j - 2))
                for half in range(2):
                    dve.wait_ge(s.da.sem, s.da.at(n, 2 * j - 1 + half))
                    nc.vector.tensor_tensor_scan(hst[:, k % 2, half], da[:, k % RING, half], db[:, k % 2, half], 0.0,
                                                 ALU.mult, ALU.add).then_inc(s.st.sem, 1)

            def read_out(n, d, k):
                j = NS * d + k + 1
                dve.wait_ge(s.st.sem, s.st.at(n, 2 * j))
                dve.wait_ge(s.cb.sem, s.cb.at(n, j))
                dve.wait_ge(s.ys.sem, s.ys.at(n, j - 2))
                nc.vector.tensor_tensor(hc[:, k % 2], hst[:, k % 2], c_ps[:, k % 2, 0:T].unsqueeze(1).to_broadcast([P, 2, T]),
                                        ALU.mult).then_inc(s.hc.sem, 1)

            def skip(n, d):
                dve.wait_ge(s.ys.sem, s.ys.at(n, NS * (d + 1)))
                dve.wait_ge(s.yz.sem, s.yz.at(n, d))
                for half in range(2):
                    out = images(yd[:, half])
                    nc.vector.scalar_tensor_tensor(out=out[:, :, ::-1] if d else out, in0=images(xc[:, d, half]),
                                                   scalar=S.skip_half[:, d, half:half + 1],
                                                   in1=images(y_ps[:, half, 0:T]),
                                                   op0=ALU.mult, op1=ALU.add).then_inc(s.yd.sem, 1)

            def half_sum(n):
                dve.wait_ge(nrm[LN_F].sem, nrm[LN_F].at(n))
                dve.wait_ge(nrm[LN_B].sem, nrm[LN_B].at(n))
                dve.wait_ge(cen[LN_FF].sem, cen[LN_FF].at(n - 1))
                nc.vector.scalar_tensor_tensor(out=h2[:], in0=cg[:, 0], scalar=S.b_half[:], in1=cg[:, 1],
                                               op0=ALU.add, op1=ALU.add).then_inc(s.h2.sem, 1)

            def residual(n):
                dve.wait_ge(nrm[LN_FF].sem, nrm[LN_FF].at(n))
                nc.vector.scalar_tensor_tensor(out=h_of(n), in0=cg[:, LN_FF % 2], scalar=col(S, "ff_b"), in1=h_of(n),
                                               op0=ALU.add, op1=ALU.add).then_inc(s.hn.sem, 1)

            def token_sums(n):
                dve.wait_ge(nrm[LN_X].sem, nrm[LN_X].at(n))
                nc.vector.tensor_reduce(S.sums[:, bass.ds(n * PAIR, PAIR)], x_of(n)[:, :, 3:PADL], AXX, ALU.add)\
                    .then_inc(s.sums.sem, 1)

            def unit(n, d, first=False, ahead=True, late=True):
                for k in range(NS):
                    scan(n, d, k)
                    if k == 1 and not first:
                        skip(*preceding(n, d))
                    if k > 0:
                        read_out(n, d, k - 1)
                    elif not first:
                        read_out(*preceding(n, d), NS - 1)
                    if ahead:
                        project(*following(n, d), k)
                    if k == 7:
                        dve.wait_ge(s.zr.sem, s.zr.at(n, 2 * d + 2))
                        dve.wait_ge(s.zt.sem, s.zt.at(n, 2 * d + 2))
                        nc.vector.scalar_tensor_tensor(out=zs[:, d], in0=mag[:], scalar=1.0, in1=zs[:, d], op0=ALU.add,
                                                       op1=ALU.mult).then_inc(s.zs.sem, 1)
                    if k == 10 and d == 0 and not first:
                        half_sum(n - 1)
                    if k == 4 and d == 1 and late:
                        residual(n - 1)
                    if k == 14 and d == 1 and late:
                        token_sums(n - 1)

            nc.vector.memset(da[:], 0.0).then_inc(cleared, 1)
            nc.vector.memset(xflip[:], 0.0).then_inc(cleared, 1)
            for k in range(NS):
                project(0, 0, k)
            unit(0, 0, first=True)
            unit(0, 1, late=False)
            with dve.Fori(1, G - 1) as n:
                unit(n, 0)
                unit(n, 1)
            unit(G - 1, 0)
            unit(G - 1, 1, ahead=False)
            read_out(G - 1, 1, NS - 1)
            skip(G - 1, 1)
            half_sum(G - 1)
            residual(G - 1)
            token_sums(G - 1)


def route(nc, S, I):
    B = S.B
    with ExitStack() as ctx:
        def sb(name, shape):
            return ctx.enter_context(nc.sbuf_tensor(f"rt_{name}", shape, F32))
        rw, keys, pw = sb("rw", [P, NPART]), sb("keys", [B, NPART]), sb("pw", [NPART, EXP * D])
        lg, pr, eq, rest, one, two, sel = (sb(x, [B, NPART]) for x in ("lg", "pr", "eq", "rest", "one", "two", "sel"))
        selt = sb("selt", [NPART, B])
        sc = sb("sc", [B, 8])
        ps = ctx.enter_context(nc.psum_tensor("rt_ps", [P, 3, 512], F32))
        loaded = ctx.enter_context(nc.semaphore("rt_loaded"))
        logits = ctx.enter_context(nc.semaphore("rt_logits"))
        shifted = ctx.enter_context(nc.semaphore("rt_shifted"))
        expd = ctx.enter_context(nc.semaphore("rt_exp"))
        chosen = ctx.enter_context(nc.semaphore("rt_chosen"))
        turned = ctx.enter_context(nc.semaphore("rt_turned"))
        copied = ctx.enter_context(nc.semaphore("rt_copied"))
        spread = ctx.enter_context(nc.semaphore("rt_spread"))
        step = ctx.enter_context(nc.semaphore("rt_dve_step"))
        block = ctx.enter_context(nc.Block())

        @block.sync
        def _(sp):
            sp.dma_start(rw[:], I.router_w).then_inc(loaded, 16)
            sp.dma_start(keys[:], I.keys[0:B, :]).then_inc(loaded, 16)
            sp.dma_start(pw[:], I.part_w).then_inc(loaded, 16)
            sp.dma_start(S.mw1[:], I.moe_w1).then_inc(loaded, 16)
            sp.dma_start(S.mw2[:], I.moe_w2).then_inc(loaded, 16)

        @block.tensor
        def _(pe):
            pe.wait_ge(loaded, 16 * 5)
            nc.tensor.matmul(ps[0:B, 0, 0:NPART], S.sums[:], rw[:], start=True, stop=True).then_inc(logits, 1)
            pe.wait_ge(chosen, 1)
            nc.tensor.transpose(ps[0:NPART, 1, 0:B], sel[:], S.ident[0:B, 0:B]).then_inc(turned, 1)
            pe.wait_ge(copied, 1)
            for e in range(EXP):
                mm = nc.tensor.matmul(ps[:, 2, e * B:(e + 1) * B], pw[:, e * D:(e + 1) * D], selt[:], start=True, stop=True)
            mm.then_inc(spread, 1)

        @block.scalar
        def _(act):
            act.wait_ge(shifted, 1)
            nc.scalar.activation(pr[:], lg[:], ACT.Exp).then_inc(expd, 1)

        @block.vector
        def _(dve):
            done = [0]

            def then(ins):
                done[0] += 1
                ins.then_inc(step, 1)
                dve.wait_ge(step, done[0])

            v = nc.vector
            dve.wait_ge(logits, 1)
            then(v.tensor_scalar(eq[:], ps[0:B, 0, 0:NPART], 1.0 / L, None, ALU.mult))
            then(v.tensor_reduce(sc[:, 0:1], eq[:], AXX, ALU.max))
            v.tensor_scalar(lg[:], eq[:], sc[:, 0:1], None, ALU.subtract).then_inc(shifted, 1)
            dve.wait_ge(expd, 1)
            then(v.tensor_reduce(sc[:, 1:2], pr[:], AXX, ALU.add))
            then(v.reciprocal(sc[:, 2:3], sc[:, 1:2]))
            then(v.tensor_scalar(rest[:], pr[:], sc[:, 2:3], None, ALU.mult))
            for hot, c in ((one, 3), (two, 4)):
                then(v.tensor_reduce(sc[:, c:c + 1], rest[:], AXX, ALU.max))
                then(v.scalar_tensor_tensor(out=eq[:], in0=rest[:], scalar=sc[:, c:c + 1], in1=keys[:],
                                            op0=ALU.is_equal, op1=ALU.mult))
                then(v.tensor_reduce(sc[:, 5:6], eq[:], AXX, ALU.max))
                then(v.tensor_scalar(hot[:], eq[:], sc[:, 5:6], None, ALU.is_equal))
                if hot is one:
                    then(v.scalar_tensor_tensor(out=rest[:], in0=one[:], scalar=-2.0, in1=rest[:],
                                                op0=ALU.mult, op1=ALU.add))
            then(v.tensor_tensor(sc[:, 6:7], sc[:, 3:4], sc[:, 4:5], ALU.add))
            then(v.reciprocal(sc[:, 7:8], sc[:, 6:7]))
            then(v.tensor_scalar(sc[:, 3:5], sc[:, 3:5], sc[:, 7:8], None, ALU.mult))
            then(v.tensor_scalar(eq[:], one[:], sc[:, 3:4], None, ALU.mult))
            v.scalar_tensor_tensor(out=sel[:], in0=two[:], scalar=sc[:, 4:5], in1=eq[:], op0=ALU.mult,
                                   op1=ALU.add).then_inc(chosen, 1)
            dve.wait_ge(turned, 1)
            v.tensor_copy(selt[:], ps[0:NPART, 1, 0:B]).then_inc(copied, 1)
            dve.wait_ge(spread, 1)
            then(v.tensor_copy(S.ew[:], ps[:, 2, 0:EXP * B]))
            then(v.scalar_tensor_tensor(out=S.ew[:], in0=S.ew[:], scalar=1e-6, in1=S.ew[:], op0=ALU.is_gt,
                                        op1=ALU.mult))
            then(v.tensor_scalar(S.eb[:], S.ew[:, 0:B], col(S, "moe_b2", 0), None, ALU.mult))
            for e in range(1, EXP):
                then(v.scalar_tensor_tensor(out=S.eb[:], in0=S.ew[:, e * B:(e + 1) * B], scalar=col(S, "moe_b2", e),
                                            in1=S.eb[:], op0=ALU.mult, op1=ALU.add))


def experts(nc, S, I):
    G = S.G
    with ExitStack() as ctx:
        gl = ctx.enter_context(nc.sbuf_tensor("ex_gl", [P, 4, T], F32))
        up_ps = ctx.enter_context(nc.psum_tensor("ex_up_ps", [P, 4, 512], F32))
        out_ps = ctx.enter_context(nc.psum_tensor("ex_out_ps", [P, 2, 512], F32))
        s = signals(ctx, nc, "ex", up=EXP * EC, gl=EXP * EC, down=EXP, biased=1, added=2 * EXP)
        used = Signal(ctx, nc, "ex_used", EXP * EC)
        block = ctx.enter_context(nc.Block())
        N = EXP * EC
        LEAD = 2

        @block.tensor
        def _(pe):
            for sig in (s.up, s.down, used):
                sig.seed(pe)
            with pe.Fori(0, G) as n:
                xn = S.X[:, bass.ds(n * XP, XP)].rearrange("q (b t) -> q b t", b=PAIR)[:, :, 3:PADL]
                for c in range(N + LEAD):
                    if c < N:
                        pe.wait_ge(s.gl.sem, s.gl.at(n, c + 1 - 4))
                        nc.tensor.matmul(up_ps[:, c % 4, 0:T], S.mw1[:, c * D:(c + 1) * D], xn, start=True,
                                         stop=True).then_inc(s.up.sem, 1)
                    k = c - LEAD
                    if k >= 0:
                        e, part = k // EC, k % EC
                        pe.wait_ge(s.gl.sem, s.gl.at(n, k + 1))
                        if part == 0:
                            pe.wait_ge(s.added.sem, s.added.at(n, 2 * (e + 1) - 4))
                        mm = nc.tensor.matmul(out_ps[:, e % 2, 0:T], S.mw2[:, k * D:(k + 1) * D], gl[:, k % 4],
                                              start=(part == 0), stop=(part == EC - 1))
                        mm.then_inc(used.sem, 1)

        @block.scalar
        def _(act):
            s.gl.seed(act)
            with act.Fori(0, G) as n:
                for c in range(N):
                    act.wait_ge(s.up.sem, s.up.at(n, c + 1))
                    act.wait_ge(used.sem, used.at(n, c + 1 - 4))
                    nc.scalar.activation(gl[:, c % 4], up_ps[:, c % 4, 0:T], ACT.Gelu, bias=col(S, "moe_b1", c))\
                        .then_inc(s.gl.sem, 1)

        @block.vector
        def _(dve):
            s.added.seed(dve)
            s.biased.seed(dve)
            with dve.Fori(0, G) as n:
                for e in range(EXP):
                    dve.wait_ge(used.sem, used.at(n, (e + 1) * EC))
                    for b in range(PAIR):
                        hb = S.h[:, bass.ds(n * T + b * L, L)]
                        if e == 0:
                            nc.vector.tensor_scalar(hb, hb, S.eb[:, bass.ds(n * PAIR + b, 1)], None, ALU.add)\
                                .then_inc(s.biased.sem, 1)
                    if e == 0:
                        dve.wait_ge(s.biased.sem, 2 * n + 4)
                    else:
                        dve.wait_ge(s.added.sem, s.added.at(n, 2 * e))
                    for b in range(PAIR):
                        hb = S.h[:, bass.ds(n * T + b * L, L)]
                        nc.vector.scalar_tensor_tensor(
                            out=hb, in0=out_ps[:, e % 2, b * L:(b + 1) * L],
                            scalar=S.ew[:, bass.ds(n * PAIR + b + e * S.B, 1)], in1=hb, op0=ALU.mult,
                            op1=ALU.add).then_inc(s.added.sem, 1)


def spectrum(nc, S, I):
    G, B = S.G, S.B
    L2 = L - P
    with ExitStack() as ctx:
        def sb(name, shape):
            return ctx.enter_context(nc.sbuf_tensor(f"sp_{name}", shape, F32))
        dft = sb("dft", [P, 2, 3 * MODES])
        sq, rec, y = (sb(x, [P, 2, T]) for x in ("sq", "rec", "y"))
        yt = sb("yt", [P, PAIR, 2, D])
        cen_ps, var_ps, t_ps, f_ps = (ctx.enter_context(nc.psum_tensor(f"sp_{x}", [P, 2, 512], F32))
                                      for x in ("cen_ps", "var_ps", "t_ps", "f_ps"))
        loaded = ctx.enter_context(nc.semaphore("sp_loaded"))
        s = signals(ctx, nc, "sp", cen=1, sq=1, var=1, log=1, rec=1, y=1, turn=2, yt=2, freq=2, q=2)
        block = ctx.enter_context(nc.Block())
        Qv = S.Q[:].rearrange("q (m c b) -> q c m b", m=MODES, c=3)

        @block.sync
        def _(sp):
            sp.dma_start(dft[:, 0], I.dft[0:P]).then_inc(loaded, 16)
            sp.dma_start(dft[0:L2, 1], I.dft[P:L]).then_inc(loaded, 16)

        @block.tensor
        def _(pe):
            for sig in (s.cen, s.var, s.turn, s.freq):
                sig.seed(pe)
            pe.wait_ge(loaded, 32)
            with pe.Fori(0, G // 2) as i:
                for p in range(2):
                    n = 2 * i + p
                    pe.wait_ge(s.y.sem, s.y.at(n - 2))
                    nc.tensor.matmul(cen_ps[:, p, 0:T], S.center[:], S.h[:, bass.ds(n * T, T)], start=True, stop=True)\
                        .then_inc(s.cen.sem, 1)
                    pe.wait_ge(s.sq.sem, s.sq.at(n))
                    pe.wait_ge(s.log.sem, s.log.at(n - 2))
                    nc.tensor.matmul(var_ps[:, p, 0:T], S.mean[:], sq[:, p], start=True, stop=True)\
                        .then_inc(s.var.sem, 1)
                    pe.wait_ge(s.y.sem, s.y.at(n))
                    for b in range(PAIR):
                        pe.wait_ge(s.yt.sem, s.yt.at(n - 1, b + 1))
                        nc.tensor.transpose(t_ps[:, b, 0:D], y[:, p, b * L:b * L + P], S.ident[:])
                        nc.tensor.transpose(t_ps[0:L2, b, D:2 * D], y[:, p, b * L + P:(b + 1) * L], S.ident[:])\
                            .then_inc(s.turn.sem, 1)
                    for b in range(PAIR):
                        pe.wait_ge(s.yt.sem, s.yt.at(n, b + 1))
                        pe.wait_ge(s.q.sem, s.q.at(n - 1, b + 1))
                        nc.tensor.matmul(f_ps[:, b, 0:3 * MODES], yt[:, b, 0], dft[:, 0], start=True, stop=False)
                        nc.tensor.matmul(f_ps[:, b, 0:3 * MODES], yt[0:L2, b, 1], dft[0:L2, 1], start=False, stop=True)\
                            .then_inc(s.freq.sem, 1)

        @block.scalar
        def _(act):
            for sig in (s.sq, s.log, s.rec, s.q):
                sig.seed(act)
            act.preload_act_table_set(LOG_EXP)
            with act.Fori(0, G // 2) as i:
                for p in range(2):
                    n = 2 * i + p
                    act.wait_ge(s.cen.sem, s.cen.at(n))
                    act.wait_ge(s.var.sem, s.var.at(n - 2))
                    nc.scalar.activation(sq[:, p], cen_ps[:, p, 0:T], ACT.Square).then_inc(s.sq.sem, 1)
                    act.wait_ge(s.var.sem, s.var.at(n))
                    act.wait_ge(s.y.sem, s.y.at(n - 2))
                    nc.scalar.activation(rec[:, p], var_ps[:, p, 0:T], ACT.Ln, bias=S.eps[:]).then_inc(s.log.sem, 1)
                    act.wait_ge(s.log.sem, s.log.at(n))
                    nc.scalar.activation(rec[:, p], rec[:, p], ACT.Exp, scale=-0.5).then_inc(s.rec.sem, 1)
                    for b in range(PAIR):
                        act.wait_ge(s.freq.sem, s.freq.at(n, b + 1))
                        nc.scalar.activation(Qv[:, :, :, bass.ds(n * PAIR + b, 1)],
                                             f_ps[:, b, 0:3 * MODES].rearrange("q (c m o) -> q c m o", c=3, o=1), ACT.Copy)\
                            .then_inc(s.q.sem, 1)

        @block.vector
        def _(dve):
            for sig in (s.y, s.yt):
                sig.seed(dve)
            with dve.Fori(0, G // 2) as i:
                for p in range(2):
                    n = 2 * i + p
                    dve.wait_ge(s.rec.sem, s.rec.at(n))
                    dve.wait_ge(s.turn.sem, s.turn.at(n - 2))
                    nc.vector.tensor_tensor(y[:, p], cen_ps[:, p, 0:T], rec[:, p], ALU.mult).then_inc(s.y.sem, 1)
                    for b in range(PAIR):
                        dve.wait_ge(s.turn.sem, s.turn.at(n, b + 1))
                        dve.wait_ge(s.freq.sem, s.freq.at(n - 1, b + 1))
                        nc.vector.tensor_copy(yt[:, b, 0], t_ps[:, b, 0:D])
                        nc.vector.tensor_copy(yt[0:L2, b, 1], t_ps[0:L2, b, D:2 * D]).then_inc(s.yt.sem, 1)


def mix(nc, S, I):
    B = S.B
    NB = MODES // MB
    with ExitStack() as ctx:
        w = ctx.enter_context(nc.sbuf_tensor("mx_w", [P, 4, MB, 2, D], F32))
        ps = ctx.enter_context(nc.psum_tensor("mx_ps", [P, 4, 512], F32))
        wl = [Signal(ctx, nc, f"mx_wl{p}", 1, 16) for p in range(4)]
        s = signals(ctx, nc, "mx", mul=4, o=4)
        block = ctx.enter_context(nc.Block())
        Ov = S.O[:].rearrange("q (b c m) -> q m c b", c=2, m=MODES)

        @block.sync
        def _(sp):
            for p in range(4):
                wl[p].seed(sp)
            with sp.Fori(0, NB // 4) as i:
                for p in range(4):
                    sp.wait_ge(s.mul.sem, s.mul.at(i, p + 1 - 4))
                    sp.dma_start(w[:, p].rearrange("q m c e -> q (m c e)"),
                                   I.modes_w[bass.ds(4 * i + p, 1)].rearrange("o q t -> (o q) t"))\
                        .then_inc(wl[p].sem, 16)

        @block.tensor
        def _(pe):
            s.mul.seed(pe)
            with pe.Fori(0, NB // 4) as i:
                for p in range(4):
                    pe.wait_ge(wl[p].sem, wl[p].at(i))
                    pe.wait_ge(s.o.sem, s.o.at(i, p + 1 - 4))
                    for m in range(MB):
                        out = ps[:, p, m * 2 * B:(m + 1) * 2 * B]
                        at = ((4 * i + p) * MB + m) * 3 * B
                        nc.tensor.matmul(out, w[:, p, m, 0], S.Q[:, bass.ds(at + B, 2 * B)], start=True, stop=False,
                                         skip_group_check=True)
                        mm = nc.tensor.matmul(out, w[:, p, m, 1], S.Q[:, bass.ds(at, 2 * B)], start=False, stop=True,
                                              skip_group_check=True)
                    mm.then_inc(s.mul.sem, 1)

        @block.vector
        def _(dve):
            s.o.seed(dve)
            with dve.Fori(0, NB // 4) as i:
                for p in range(4):
                    dve.wait_ge(s.mul.sem, s.mul.at(i, p + 1))
                    nc.vector.tensor_copy(Ov[:, bass.ds((4 * i + p) * MB, MB)],
                                          ps[:, p, 0:MB * 2 * B].rearrange("q (m c b) -> q m c b", m=MB, c=2))\
                        .then_inc(s.o.sem, 1)


def finish(nc, S, I, out):
    G = S.G
    with ExitStack() as ctx:
        def sb(name, shape):
            return ctx.enter_context(nc.sbuf_tensor(f"fi_{name}", shape, F32))
        idft = sb("idft", [P, L])
        of = sb("of", [P, PAIR, P])
        ot = sb("ot", [P, PAIR, D])
        hv, sq, rec, nrm, res = (sb(x, [P, 2, T]) for x in ("hv", "sq", "rec", "nrm", "res"))
        t_ps, i_ps, cen_ps, var_ps = (ctx.enter_context(nc.psum_tensor(f"fi_{x}", [P, 2, 512], F32))
                                      for x in ("t_ps", "i_ps", "cen_ps", "var_ps"))
        loaded = ctx.enter_context(nc.semaphore("fi_loaded"))
        s = signals(ctx, nc, "fi", of=1, turn=1, ot=1, inv=1, hv=1, cen=1, sq=1, var=1, log=1, rec=1, nrm=1, res=1)
        stored = [Signal(ctx, nc, f"fi_stored{p}", 1, 16) for p in range(2)]
        block = ctx.enter_context(nc.Block())

        @block.sync
        def _(sp):
            for p in range(2):
                stored[p].seed(sp)
            sp.dma_start(idft[:], I.idft).then_inc(loaded, 16)
            with sp.Fori(0, G // 2) as i:
                for p in range(2):
                    sp.wait_ge(s.res.sem, s.res.at(2 * i + p))
                    sp.dma_start(out[bass.ds(2 * i + p, 1)].rearrange("o q t -> (o q) t"), res[:, p])\
                        .then_inc(stored[p].sem, 16)
            for p in range(2):
                sp.wait_ge(stored[p].sem, stored[p].at(G // 2 - 1))

        @block.tensor
        def _(pe):
            for sig in (s.turn, s.inv, s.cen, s.var):
                sig.seed(pe)
            pe.wait_ge(loaded, 16)
            with pe.Fori(0, G // 2) as i:
                for p in range(2):
                    n = 2 * i + p
                    pe.wait_ge(s.of.sem, s.of.at(n))
                    pe.wait_ge(s.ot.sem, s.ot.at(n - 2))
                    for b in range(PAIR):
                        mm = nc.tensor.transpose(t_ps[:, p, b * D:(b + 1) * D], of[:, b], S.ident[:])
                    mm.then_inc(s.turn.sem, 1)
                    pe.wait_ge(s.ot.sem, s.ot.at(n))
                    pe.wait_ge(s.hv.sem, s.hv.at(n - 2))
                    for b in range(PAIR):
                        mm = nc.tensor.matmul(i_ps[:, p, b * L:(b + 1) * L], ot[:, b], idft[:], start=True, stop=True)
                    mm.then_inc(s.inv.sem, 1)
                    pe.wait_ge(s.hv.sem, s.hv.at(n))
                    pe.wait_ge(s.nrm.sem, s.nrm.at(n - 2))
                    nc.tensor.matmul(cen_ps[:, p, 0:T], S.center[:], hv[:, p], start=True, stop=True)\
                        .then_inc(s.cen.sem, 1)
                    pe.wait_ge(s.sq.sem, s.sq.at(n))
                    pe.wait_ge(s.log.sem, s.log.at(n - 2))
                    nc.tensor.matmul(var_ps[:, p, 0:T], S.mean[:], sq[:, p], start=True, stop=True)\
                        .then_inc(s.var.sem, 1)

        @block.scalar
        def _(act):
            for sig in (s.ot, s.sq, s.log, s.rec):
                sig.seed(act)
            act.preload_act_table_set(LOG_EXP)
            with act.Fori(0, G // 2) as i:
                for p in range(2):
                    n = 2 * i + p
                    act.wait_ge(s.turn.sem, s.turn.at(n))
                    act.wait_ge(s.inv.sem, s.inv.at(n - 1))
                    nc.scalar.activation(ot[:], t_ps[:, p, 0:PAIR * D].rearrange("q (b e) -> q b e", b=PAIR), ACT.Copy)\
                        .then_inc(s.ot.sem, 1)
                    act.wait_ge(s.cen.sem, s.cen.at(n))
                    act.wait_ge(s.var.sem, s.var.at(n - 2))
                    nc.scalar.activation(sq[:, p], cen_ps[:, p, 0:T], ACT.Square).then_inc(s.sq.sem, 1)
                    act.wait_ge(s.var.sem, s.var.at(n))
                    act.wait_ge(s.nrm.sem, s.nrm.at(n - 2))
                    nc.scalar.activation(rec[:, p], var_ps[:, p, 0:T], ACT.Ln, bias=S.eps[:]).then_inc(s.log.sem, 1)
                    act.wait_ge(s.log.sem, s.log.at(n))
                    nc.scalar.activation(rec[:, p], rec[:, p], ACT.Exp, scale=-0.5).then_inc(s.rec.sem, 1)

        @block.gpsimd
        def _(pool):
            for sig in (s.of, s.res):
                sig.seed(pool)
            with pool.Fori(0, G // 2) as i:
                for p in range(2):
                    n = 2 * i + p
                    pool.wait_ge(s.turn.sem, s.turn.at(n - 1))
                    nc.gpsimd.tensor_copy(of[:].rearrange("q b m -> q (b m)"), S.O[:, bass.ds(n * PAIR * P, PAIR * P)])\
                        .then_inc(s.of.sem, 1)
                    pool.wait_ge(s.nrm.sem, s.nrm.at(n))
                    pool.wait_ge(stored[p].sem, stored[p].at(i - 1))
                    nc.gpsimd.tensor_tensor(res[:, p], nrm[:, p], hv[:, p], ALU.add).then_inc(s.res.sem, 1)

        @block.vector
        def _(dve):
            for sig in (s.hv, s.nrm):
                sig.seed(dve)
            with dve.Fori(0, G // 2) as i:
                for p in range(2):
                    n = 2 * i + p
                    dve.wait_ge(s.inv.sem, s.inv.at(n))
                    dve.wait_ge(s.res.sem, s.res.at(n - 2))
                    nc.vector.tensor_tensor(hv[:, p], S.h[:, bass.ds(n * T, T)], i_ps[:, p, 0:T], ALU.add)\
                        .then_inc(s.hv.sem, 1)
                    dve.wait_ge(s.rec.sem, s.rec.at(n))
                    nc.vector.tensor_tensor(nrm[:, p], cen_ps[:, p, 0:T], rec[:, p], ALU.mult).then_inc(s.nrm.sem, 1)


def vit_tower(nc, I, out):
    G = I.pixels.shape[0]
    B = G * PAIR
    with ExitStack() as ctx:
        def sb(name, shape, dt=F32):
            return ctx.enter_context(nc.sbuf_tensor(name, shape, dt))

        S = Shared()
        S.G, S.B = G, B
        S.center, S.mean, S.ident = sb("center", [P, D]), sb("mean", [P, D]), sb("ident", [P, D])
        S.cols, S.eps, S.past_edge = sb("cols", [P, NCOLS]), sb("eps", [P, 1]), sb("past_edge", [P, 1])
        S.h = sb("h", [P, B * L])
        S.sums = sb("sums", [P, B])
        S.tok_bias_c, S.ffn_b2_c, S.ffn_b2_cg = sb("tok_bias_c", [P, 1]), sb("ffn_b2_c", [P, 1]), sb("ffn_b2_cg", [P, 1])
        S.g_half, S.b_half = sb("g_half", [P, 2]), sb("b_half", [P, 1])
        S.conv_b_half, S.skip_half = sb("conv_b_half", [P, 2, 2]), sb("skip_half", [P, 2, 2])
        with ExitStack() as held:
            S.X = held.enter_context(nc.sbuf_tensor("X", [P, B * PADL], F32))
            with ExitStack() as weights:
                def wt(name, shape, dt=F32):
                    return weights.enter_context(nc.sbuf_tensor(name, shape, dt))
                S.neg_a = wt("neg_a", [P, 2, 2, NS])
                S.sel = wt("sel", [96, 2 * NS], BF16)
                S.convw, S.zw = wt("convw", [P, 2, TAPS, 2 * D]), wt("zw", [P, 2, 2 * D])
                S.xpw, S.dtw = wt("xpw", [P, 2, 2, 96 + R]), wt("dtw", [P, 2, 2 * D])
                S.woc, S.w1, S.w2c = wt("woc", [P, 4 * D]), wt("w1", [P, FF * D]), wt("w2c", [P, FF * D])
                setup(nc, S, I)
                tokens(nc, S, I)
                mamba(nc, S, I)
            with ExitStack() as weights:
                S.ew = weights.enter_context(nc.sbuf_tensor("ew", [P, EXP * B], F32))
                S.eb = weights.enter_context(nc.sbuf_tensor("eb", [P, B], F32))
                S.mw1 = weights.enter_context(nc.sbuf_tensor("mw1", [P, EXP * EC * D], F32))
                S.mw2 = weights.enter_context(nc.sbuf_tensor("mw2", [P, EXP * EC * D], F32))
                route(nc, S, I)
                experts(nc, S, I)
        S.O = sb("O", [P, B * 2 * MODES])
        with ExitStack() as held:
            S.Q = held.enter_context(nc.sbuf_tensor("Q", [P, MODES * 3 * B], F32))
            spectrum(nc, S, I)
            mix(nc, S, I)
        finish(nc, S, I, out)


def laid_out(x):
    f = lambda a: np.ascontiguousarray(np.asarray(a))
    B = x["x"].shape[0]
    G = B // PAIR
    m = {}
    m["pixels"] = x["x"].reshape(G, PAIR, 3, GRID, 2, 8, GRID, 2, 8).transpose(0, 7, 5, 8, 2, 4, 1, 3, 6)\
        .reshape(G, P, CH * TP)
    wm = x["L0_tok_W_main"].reshape(64, 3, 2, 8, 2, 8)
    wx = x["L0_tok_W_sx"].reshape(16, 3, 2, 8, 2, 8)
    wy = x["L0_tok_W_sy"].reshape(16, 3, 2, 8, 2, 8)
    w = np.zeros((3, D, 3, 2, 2, 8, 8), np.float32)
    at = lambda a: a.transpose(0, 1, 2, 4, 3, 5)
    w[0, 0:64] = at(wm)
    w[0, 64:80, :, :, 1] = at(wx)[:, :, :, 0]
    w[0, 80:96, :, :, 0] = at(wx)[:, :, :, 1]
    w[1, 64:80, :, :, 0] = at(wx)[:, :, :, 1]
    w[1, 80:96, :, :, 1] = at(wx)[:, :, :, 0]
    w[0, 96:112, :, 1] = at(wy)[:, :, 0]
    w[0, 112:128, :, 0] = at(wy)[:, :, 1]
    w[2, 96:112, :, 0] = at(wy)[:, :, 1]
    w[2, 112:128, :, 1] = at(wy)[:, :, 0]
    m["tok_w"] = w.transpose(1, 0, 2, 3, 4, 5, 6).reshape(D, 3 * CH, D)
    m["center"] = (np.eye(D) - 1.0 / D).astype(np.float32)
    m["mean"] = np.full((D, D), 1.0 / D, np.float32)
    m["ident"] = np.eye(D, dtype=np.float32)
    m["sel"] = np.tile(np.eye(2 * NS, dtype=np.float32), (3, 1))
    cols = {"tok_bias": np.concatenate([x["L0_tok_b_main"]] + [x["L0_tok_b_sx"]] * 2 + [x["L0_tok_b_sy"]] * 2),
            "tok_g": x["L0_tok_ln_g"], "tok_b": x["L0_tok_ln_b"], "cls": x["cls_tok"].reshape(D),
            "ff_g": x["L0_attn_ln_ff_g"], "ff_b": x["L0_attn_ln_ff_b"],
            "ffn_b1": x["L0_attn_ffn_b1"].reshape(FF, D).T, "ffn_b2": x["L0_attn_ffn_b2"],
            "moe_b2": x["L0_ffn_b2"].T}
    f1 = x["L0_ffn_W1"].shape[2]
    b1 = np.zeros((EXP, EC * D), np.float32)
    b1[:, :f1] = x["L0_ffn_b1"]
    cols["moe_b1"] = b1.reshape(EXP * EC, D).T
    for d, k in enumerate("fb"):
        a = lambda v: x[f"L0_attn_{k}_{v}"]
        cols[f"conv_b{d}"] = a("conv_b").reshape(2, D).T
        cols[f"skip{d}"] = a("D").reshape(2, D).T
        cols[f"dt_b{d}"] = a("dt_b").reshape(2, D).T
        cols[f"a_log{d}"] = a("A_log").reshape(2, D, NS).transpose(1, 0, 2).reshape(D, 2 * NS)
        cols[f"ln_g{d}"] = x[f"L0_attn_ln_{k}_g"]
        cols[f"ln_b{d}"] = x[f"L0_attn_ln_{k}_b"]
    m["cols"] = np.concatenate([np.asarray(cols[k]).reshape(D, wd) for k, (_, wd) in COLS.items()], axis=1)
    both = lambda g: np.stack([g(x, k) for k in "fb"], axis=1)
    m["out_w"] = both(lambda x, k: x[f"L0_attn_{k}_out_w"])
    m["ffn_w2"] = x["L0_attn_ffn_w2"]
    m["in_w_x"] = both(lambda x, k: x[f"L0_attn_{k}_in_w"].T[:, :2 * D])
    m["in_w_z"] = both(lambda x, k: x[f"L0_attn_{k}_in_w"].T[:, 2 * D:])
    m["taps"] = np.broadcast_to(both(lambda x, k: x[f"L0_attn_{k}_conv_w"].T[None])[0], (P, 2, TAPS, 2 * D))

    def xproj(x, k):
        v = x[f"L0_attn_{k}_xproj_w"]
        v = np.concatenate([v[R:]] * 3 + [v[:R]], axis=0)
        return v.T.reshape(2, D, 96 + R).transpose(1, 0, 2)
    m["xproj"] = both(xproj)
    m["dt_w"] = both(lambda x, k: x[f"L0_attn_{k}_dt_w"].T)
    m["ffn_w1"] = x["L0_attn_ffn_w1"].T
    w1 = np.zeros((EXP, D, EC * D), np.float32)
    w1[:, :, :f1] = x["L0_ffn_W1"]
    m["moe_w1"] = w1.transpose(1, 0, 2).reshape(D, EXP * EC * D)
    w2 = np.zeros((EXP, EC * D, D), np.float32)
    w2[:, :f1] = x["L0_ffn_W2"]
    m["moe_w2"] = w2.reshape(EXP * EC, D, D).transpose(1, 0, 2).reshape(D, EXP * EC * D)
    m["router_w"] = x["L0_ffn_router_w"].T
    m["keys"] = np.broadcast_to(np.arange(NPART, 0, -1, dtype=np.float32), (P, NPART))
    parts = [(6,), (5, 1), (4, 2), (4, 1, 1), (3, 3), (3, 2, 1), (3, 1, 1, 1), (2, 2, 2), (2, 2, 1, 1),
             (2, 1, 1, 1, 1), (1, 1, 1, 1, 1, 1)]
    pw = np.zeros((NPART, EXP), np.float32)
    for i, part in enumerate(parts):
        pw[i, :len(part)] = [v / 6 for v in part]
    m["part_w"] = np.broadcast_to(pw[:, :, None], (NPART, EXP, D)).reshape(NPART, EXP * D)
    angle = 2 * np.pi * (np.outer(np.arange(L), np.arange(MODES)) % L) / L
    m["dft"] = np.concatenate([np.sin(angle), np.cos(angle), -np.sin(angle)], axis=1).astype(np.float32)
    twice = np.where(np.arange(MODES) == 0, 1.0, 2.0)[:, None] / L
    m["idft"] = np.concatenate([np.cos(angle).T * twice, -np.sin(angle).T * twice]).astype(np.float32)
    wr, wi = x["L1_attn_weights_real"], x["L1_attn_weights_imag"]
    m["modes_w"] = np.stack([wr, wi]).transpose(3, 1, 0, 2).reshape(MODES // MB, MB, D, 2, D)\
        .transpose(0, 2, 1, 3, 4).reshape(MODES // MB, D, MB * 2 * D)
    return {k: f(v) for k, v in m.items()}


def kernel(**inputs):
    import concourse.bacc as bacc
    from concourse.bass_utils import run_bass_kernel_spmd as run

    arrays = {f"in_{k}": v for k, v in laid_out({k: np.asarray(v) for k, v in inputs.items()}).items()}
    nc = bacc.Bacc("TRN2", target_bir_lowering=False, num_devices=1)
    given = [nc.dram_tensor(k, v.shape, mybir.dt.from_np(v.dtype), kind="ExternalInput").ap() for k, v in arrays.items()]
    I = namedtuple("Inputs", [k[3:] for k in arrays])(*given)
    G = arrays["in_pixels"].shape[0]
    out = nc.dram_tensor("out_0", (G, P, T), F32, kind="ExternalOutput").ap()
    vit_tower(nc, I, out)
    got = run(nc, [arrays], core_ids=[0]).results[0]["out_0"]
    return got.reshape(G, D, PAIR, L).transpose(0, 2, 3, 1).reshape(G * PAIR, L, D)
```

```python
from collections import namedtuple
from contextlib import ExitStack

import concourse.bass as bass
from concourse import mybir
import numpy as np

F32 = mybir.dt.float32
BF16 = mybir.dt.bfloat16
F32R = mybir.dt.float32r
ALU = mybir.AluOpType
ACT = mybir.ActivationFunctionType
AXX = mybir.AxisListType.X

P = 128
D = 128
GRID = 14
NPATCH = GRID * GRID
L = NPATCH + 1
PAIR = 2
T = PAIR * L
TP = PAIR * NPATCH
PADL = L + 3
XP = PAIR * PADL
CH = 6
NS = 16
TAPS = 4
R = 8
FF = 4
EXP = 6
EC = 3
NPART = 11
MODES = 64
MB = 4
RING = 4
EPS = 1e-5
EDGE = 1.0 / 31.0
LOG_EXP = "natural_log_exp_and_others"

COLS = {}
for _name, _width in [("tok_bias", 1), ("tok_g", 1), ("tok_b", 1), ("cls", 1)] + [
        (f"{_v}{_d}", _w) for _d in range(2)
        for _v, _w in (("conv_b", 2), ("skip", 2), ("dt_b", 2), ("a_log", 2 * NS), ("ln_g", 1), ("ln_b", 1))] + [
        ("ff_g", 1), ("ff_b", 1), ("ffn_b1", FF), ("ffn_b2", 1), ("moe_b1", EXP * EC), ("moe_b2", EXP)]:
    COLS[_name] = (sum(w for _, w in COLS.values()), _width)
NCOLS = sum(w for _, w in COLS.values())


class Signal:

    def __init__(self, ctx, nc, name, per=1, unit=1):
        self.sem = ctx.enter_context(nc.semaphore(name))
        self.per, self.unit = per, unit

    def seed(self, eng):
        eng.sem_inc(self.sem, 2 * self.per * self.unit)

    def at(self, n, j=None):
        return (n * self.per + 2 * self.per + (self.per if j is None else j)) * self.unit


class Shared:
    pass


def signals(ctx, nc, prefix, **per):
    made = [Signal(ctx, nc, f"{prefix}_{k}", v) for k, v in per.items()]
    return namedtuple("Signals", list(per))(*made)


def col(S, name, i=0):
    a = COLS[name][0] + i
    return S.cols[:, a:a + 1]


def in_stages(eng, G, lead, step):
    for n in range(-lead, 0):
        step(n, n // 2, n % 2, lambda k: n + k >= 0)
    whole = (G - lead) // 2
    with eng.Fori(0, whole) as i:
        for p in range(2):
            step(2 * i + p, i, p, lambda k: True)
    for n in range(2 * whole, G):
        step(n, n // 2, n % 2, lambda k: n + k < G)


def setup(nc, S, I):
    with ExitStack() as ctx:
        loaded = ctx.enter_context(nc.semaphore("su_loaded"))
        cleared = ctx.enter_context(nc.semaphore("su_cleared"))
        folded_pe = ctx.enter_context(nc.semaphore("su_folded_pe"))
        a_exp = ctx.enter_context(nc.semaphore("su_a_exp"))
        dve_step = ctx.enter_context(nc.semaphore("su_dve_step"))
        out_w = ctx.enter_context(nc.sbuf_tensor("su_out_w", [P, 2, 2 * D], F32))
        w2 = ctx.enter_context(nc.sbuf_tensor("su_w2", [P, FF * D], F32))
        in_w = ctx.enter_context(nc.sbuf_tensor("su_in_w", [P, 2, 2 * D], F32))
        taps = ctx.enter_context(nc.sbuf_tensor("su_taps", [P, 2, TAPS, 2 * D], F32))
        sel = ctx.enter_context(nc.sbuf_tensor("su_sel", [96, 2 * NS], F32))
        ps = ctx.enter_context(nc.psum_tensor("su_ps", [P, 8, 512], F32))
        block = ctx.enter_context(nc.Block())
        loads = [(S.center[:], I.center), (S.mean[:], I.mean), (S.ident[:], I.ident), (sel[:], I.sel),
                 (S.cols[:], I.cols), (out_w[:], I.out_w), (w2[:], I.ffn_w2), (in_w[:], I.in_w_x), (taps[:], I.taps),
                 (S.zw[:], I.in_w_z), (S.xpw[:], I.xproj), (S.dtw[96:96 + R], I.dt_w), (S.w1[:], I.ffn_w1)]

        @block.sync
        def _(sp):
            for dst, src in loads:
                sp.dma_start(dst, src).then_inc(loaded, 16)

        @block.tensor
        def _(pe):
            pe.wait_ge(loaded, 16 * len(loads))
            for d in range(2):
                for half in range(2):
                    nc.tensor.matmul(ps[:, 0, (2 * d + half) * D:(2 * d + half + 1) * D],
                                     out_w[:, d, half * D:(half + 1) * D], S.center[:], start=True, stop=True)
            for k in range(FF):
                nc.tensor.matmul(ps[:, 1, k * D:(k + 1) * D], w2[:, k * D:(k + 1) * D], S.center[:],
                                 start=True, stop=True)
            nc.tensor.matmul(ps[:, 2, 0:1], S.center[:], col(S, "tok_bias"), start=True, stop=True)
            nc.tensor.matmul(ps[:, 2, 1:2], S.center[:], col(S, "ffn_b2"), start=True, stop=True)\
                .then_inc(folded_pe, 1)

        @block.scalar
        def _(act):
            act.wait_ge(loaded, 16 * len(loads))
            nc.scalar.activation(S.sel[:], sel[:], ACT.Copy)
            for d in range(2):
                a = COLS[f"a_log{d}"][0]
                nc.scalar.activation(S.neg_a[:, d], S.cols[:, a:a + 2 * NS].rearrange("p (h s) -> p h s", h=2),
                                     ACT.Exp).then_inc(a_exp, 1)

        @block.gpsimd
        def _(pool):
            nc.gpsimd.memset(S.X[:], 0.0).then_inc(cleared, 1)
            pool.wait_ge(loaded, 16 * len(loads))
            for d in range(2):
                for k in range(TAPS):
                    nc.gpsimd.tensor_tensor(S.convw[:, d, k, :], in_w[:, d, :], taps[:, d, k, :], ALU.mult)

        @block.vector
        def _(dve):
            nc.vector.memset(S.eps[:], EPS)
            nc.vector.memset(S.past_edge[:], 1.0 / (1.0 + EDGE))
            dve.wait_ge(loaded, 16 * len(loads))
            nc.vector.tensor_copy(S.h[:].rearrange("p (b t) -> p b t", t=L)[:, :, 0:1],
                                  col(S, "cls").unsqueeze(1).to_broadcast([P, S.B, 1]))
            for d in range(2):
                nc.vector.tensor_scalar(S.g_half[:, d:d + 1], col(S, f"ln_g{d}"), 0.5, None, ALU.mult)
            nc.vector.tensor_tensor(S.b_half[:], col(S, "ln_b0"), col(S, "ln_b1"), ALU.add).then_inc(dve_step, 1)
            dve.wait_ge(dve_step, 1)
            nc.vector.tensor_scalar(S.b_half[:], S.b_half[:], 0.5, None, ALU.mult)
            nc.vector.tensor_scalar(S.xpw[:], S.xpw[:], 0.5, None, ALU.mult).then_inc(dve_step, 1)
            dve.wait_ge(dve_step, 2)
            parts = S.xpw[:, :, :, 0:96].rearrange("p d h (part bc s) -> p (d h) part bc s", part=3, bc=2)
            for d in range(2):
                for half in range(2):
                    c = parts[:, 2 * d + half, :, 1]
                    nc.vector.tensor_scalar(c, c, 0.5, None, ALU.mult)
                    nc.vector.tensor_scalar(S.conv_b_half[:, d, half:half + 1], col(S, f"conv_b{d}", half), 0.5, None,
                                            ALU.mult)
                    nc.vector.tensor_scalar(S.skip_half[:, d, half:half + 1], col(S, f"skip{d}", half), 0.5, None,
                                            ALU.mult)
            dve.wait_ge(a_exp, 2)
            nc.vector.tensor_scalar(S.neg_a[:], S.neg_a[:], -1.0, None, ALU.mult)
            dve.wait_ge(folded_pe, 1)
            nc.vector.tensor_scalar(S.woc[:], ps[:, 0, :], 0.5, None, ALU.mult)
            nc.vector.tensor_copy(S.w2c[:], ps[:, 1, :])
            nc.vector.tensor_copy(S.tok_bias_c[:], ps[:, 2, 0:1])
            nc.vector.tensor_copy(S.ffn_b2_c[:], ps[:, 2, 1:2]).then_inc(dve_step, 1)
            dve.wait_ge(dve_step, 3)
            nc.vector.tensor_tensor(S.ffn_b2_cg[:], S.ffn_b2_c[:], col(S, "ff_g"), ALU.mult)


def tokens(nc, S, I):
    G = S.G
    M = NPATCH - GRID
    with ExitStack() as ctx:
        def sb(name, shape, dt=F32):
            return ctx.enter_context(nc.sbuf_tensor(f"tk_{name}", shape, dt))

        work = sb("work", [P, 6 * T])
        w_nat = work[:, 0:3 * CH * D].rearrange("q (k d) -> q k d", d=D)
        sq, rec, nrm = (work[:, x * 2 * T:(x + 1) * 2 * T].rearrange("q (p t) -> q p t", p=2) for x in range(3))
        wh, wl = sb("wh", [P, 3 * CH, D], F32R), sb("wl", [P, 3 * CH, D], F32R)
        pix = sb("pix", [P, 2, CH, TP])
        ph, pl, sh, sl = (sb(x, [P, CH, TP], F32R) for x in ("ph", "pl", "sh", "sl"))
        tok_ps, var_ps, cen_ps = (ctx.enter_context(nc.psum_tensor(f"tk_{x}", [P, 2, 512], F32))
                                  for x in ("tok_ps", "var_ps", "cen_ps"))
        wload = ctx.enter_context(nc.semaphore("tk_wload"))
        wfold_pe = ctx.enter_context(nc.semaphore("tk_wfold_pe"))
        wfold = ctx.enter_context(nc.semaphore("tk_wfold"))
        wlow = ctx.enter_context(nc.semaphore("tk_wlow"))
        cleared = ctx.enter_context(nc.semaphore("tk_cleared"))
        s = signals(ctx, nc, "tk", high=CH, low=CH, shifted=4 * CH, tok=CH, sq=1, var=1, log=1, rec=1, nrm=1, h=1,
                    cen=1, sq2=1, var2=1, log2=1, rec2=1, x=1)
        pix_in = [Signal(ctx, nc, f"tk_pix_in{p}", 1, 16) for p in range(2)]
        block = ctx.enter_context(nc.Block())

        def images(ap):
            return ap.rearrange("q (b t) -> q b t", b=PAIR)

        def bank_of(k):
            return (tok_ps, var_ps, cen_ps)[(k % 6) // 2][:, k % 2, 0:D]

        LEAD = 3

        @block.sync
        def _(sp):
            for p in range(2):
                pix_in[p].seed(sp)
            sp.dma_start(w_nat, I.tok_w).then_inc(wload, 16)
            with sp.Fori(0, G // 2) as i:
                for p in range(2):
                    sp.wait_ge(s.low.sem, s.low.at(2 * i + p - 2))
                    sp.dma_start(pix[:, p].rearrange("q c t -> q (c t)"),
                                 I.pixels[bass.ds(2 * i + p, 1)].rearrange("o q t -> (o q) t"))\
                        .then_inc(pix_in[p].sem, 16)

        @block.tensor
        def _(pe):
            for sig in (s.tok, s.var, s.cen, s.var2):
                sig.seed(pe)
            pe.wait_ge(wload, 16)
            for k in range(3 * CH):
                if k >= 6:
                    pe.wait_ge(wlow, k - 5)
                nc.tensor.matmul(bank_of(k), w_nat[:, k], S.center[:], start=True, stop=True).then_inc(wfold_pe, 1)
            pe.wait_ge(wlow, 3 * CH)

            def three(out, k, high, low, first=False, last=False):
                nc.tensor.matmul(out, wh[:, k], high, start=first, stop=False, skip_group_check=True)
                nc.tensor.matmul(out, wh[:, k], low, start=False, stop=False, skip_group_check=True)
                return nc.tensor.matmul(out, wl[:, k], high, start=False, stop=last, skip_group_check=True)

            def chunk(n, p, c):
                acc = tok_ps[:, p, 0:TP]
                if c == 0:
                    pe.wait_ge(s.nrm.sem, s.nrm.at(n - 2))
                pe.wait_ge(s.high.sem, s.high.at(n, c + 1))
                pe.wait_ge(s.low.sem, s.low.at(n, c + 1))
                three(acc, c, ph[:, c], pl[:, c], first=(c == 0))
                a, b = (0, GRID) if c % 2 == 0 else (GRID, 0)
                three(images(acc)[:, :, a:a + M], 2 * CH + c, images(ph[:, c])[:, :, b:b + M],
                      images(pl[:, c])[:, :, b:b + M])
                pe.wait_ge(s.shifted.sem, s.shifted.at(n, 4 * (c + 1)))
                three(acc, CH + c, sh[:, c], sl[:, c], last=(c == CH - 1)).then_inc(s.tok.sem, 1)

            def step(n, i, p, live):
                for c in range(CH):
                    if live(2):
                        chunk(n + 2, p, c)
                    if live(1) and c == 1:
                        pe.wait_ge(s.sq.sem, s.sq.at(n + 1))
                        pe.wait_ge(s.log2.sem, s.log2.at(n - 1))
                        nc.tensor.matmul(var_ps[:, 1 - p, 0:TP], S.mean[:], sq[:, 1 - p, 0:TP], start=True, stop=True)\
                            .then_inc(s.var.sem, 1)
                    if live(1) and c == 4:
                        pe.wait_ge(s.h.sem, s.h.at(n + 1))
                        pe.wait_ge(s.x.sem, s.x.at(n - 1))
                        nc.tensor.matmul(cen_ps[:, 1 - p, 0:T], S.center[:], S.h[:, bass.ds((n + 1) * T, T)],
                                         start=True, stop=True).then_inc(s.cen.sem, 1)
                if live(1):
                    pe.wait_ge(s.sq2.sem, s.sq2.at(n + 1))
                    nc.tensor.matmul(var_ps[:, 1 - p, 0:T], S.mean[:], sq[:, 1 - p], start=True, stop=True)\
                        .then_inc(s.var2.sem, 1)

            in_stages(pe, G, LEAD, step)

        @block.scalar
        def _(act):
            for sig in (s.high, s.sq, s.log, s.rec, s.sq2, s.log2, s.rec2):
                sig.seed(act)

            def inverse_root(n, p, width, var, log, rec_done):
                act.wait_ge(var.sem, var.at(n))
                nc.scalar.activation(rec[:, p, 0:width], var_ps[:, p, 0:width], ACT.Ln, bias=S.eps[:])\
                    .then_inc(log.sem, 1)
                act.wait_ge(log.sem, log.at(n))
                nc.scalar.activation(rec[:, p, 0:width], rec[:, p, 0:width], ACT.Exp, scale=-0.5)\
                    .then_inc(rec_done.sem, 1)

            def step(n, i, p, live):
                if live(1):
                    act.wait_ge(s.tok.sem, s.tok.at(n + 1))
                    act.wait_ge(s.var2.sem, s.var2.at(n - 1))
                    nc.scalar.activation(sq[:, 1 - p, 0:TP], tok_ps[:, 1 - p, 0:TP], ACT.Square, bias=S.tok_bias_c[:])\
                        .then_inc(s.sq.sem, 1)
                if live(0):
                    act.wait_ge(s.nrm.sem, s.nrm.at(n))
                    inverse_root(n, p, T, s.var2, s.log2, s.rec2)
                for c in range(CH):
                    if live(3):
                        if c == 0:
                            act.wait_ge(pix_in[1 - p].sem, pix_in[1 - p].at(i + 1 + p))
                        act.wait_ge(s.tok.sem, s.tok.at(n + 2, c + 1))
                        act.wait_ge(s.shifted.sem, s.shifted.at(n + 2, 4 * (c + 1)))
                        nc.scalar.activation(ph[:, c], pix[:, 1 - p, c], ACT.Copy).then_inc(s.high.sem, 1)
                    if live(1) and c == 1:
                        act.wait_ge(s.x.sem, s.x.at(n - 1))
                        inverse_root(n + 1, 1 - p, TP, s.var, s.log, s.rec)
                    if live(1) and c == 4:
                        act.wait_ge(s.cen.sem, s.cen.at(n + 1))
                        nc.scalar.activation(sq[:, 1 - p], cen_ps[:, 1 - p, 0:T], ACT.Square).then_inc(s.sq2.sem, 1)

            act.preload_act_table_set(LOG_EXP)
            in_stages(act, G, LEAD, step)

        @block.gpsimd
        def _(pool):
            s.low.seed(pool)

            def step(n, i, p, live):
                if live(3):
                    for c in range(CH):
                        pool.wait_ge(s.high.sem, s.high.at(n + 3, c + 1))
                        pool.wait_ge(s.tok.sem, s.tok.at(n + 2, c + 1))
                        pool.wait_ge(s.shifted.sem, s.shifted.at(n + 2, 4 * (c + 1)))
                        nc.gpsimd.tensor_tensor(pl[:, c], pix[:, 1 - p, c], ph[:, c], ALU.subtract)\
                            .then_inc(s.low.sem, 1)

            in_stages(pool, G, LEAD, step)

        @block.vector
        def _(dve):
            for sig in (s.shifted, s.nrm, s.h, s.x):
                sig.seed(dve)
            for dst in (sh, sl):
                for c in range(CH):
                    nc.vector.tensor_copy(dst[:, c], S.X[:, 0:TP]).then_inc(cleared, 1)
            for k in range(3 * CH):
                dve.wait_ge(wfold_pe, k + 1)
                nc.vector.tensor_copy(wh[:, k], bank_of(k)).then_inc(wfold, 1)
                dve.wait_ge(wfold, k + 1)
                nc.vector.tensor_tensor(wl[:, k], bank_of(k), wh[:, k], ALU.subtract).then_inc(wlow, 1)
            dve.wait_ge(cleared, 2 * CH)

            def shift(n, c):
                dve.wait_ge(s.high.sem, s.high.at(n, c + 1))
                dve.wait_ge(s.tok.sem, s.tok.at(n - 1, c + 1))
                for src, dst, ready in ((ph, sh, s.high), (pl, sl, s.low)):
                    dve.wait_ge(ready.sem, ready.at(n, c + 1))
                    a = src[:, c].rearrange("q (r j) -> q r j", j=GRID)
                    b = dst[:, c].rearrange("q (r j) -> q r j", j=GRID)
                    nc.vector.tensor_copy(b[0:64, :, 0:GRID - 1], a[0:64, :, 1:GRID]).then_inc(s.shifted.sem, 1)
                    nc.vector.tensor_copy(b[64:P, :, 1:GRID], a[64:P, :, 0:GRID - 1]).then_inc(s.shifted.sem, 1)

            def normalize(n, p):
                dve.wait_ge(s.rec.sem, s.rec.at(n))
                nc.vector.scalar_tensor_tensor(out=nrm[:, p, 0:TP], in0=tok_ps[:, p, 0:TP], scalar=S.tok_bias_c[:],
                                               in1=rec[:, p, 0:TP], op0=ALU.add, op1=ALU.mult)\
                    .then_inc(s.nrm.sem, 1)
                dve.wait_ge(s.nrm.sem, s.nrm.at(n))
                nc.vector.tensor_scalar(images(S.h[:, bass.ds(n * T, T)])[:, :, 1:L], images(nrm[:, p, 0:TP]),
                                        col(S, "tok_g"), col(S, "tok_b"), ALU.mult, ALU.add).then_inc(s.h.sem, 1)

            def step(n, i, p, live):
                for c in range(CH):
                    if live(3):
                        shift(n + 3, c)
                    if live(0) and c == 0:
                        dve.wait_ge(s.rec2.sem, s.rec2.at(n))
                        nc.vector.tensor_tensor(images(S.X[:, bass.ds(n * XP, XP)])[:, :, 3:PADL],
                                                images(cen_ps[:, p, 0:T]), images(rec[:, p]), ALU.mult)\
                            .then_inc(s.x.sem, 1)
                    if live(1) and c == 1:
                        normalize(n + 1, 1 - p)

            in_stages(dve, G, LEAD, step)


def mamba(nc, S, I):
    G = S.G
    with ExitStack() as ctx:
        def sb(name, shape, dt=F32):
            return ctx.enter_context(nc.sbuf_tensor(f"mb_{name}", shape, dt))

        xflip = sb("xflip", [P, XP])
        xc = sb("xc", [P, 2, 2, T])
        zs = sb("zs", [P, 2, 2, T])
        bc = sb("bc", [96, 2, T], BF16)
        rest = sb("rest", [P, 2, T])
        res1, dtr = rest[0:96, 0], rest[96:96 + R, 0]
        part2 = sb("part2", [96, T], BF16)
        mag = sb("mag", [P, 2, T])
        v = sb("v", [P, 2, T])
        dt = sb("dt", [P, 2, 2, T])
        dtx = sb("dtx", [P, 2, 2, T])
        bs = sb("bs", [P, RING, T])
        db = sb("db", [P, 2, 2, T])
        da = sb("da", [P, RING, 2, T])
        hst = sb("hst", [P, 2, 2, T])
        hc = sb("hc", [P, 2, 2, T])
        yd = sb("yd", [P, 2, T])
        cg = sb("cg", [P, 2, T])
        sq = sb("sq", [P, T])
        h2 = sb("h2", [P, T])
        gl3 = sb("gl3", [P, T])
        ps = ctx.enter_context(nc.psum_tensor("mb_ps", [P, 8, 512], F32))
        b_ps, c_ps, y_ps, proj_ps, post_ps = ps[:, 0:2], ps[:, 2:4], ps[:, 4:6], ps[:, 6], ps[:, 7]

        cleared = ctx.enter_context(nc.semaphore("mb_cleared"))
        s = signals(
            ctx, nc, "mb", flip=1, conv=4, th=4, xb=4, xc=2, z=4, zt=4, zr=4, zs=2, xp=2, bc1=2, res1=2, part2=2,
            second=2, third=2, dtr=2, dtp=4, dx=4, relu=2, mag=2, u=2, logw=2, poly=10, dt=2, dtx=2,
            bb=2 * NS, bs=2 * NS, db=2 * NS, da=4 * NS, st=2 * NS, cb=2 * NS, hc=2 * NS, ys=2 * NS,
            yd=4, yz=2, h2=1, up=4, gl=4, hn=1, sums=1)
        LN_F, LN_B, LN_FF, LN_X = range(4)
        cen, cgd, sqd, var, log, rec, nrm = (
            [Signal(ctx, nc, f"mb_{x}{w}") for w in ("f", "b", "ff", "x")]
            for x in ("cen", "cg", "sq", "var", "log", "rec", "nrm"))
        block = ctx.enter_context(nc.Block())

        def images(ap):
            return ap.rearrange("q (b t) -> q b t", b=PAIR)

        gl = [rest[:, 0], rest[:, 1], images(xflip[:])[:, :, 3:PADL], gl3[:]]

        def x_of(n):
            return images(S.X[:, bass.ds(n * XP, XP)])

        def h_of(n):
            return S.h[:, bass.ds(n * T, T)]

        def before(which, n, last):
            if which == LN_X:
                return (LN_FF, n) if last else (LN_F, n + 1)
            return {LN_F: (LN_FF, n - 1), LN_B: (LN_X, n - 1), LN_FF: (LN_B, n)}[which]

        def following(n, d):
            return (n, 1) if d == 0 else (n + 1, 0)

        def preceding(n, d):
            return (n - 1, 1) if d == 0 else (n, 0)

        def later(n, d, k, steps, ahead):
            if k + steps < NS:
                return [(n, d, k + steps)]
            return [(*following(n, d), k + steps - NS)] if ahead else []

        @block.tensor
        def _(pe):
            for sig in (s.conv, s.z, s.xp, s.dtp, s.bb, s.cb, s.ys, s.up, *cen, *var):
                sig.seed(pe)

            def conv(n, d, half, taps):
                xin = x_of(n) if d == 0 else images(xflip[:])
                bank = post_ps if half else proj_ps
                if 0 in taps:
                    if half:
                        w = LN_X if d else LN_FF
                        pe.wait_ge(log[w].sem, log[w].at(n - 2))
                    elif d:
                        pe.wait_ge(s.dx.sem, s.dx.at(n, 2))
                        pe.wait_ge(s.flip.sem, s.flip.at(n))
                    else:
                        pe.wait_ge(s.gl.sem, s.gl.at(n - 2))
                for k in taps:
                    mm = nc.tensor.matmul(bank[:, 0:T], S.convw[:, d, k, half * D:(half + 1) * D],
                                          xin[:, :, k:k + L], start=(k == 0), stop=(k == TAPS - 1))
                if TAPS - 1 in taps:
                    mm.then_inc(s.conv.sem, 1)

            def gate(n, d, half, ahead):
                if half:
                    pe.wait_ge(s.zr.sem, s.zr.at(n, 2 * d + 1))
                elif ahead:
                    a, e = following(n, d)
                    pe.wait_ge(s.xb.sem, s.xb.at(a, 2 * e + 1))
                else:
                    pe.wait_ge(s.gl.sem, s.gl.at(n - 1))
                nc.tensor.matmul(proj_ps[:, 0:T], S.zw[:, d, half * D:(half + 1) * D], x_of(n)[:, :, 3:PADL],
                                 start=True, stop=True).then_inc(s.z.sem, 1)

            def project(n, d, k, gated=None):
                if k < 4:
                    conv(n, d, k // 2, [2 * (k % 2), 2 * (k % 2) + 1])
                elif k == 6:
                    if gated:
                        pe.wait_ge(s.zr.sem, s.zr.at(gated[0], 2 * gated[1] + 2))
                    pe.wait_ge(s.xc.sem, s.xc.at(n, d + 1))
                    for half in range(2):
                        mm = nc.tensor.matmul(proj_ps[0:96 + R, 0:T], S.xpw[:, d, half, :], xc[:, d, half],
                                              start=(half == 0), stop=(half == 1))
                    mm.then_inc(s.xp.sem, 1)
                elif k in (8, 9):
                    half = k - 8
                    if half == 0:
                        pe.wait_ge(s.dtr.sem, s.dtr.at(n, d + 1))
                        pe.wait_ge(s.res1.sem, s.res1.at(n, d + 1))
                    else:
                        pe.wait_ge(s.dx.sem, s.dx.at(n, 2 * d + 1))
                    nc.tensor.matmul(proj_ps[:, 0:T], S.dtw[96:96 + R, d, half * D:(half + 1) * D], dtr,
                                     start=True, stop=True).then_inc(s.dtp.sem, 1)

            def spread_b(n, d, k):
                if k == 0:
                    pe.wait_ge(s.second.sem, s.second.at(n, d + 1))
                    pe.wait_ge(s.third.sem, s.third.at(n, d + 1))
                pe.wait_ge(s.bs.sem, s.bs.at(n, NS * d + k - 1))
                nc.tensor.matmul(b_ps[:, k % 2, 0:T], S.sel[:, k:k + 1].to_broadcast([96, D]), bc[:, d], start=True, stop=True)\
                    .then_inc(s.bb.sem, 1)

            def spread_c(n, d, k):
                pe.wait_ge(s.hc.sem, s.hc.at(n, NS * d + k - 1))
                nc.tensor.matmul(c_ps[:, k % 2, 0:T], S.sel[:, NS + k:NS + k + 1].to_broadcast([96, D]), bc[:, d], start=True, stop=True)\
                    .then_inc(s.cb.sem, 1)

            def add(n, d, k):
                if k == 0:
                    pe.wait_ge(s.yd.sem, s.yd.at(n, 2 * d))
                pe.wait_ge(s.hc.sem, s.hc.at(n, NS * d + k + 1))
                for half in range(2):
                    mm = nc.tensor.matmul(y_ps[:, half, 0:T], S.ident[:], hc[:, k % 2, half], start=(k == 0),
                                          stop=(k == NS - 1))
                mm.then_inc(s.ys.sem, 1)

            def variance(which, n):
                pe.wait_ge(sqd[which].sem, sqd[which].at(n))
                nc.tensor.matmul(post_ps[:, 0:T], S.mean[:], sq[:], start=True, stop=True).then_inc(var[which].sem, 1)

            def free_bank(which, n, last=False):
                w, m = before(which, n, last)
                pe.wait_ge(log[w].sem, log[w].at(m))

            def out_project(n, d, ahead):
                if ahead:
                    pe.wait_ge(s.xb.sem, s.xb.at(n + 1, 2 * d + 2))
                else:
                    free_bank(LN_F + d, n)
                pe.wait_ge(s.yz.sem, s.yz.at(n, d + 1))
                for half in range(2):
                    nc.tensor.matmul(post_ps[:, 0:T], S.woc[:, (2 * d + half) * D:(2 * d + half + 1) * D], zs[:, d, half],
                                     start=(half == 0), stop=False)
                nc.tensor.matmul(post_ps[:, 0:T], S.ident[:], x_of(n)[:, :, 3:PADL], start=False, stop=True)\
                    .then_inc(cen[LN_F + d].sem, 1)

            def up(n, k, last):
                if k == 0:
                    free_bank(LN_FF, n)
                    pe.wait_ge(s.h2.sem, s.h2.at(n))
                elif k > 1:
                    pe.wait_ge(s.gl.sem, s.gl.at(n, k - 1))
                elif last:
                    pe.wait_ge(s.zr.sem, s.zr.at(n, 4))
                else:
                    pe.wait_ge(s.dx.sem, s.dx.at(n + 1, 4))
                bank = proj_ps if k % 2 else post_ps
                nc.tensor.matmul(bank[:, 0:T], S.w1[:, k * D:(k + 1) * D], h2[:], start=True, stop=True)\
                    .then_inc(s.up.sem, 1)

            def down(n, chunks):
                if 0 in chunks:
                    pe.wait_ge(s.gl.sem, s.gl.at(n, FF - 1))
                    nc.tensor.matmul(post_ps[:, 0:T], S.center[:], h2[:], start=True, stop=False)
                for k in chunks:
                    pe.wait_ge(s.gl.sem, s.gl.at(n, k + 1))
                    mm = nc.tensor.matmul(post_ps[:, 0:T], S.w2c[:, k * D:(k + 1) * D], gl[k], start=False,
                                          stop=(k == FF - 1))
                if FF - 1 in chunks:
                    mm.then_inc(cen[LN_FF].sem, 1)

            def center(n, last=False):
                free_bank(LN_X, n, last)
                pe.wait_ge(s.hn.sem, s.hn.at(n))
                nc.tensor.matmul(post_ps[:, 0:T], S.center[:], h_of(n), start=True, stop=True).then_inc(cen[LN_X].sem, 1)

            def forward_norm(n, k, ahead):
                if k == 6:
                    out_project(n, 0, ahead)
                elif k == 8:
                    variance(LN_F, n)

            def feed_forward(n, k, last=False):
                if k == 6:
                    out_project(n, 1, ahead=not last)
                elif k == 8:
                    variance(LN_B, n)
                elif k == 12:
                    for j in range(FF):
                        up(n, j, last)
                elif k == 13:
                    down(n, [0, 1])
                elif k == 14:
                    down(n, [2, 3])
                elif k == 15 and last:
                    variance(LN_FF, n)

            def expert_norm(n, k, last=False):
                if k == 0 and not last:
                    variance(LN_FF, n)
                elif k == 9:
                    center(n, last)
                elif k == 11:
                    variance(LN_X, n)

            def unit(n, d, first=False, ahead=True, late=True):
                for k in range(NS):
                    if k == 0 and not first:
                        add(*preceding(n, d), NS - 1)
                    if ahead:
                        project(*following(n, d), k, gated=(n, d))
                    for state in later(n, d, k, 3, ahead):
                        spread_b(*state)
                    for state in later(n, d, k, 1, ahead):
                        spread_c(*state)
                    if k in (3, 5):
                        gate(n, d, (k - 3) // 2, ahead)
                    if d == 0 and not first:
                        feed_forward(n - 1, k)
                    elif d == 1:
                        if late:
                            expert_norm(n - 1, k)
                        forward_norm(n, k, ahead)
                    if k > 0:
                        add(n, d, k - 1)

            for k in range(NS):
                project(0, 0, k)
            spread_b(0, 0, 0)
            spread_b(0, 0, 1)
            spread_b(0, 0, 2)
            spread_c(0, 0, 0)
            unit(0, 0, first=True)
            unit(0, 1, late=False)
            with pe.Fori(1, G - 1) as n:
                unit(n, 0)
                unit(n, 1)
            unit(G - 1, 0)
            unit(G - 1, 1, ahead=False)
            add(G - 1, 1, NS - 1)
            for k in range(NS):
                feed_forward(G - 1, k, last=True)
            for k in range(NS):
                expert_norm(G - 1, k, last=True)

        @block.scalar
        def _(act):
            for sig in (s.th, s.xb, s.zt, s.zr, s.part2, s.second, s.dtr, s.dx, s.mag, s.u, s.logw, s.bs, s.da, s.gl, s.flip,
                        *cgd, *sqd, *log, *rec):
                sig.seed(act)

            def flip(n):
                act.wait_ge(s.conv.sem, s.conv.at(n - 1))
                act.wait_ge(cen[LN_FF].sem, cen[LN_FF].at(n - 2))
                nc.scalar.activation(images(xflip[:])[:, :, PADL - 1:2:-1], x_of(n)[:, :, 3:PADL], ACT.Copy)\
                    .then_inc(s.flip.sem, 1)

            def silu_parts(n, d, half, kind):
                i = 2 * d + half + 1
                bank = post_ps if half and kind == "conv" else proj_ps
                if kind == "conv":
                    act.wait_ge(s.conv.sem, s.conv.at(n, i))
                    act.wait_ge(s.poly.sem, s.poly.at(n, 5 * d))
                    nc.scalar.activation(v[:, half], bank[:, 0:T], ACT.Tanh, bias=S.conv_b_half[:, d, half:half + 1],
                                         scale=0.5).then_inc(s.th.sem, 1)
                    act.wait_ge(s.yd.sem, s.yd.at(n - 1, 2 * d + 2))
                    act.wait_ge(s.dtx.sem, s.dtx.at(n - 1, d + 1))
                    nc.scalar.activation(xc[:, d, half], bank[:, 0:T], ACT.Identity, bias=col(S, f"conv_b{d}", half))\
                        .then_inc(s.xb.sem, 1)
                else:
                    act.wait_ge(s.z.sem, s.z.at(n, i))
                    act.wait_ge(s.dt.sem, s.dt.at(n, d + 1))
                    nc.scalar.activation(mag[:, half], bank[:, 0:T], ACT.Tanh, scale=0.5).then_inc(s.zt.sem, 1)
                    act.wait_ge(cen[LN_F + d].sem, cen[LN_F + d].at(n - 1))
                    nc.scalar.activation(zs[:, d, half], bank[:, 0:T], ACT.Copy).then_inc(s.zr.sem, 1)

            def project(n, d, k, gated=None):
                if k in (2, 4):
                    silu_parts(n, d, k // 2 - 1, "conv")
                elif k == 7:
                    act.wait_ge(s.xp.sem, s.xp.at(n, d + 1))
                    act.wait_ge(s.dtp.sem, s.dtp.at(n, 2 * d))
                    act.wait_ge(cen[LN_FF].sem, cen[LN_FF].at(n - 2))
                    nc.scalar.activation(dtr, proj_ps[96:96 + R, 0:T], ACT.Copy).then_inc(s.dtr.sem, 1)
                elif k == 8:
                    act.wait_ge(s.res1.sem, s.res1.at(n, d + 1))
                    act.wait_ge(s.third.sem, s.third.at(n, d))
                    nc.scalar.activation(part2[64:96], res1[64:96], ACT.Copy).then_inc(s.part2.sem, 1)
                    nc.scalar.activation(bc[32:64, d], res1[32:64], ACT.Copy).then_inc(s.second.sem, 1)
                    dt_in(n, d, 0)
                elif k == 10:
                    dt_in(n, d, 1)
                    act.wait_ge(s.dx.sem, s.dx.at(n, 2 * d + 2))
                    if gated:
                        act.wait_ge(s.zs.sem, s.zs.at(gated[0], gated[1] + 1))
                    nc.scalar.activation(mag[:], dt[:, d], ACT.Abs).then_inc(s.mag.sem, 1)
                    act.wait_ge(s.mag.sem, s.mag.at(n, d + 1))
                    act.wait_ge(s.db.sem, s.db.at(n - 1, NS * (d + 1)))
                    nc.scalar.activation(dtx[:, d], mag[:], ACT.Exp, scale=-1.0).then_inc(s.u.sem, 1)
                    act.wait_ge(s.u.sem, s.u.at(n, d + 1))
                    nc.scalar.activation(mag[:], dtx[:, d], ACT.Ln, bias=S.past_edge[:], scale=1.0 / (1.0 + EDGE))\
                        .then_inc(s.logw.sem, 1)

            def dt_in(n, d, half):
                act.wait_ge(s.dtp.sem, s.dtp.at(n, 2 * d + half + 1))
                act.wait_ge(s.da.sem, s.da.at(n - 1, 2 * NS * (d + 1)))
                nc.scalar.activation(dt[:, d, half], proj_ps[:, 0:T], ACT.Identity, bias=col(S, f"dt_b{d}", half))\
                    .then_inc(s.dx.sem, 1)

            def copy_b(n, d, k):
                j = NS * d + k + 1
                act.wait_ge(s.bb.sem, s.bb.at(n, j))
                act.wait_ge(s.db.sem, s.db.at(n, j - RING))
                nc.scalar.activation(bs[:, k % RING], b_ps[:, k % 2, 0:T], ACT.Copy).then_inc(s.bs.sem, 1)

            def decay(n, d, k):
                if k == 0:
                    act.wait_ge(s.dt.sem, s.dt.at(n, d + 1))
                act.wait_ge(s.st.sem, s.st.at(n, NS * d + k + 1 - RING))
                for half in range(2):
                    nc.scalar.activation(images(da[:, k % RING, half])[:, :, 1:L], images(dt[:, d, half])[:, :, 1:L],
                                         ACT.Exp, scale=S.neg_a[:, d, half, k:k + 1]).then_inc(s.da.sem, 1)

            def squares(which, n, last=False):
                act.wait_ge(cen[which].sem, cen[which].at(n))
                w, m = before(which, n, last)
                act.wait_ge(nrm[w].sem, nrm[w].at(m))
                if which == LN_F:
                    act.wait_ge(s.hn.sem, s.hn.at(n - 1))
                elif which == LN_B:
                    act.wait_ge(nrm[LN_X].sem, nrm[LN_X].at(n - 1))
                else:
                    act.wait_ge(s.h2.sem, s.h2.at(n))
                g = cg[:, which % 2]
                if which in (LN_F, LN_B):
                    nc.scalar.activation(g, post_ps[:, 0:T], ACT.Copy,
                                         scale=S.g_half[:, which:which + 1]).then_inc(cgd[which].sem, 1)
                elif which == LN_FF:
                    nc.scalar.activation(g, post_ps[:, 0:T], ACT.Identity, bias=S.ffn_b2_cg[:],
                                         scale=col(S, "ff_g")).then_inc(cgd[which].sem, 1)
                else:
                    nc.scalar.activation(g, post_ps[:, 0:T], ACT.Copy).then_inc(cgd[which].sem, 1)
                if which == LN_FF:
                    nc.scalar.activation(sq[:], post_ps[:, 0:T], ACT.Square, bias=S.ffn_b2_c[:])\
                        .then_inc(sqd[which].sem, 1)
                else:
                    nc.scalar.activation(sq[:], post_ps[:, 0:T], ACT.Square).then_inc(sqd[which].sem, 1)

            def inverse_root(which, n):
                act.wait_ge(var[which].sem, var[which].at(n))
                nc.scalar.activation(sq[:], post_ps[:, 0:T], ACT.Ln, bias=S.eps[:]).then_inc(log[which].sem, 1)
                act.wait_ge(log[which].sem, log[which].at(n))
                nc.scalar.activation(sq[:], sq[:], ACT.Exp, scale=-0.5).then_inc(rec[which].sem, 1)

            def forward_norm(n, k):
                if k == 7:
                    squares(LN_F, n)
                elif k == 9:
                    inverse_root(LN_F, n)

            def feed_forward(n, k, last=False):
                if k == 7:
                    squares(LN_B, n)
                elif k == 9:
                    inverse_root(LN_B, n)
                elif k == 12:
                    act.wait_ge(cen[LN_FF].sem, cen[LN_FF].at(n - 1))
                    if not last:
                        act.wait_ge(s.second.sem, s.second.at(n + 1, 2))
                        act.wait_ge(s.third.sem, s.third.at(n + 1, 2))
                        act.wait_ge(s.dtp.sem, s.dtp.at(n + 1, 4))
                        act.wait_ge(s.conv.sem, s.conv.at(n + 1, 4))
                    for j in range(FF):
                        bank = proj_ps if j % 2 else post_ps
                        act.wait_ge(s.up.sem, s.up.at(n, j + 1))
                        src = images(bank[:, 0:T]) if j == 2 else bank[:, 0:T]
                        nc.scalar.activation(gl[j], src, ACT.Gelu_apprx_tanh, bias=col(S, "ffn_b1", j))\
                            .then_inc(s.gl.sem, 1)
                    act.preload_act_table_set(LOG_EXP)
                elif k == 15:
                    squares(LN_FF, n)
                    if last:
                        inverse_root(LN_FF, n)

            def expert_norm(n, k, last=False):
                if k == 1 and not last:
                    inverse_root(LN_FF, n)
                elif k == 10:
                    squares(LN_X, n, last)
                elif k == 12:
                    inverse_root(LN_X, n)

            def unit(n, d, first=False, ahead=True, late=True):
                for k in range(NS):
                    for state in later(n, d, k, 2, ahead):
                        copy_b(*state)
                        if k < NS - 2:
                            decay(*state)
                    if ahead:
                        project(*following(n, d), k, gated=(n, d))
                    if k in (4, 5):
                        silu_parts(n, d, k - 4, "gate")
                    if k == 5:
                        act.preload_act_table_set(LOG_EXP)
                    if d == 0 and not first:
                        feed_forward(n - 1, k)
                    elif d == 1:
                        forward_norm(n, k)
                        if late:
                            expert_norm(n - 1, k)
                    if d == 1 and ahead and k == 13:
                        flip(n + 1)
                    if k >= NS - 2 and ahead:
                        decay(*following(n, d), k + 2 - NS)

            act.wait_ge(cleared, 2)
            flip(0)
            for k in range(NS):
                if k == 6:
                    act.preload_act_table_set(LOG_EXP)
                project(0, 0, k)
            for k in range(2):
                copy_b(0, 0, k)
                decay(0, 0, k)
            unit(0, 0, first=True)
            unit(0, 1, late=False)
            with act.Fori(1, G - 1) as n:
                unit(n, 0)
                unit(n, 1)
            unit(G - 1, 0)
            unit(G - 1, 1, ahead=False)
            for k in range(NS):
                feed_forward(G - 1, k, last=True)
            for k in range(NS):
                expert_norm(G - 1, k, last=True)

        @block.gpsimd
        def _(pool):
            for sig in (s.third, s.dtx, s.db, s.yz, *nrm):
                sig.seed(pool)

            def project(n, d, k):
                if k == 8:
                    pool.wait_ge(s.part2.sem, s.part2.at(n, d + 1))
                    a, e = preceding(n, d)
                    pool.wait_ge(s.db.sem, s.db.at(a, NS * e + 10))
                    nc.gpsimd.tensor_tensor(bc[64:96, d], res1[64:96], part2[64:96], ALU.subtract)\
                        .then_inc(s.third.sem, 1)
                    pool.wait_ge(s.third.sem, s.third.at(n, d + 1))
                elif k == 14:
                    pool.wait_ge(s.dt.sem, s.dt.at(n, d + 1))
                    nc.gpsimd.tensor_tensor(dtx[:, d], dt[:, d], xc[:, d], ALU.mult).then_inc(s.dtx.sem, 1)

            def drive(n, d, k):
                j = NS * d + k + 1
                if k == 0:
                    pool.wait_ge(s.dtx.sem, s.dtx.at(n, d + 1))
                pool.wait_ge(s.bs.sem, s.bs.at(n, j))
                pool.wait_ge(s.st.sem, s.st.at(n, j - 2))
                nc.gpsimd.tensor_tensor(db[:, k % 2], dtx[:, d], bs[:, k % RING].unsqueeze(1).to_broadcast([P, 2, T]),
                                        ALU.mult).then_inc(s.db.sem, 1)

            def gate(n, d):
                pool.wait_ge(s.yd.sem, s.yd.at(n, 2 * d + 2))
                pool.wait_ge(s.zs.sem, s.zs.at(n, d + 1))
                nc.gpsimd.tensor_tensor(zs[:, d], yd[:], zs[:, d], ALU.mult).then_inc(s.yz.sem, 1)

            def norm(which, n):
                g = cg[:, which % 2]
                pool.wait_ge(rec[which].sem, rec[which].at(n))
                if which == LN_X:
                    nc.gpsimd.tensor_tensor(x_of(n)[:, :, 3:PADL], images(g), images(sq[:]), ALU.mult)\
                        .then_inc(nrm[which].sem, 1)
                else:
                    nc.gpsimd.tensor_tensor(g, g, sq[:], ALU.mult).then_inc(nrm[which].sem, 1)

            def unit(n, d, first=False, ahead=True, late=True):
                for k in range(NS):
                    for state in later(n, d, k, 1, ahead):
                        drive(*state)
                    if ahead:
                        project(*following(n, d), k)
                    if k == 2 and d == 1 and late:
                        norm(LN_FF, n - 1)
                    if k == 2 and not first:
                        gate(*preceding(n, d))
                    if k == 10 and not first:
                        norm(LN_F, n) if d else norm(LN_B, n - 1)
                    if k == 13 and d == 1 and late:
                        norm(LN_X, n - 1)

            for k in range(NS):
                project(0, 0, k)
            drive(0, 0, 0)
            unit(0, 0, first=True)
            unit(0, 1, late=False)
            with pool.Fori(1, G - 1) as n:
                unit(n, 0)
                unit(n, 1)
            unit(G - 1, 0)
            unit(G - 1, 1, ahead=False)
            gate(G - 1, 1)
            for which in (LN_B, LN_FF, LN_X):
                norm(which, G - 1)

        @block.vector
        def _(dve):
            for sig in (s.bc1, s.res1, s.relu, s.poly, s.dt, s.xc, s.zs, s.st, s.hc, s.yd, s.h2, s.hn, s.sums):
                sig.seed(dve)

            def project(n, d, k):
                step = lambda i: s.poly.at(n, 5 * d + i)
                if k == 5:
                    dve.wait_ge(s.xb.sem, s.xb.at(n, 2 * d + 2))
                    dve.wait_ge(s.th.sem, s.th.at(n, 2 * d + 2))
                    nc.vector.scalar_tensor_tensor(out=xc[:, d], in0=v[:], scalar=1.0, in1=xc[:, d], op0=ALU.add,
                                                   op1=ALU.mult).then_inc(s.xc.sem, 1)
                elif k == 7:
                    dve.wait_ge(s.xp.sem, s.xp.at(n, d + 1))
                    dve.wait_ge(s.cb.sem, s.cb.at(n - 1, NS * (d + 1)))
                    dve.wait_ge(s.bb.sem, s.bb.at(n - 1, NS * (d + 1)))
                    nc.vector.tensor_copy(bc[:, d], proj_ps[0:96, 0:T]).then_inc(s.bc1.sem, 1)
                    dve.wait_ge(s.bc1.sem, s.bc1.at(n, d + 1))
                    dve.wait_ge(s.second.sem, s.second.at(n, d))
                    dve.wait_ge(s.third.sem, s.third.at(n, d))
                    dve.wait_ge(cen[LN_FF].sem, cen[LN_FF].at(n - 2))
                    nc.vector.tensor_tensor(res1, proj_ps[0:96, 0:T], bc[:, d], ALU.subtract).then_inc(s.res1.sem, 1)
                elif k == 11:
                    dve.wait_ge(s.u.sem, s.u.at(n, d + 1))
                    nc.vector.tensor_scalar(v[:], dtx[:, d], EDGE, None, ALU.min).then_inc(s.poly.sem, 1)
                    dve.wait_ge(s.poly.sem, step(1))
                    dve.wait_ge(s.logw.sem, s.logw.at(n, d + 1))
                    nc.vector.scalar_tensor_tensor(out=dtx[:, d], in0=v[:], scalar=-4.0 / 3.0, in1=v[:],
                                                   op0=ALU.add, op1=ALU.mult).then_inc(s.poly.sem, 1)
                    dve.wait_ge(s.mag.sem, s.mag.at(n, d + 1))
                    nc.vector.tensor_scalar(dt[:, d], dt[:, d], 0.0, None, ALU.max).then_inc(s.relu.sem, 1)
                elif k == 12:
                    dve.wait_ge(s.poly.sem, step(2))
                    nc.vector.scalar_tensor_tensor(out=dtx[:, d], in0=dtx[:, d], scalar=2.0, in1=v[:],
                                                   op0=ALU.add, op1=ALU.mult).then_inc(s.poly.sem, 1)
                    dve.wait_ge(s.poly.sem, step(3))
                    nc.vector.scalar_tensor_tensor(out=dtx[:, d], in0=dtx[:, d], scalar=-4.0, in1=v[:],
                                                   op0=ALU.add, op1=ALU.mult).then_inc(s.poly.sem, 1)
                elif k == 13:
                    dve.wait_ge(s.relu.sem, s.relu.at(n, d + 1))
                    nc.vector.scalar_tensor_tensor(out=mag[:], in0=mag[:], scalar=0.0, in1=dt[:, d],
                                                   op0=ALU.max, op1=ALU.add).then_inc(s.poly.sem, 1)
                    dve.wait_ge(s.poly.sem, step(5))
                    nc.vector.scalar_tensor_tensor(out=dt[:, d], in0=dtx[:, d], scalar=-0.25, in1=mag[:],
                                                   op0=ALU.mult, op1=ALU.add).then_inc(s.dt.sem, 1)

            def scan(n, d, k):
                j = NS * d + k + 1
                dve.wait_ge(s.db.sem, s.db.at(n, j))
                dve.wait_ge(s.hc.sem, s.hc.at(n, j - 2))
                dve.wait_ge(s.da.sem, s.da.at(n, 2 * j))
                nc.vector.tensor_tensor_scan(hst[:, k % 2].rearrange("q h t -> q (h t)"),
                                             da[:, k % RING].rearrange("q h t -> q (h t)"),
                                             db[:, k % 2].rearrange("q h t -> q (h t)"), 0.0, ALU.mult, ALU.add)\
                    .then_inc(s.st.sem, 1)

            def read_out(n, d, k):
                j = NS * d + k + 1
                dve.wait_ge(s.st.sem, s.st.at(n, j))
                dve.wait_ge(s.cb.sem, s.cb.at(n, j))
                dve.wait_ge(s.ys.sem, s.ys.at(n, j - 2))
                nc.vector.tensor_tensor(hc[:, k % 2], hst[:, k % 2], c_ps[:, k % 2, 0:T].unsqueeze(1).to_broadcast([P, 2, T]),
                                        ALU.mult).then_inc(s.hc.sem, 1)

            def skip(n, d):
                dve.wait_ge(s.ys.sem, s.ys.at(n, NS * (d + 1)))
                dve.wait_ge(s.yz.sem, s.yz.at(n, d))
                for half in range(2):
                    out = images(yd[:, half])
                    nc.vector.scalar_tensor_tensor(out=out[:, :, ::-1] if d else out, in0=images(xc[:, d, half]),
                                                   scalar=S.skip_half[:, d, half:half + 1],
                                                   in1=images(y_ps[:, half, 0:T]),
                                                   op0=ALU.mult, op1=ALU.add).then_inc(s.yd.sem, 1)

            def half_sum(n):
                dve.wait_ge(nrm[LN_F].sem, nrm[LN_F].at(n))
                dve.wait_ge(nrm[LN_B].sem, nrm[LN_B].at(n))
                dve.wait_ge(cen[LN_FF].sem, cen[LN_FF].at(n - 1))
                nc.vector.scalar_tensor_tensor(out=h2[:], in0=cg[:, 0], scalar=S.b_half[:], in1=cg[:, 1],
                                               op0=ALU.add, op1=ALU.add).then_inc(s.h2.sem, 1)

            def residual(n):
                dve.wait_ge(nrm[LN_FF].sem, nrm[LN_FF].at(n))
                nc.vector.scalar_tensor_tensor(out=h_of(n), in0=cg[:, LN_FF % 2], scalar=col(S, "ff_b"), in1=h_of(n),
                                               op0=ALU.add, op1=ALU.add).then_inc(s.hn.sem, 1)

            def token_sums(n):
                dve.wait_ge(nrm[LN_X].sem, nrm[LN_X].at(n))
                nc.vector.tensor_reduce(S.sums[:, bass.ds(n * PAIR, PAIR)], x_of(n)[:, :, 3:PADL], AXX, ALU.add)\
                    .then_inc(s.sums.sem, 1)

            def unit(n, d, first=False, ahead=True, late=True):
                for k in range(NS):
                    scan(n, d, k)
                    if k == 1 and not first:
                        skip(*preceding(n, d))
                    if k == 7 and ahead:
                        project(*following(n, d), k)
                    if k > 0:
                        read_out(n, d, k - 1)
                    elif not first:
                        read_out(*preceding(n, d), NS - 1)
                    if k != 7 and ahead:
                        project(*following(n, d), k)
                    if k == 6:
                        dve.wait_ge(s.zr.sem, s.zr.at(n, 2 * d + 2))
                        dve.wait_ge(s.zt.sem, s.zt.at(n, 2 * d + 2))
                        nc.vector.scalar_tensor_tensor(out=zs[:, d], in0=mag[:], scalar=1.0, in1=zs[:, d], op0=ALU.add,
                                                       op1=ALU.mult).then_inc(s.zs.sem, 1)
                    if k == 11 and d == 0 and not first:
                        half_sum(n - 1)
                    if k == 4 and d == 1 and late:
                        residual(n - 1)
                    if k == 14 and d == 1 and late:
                        token_sums(n - 1)

            nc.vector.memset(da[:], 0.0).then_inc(cleared, 1)
            nc.vector.memset(xflip[:], 0.0).then_inc(cleared, 1)
            for k in range(NS):
                project(0, 0, k)
            unit(0, 0, first=True)
            unit(0, 1, late=False)
            with dve.Fori(1, G - 1) as n:
                unit(n, 0)
                unit(n, 1)
            unit(G - 1, 0)
            unit(G - 1, 1, ahead=False)
            read_out(G - 1, 1, NS - 1)
            skip(G - 1, 1)
            half_sum(G - 1)
            residual(G - 1)
            token_sums(G - 1)


def route(nc, S, I):
    B = S.B
    with ExitStack() as ctx:
        def sb(name, shape):
            return ctx.enter_context(nc.sbuf_tensor(f"rt_{name}", shape, F32))
        rw, keys, pw = sb("rw", [P, NPART]), sb("keys", [B, NPART]), sb("pw", [NPART, EXP * D])
        lg, pr, eq, rest, one, two, sel = (sb(x, [B, NPART]) for x in ("lg", "pr", "eq", "rest", "one", "two", "sel"))
        selt = sb("selt", [NPART, B])
        sc = sb("sc", [B, 8])
        ps = ctx.enter_context(nc.psum_tensor("rt_ps", [P, 3, 512], F32))
        loaded = ctx.enter_context(nc.semaphore("rt_loaded"))
        logits = ctx.enter_context(nc.semaphore("rt_logits"))
        shifted = ctx.enter_context(nc.semaphore("rt_shifted"))
        expd = ctx.enter_context(nc.semaphore("rt_exp"))
        chosen = ctx.enter_context(nc.semaphore("rt_chosen"))
        turned = ctx.enter_context(nc.semaphore("rt_turned"))
        copied = ctx.enter_context(nc.semaphore("rt_copied"))
        spread = ctx.enter_context(nc.semaphore("rt_spread"))
        step = ctx.enter_context(nc.semaphore("rt_dve_step"))
        block = ctx.enter_context(nc.Block())

        @block.sync
        def _(sp):
            sp.dma_start(rw[:], I.router_w).then_inc(loaded, 16)
            sp.dma_start(keys[:], I.keys[0:B, :]).then_inc(loaded, 16)
            sp.dma_start(pw[:], I.part_w).then_inc(loaded, 16)
            sp.dma_start(S.mw1[:], I.moe_w1).then_inc(loaded, 16)
            sp.dma_start(S.mw2[:], I.moe_w2).then_inc(loaded, 16)

        @block.tensor
        def _(pe):
            pe.wait_ge(loaded, 16 * 5)
            nc.tensor.matmul(ps[0:B, 0, 0:NPART], S.sums[:], rw[:], start=True, stop=True).then_inc(logits, 1)
            pe.wait_ge(chosen, 1)
            nc.tensor.transpose(ps[0:NPART, 1, 0:B], sel[:], S.ident[0:B, 0:B]).then_inc(turned, 1)
            pe.wait_ge(copied, 1)
            for e in range(EXP):
                mm = nc.tensor.matmul(ps[:, 2, e * B:(e + 1) * B], pw[:, e * D:(e + 1) * D], selt[:], start=True, stop=True)
            mm.then_inc(spread, 1)

        @block.scalar
        def _(act):
            act.wait_ge(shifted, 1)
            nc.scalar.activation(pr[:], lg[:], ACT.Exp).then_inc(expd, 1)

        @block.vector
        def _(dve):
            done = [0]

            def then(ins):
                done[0] += 1
                ins.then_inc(step, 1)
                dve.wait_ge(step, done[0])

            v = nc.vector
            dve.wait_ge(logits, 1)
            then(v.tensor_scalar(eq[:], ps[0:B, 0, 0:NPART], 1.0 / L, None, ALU.mult))
            then(v.tensor_reduce(sc[:, 0:1], eq[:], AXX, ALU.max))
            v.tensor_scalar(lg[:], eq[:], sc[:, 0:1], None, ALU.subtract).then_inc(shifted, 1)
            dve.wait_ge(expd, 1)
            then(v.tensor_reduce(sc[:, 1:2], pr[:], AXX, ALU.add))
            then(v.reciprocal(sc[:, 2:3], sc[:, 1:2]))
            then(v.tensor_scalar(rest[:], pr[:], sc[:, 2:3], None, ALU.mult))
            for hot, c in ((one, 3), (two, 4)):
                then(v.tensor_reduce(sc[:, c:c + 1], rest[:], AXX, ALU.max))
                then(v.scalar_tensor_tensor(out=eq[:], in0=rest[:], scalar=sc[:, c:c + 1], in1=keys[:],
                                            op0=ALU.is_equal, op1=ALU.mult))
                then(v.tensor_reduce(sc[:, 5:6], eq[:], AXX, ALU.max))
                then(v.tensor_scalar(hot[:], eq[:], sc[:, 5:6], None, ALU.is_equal))
                if hot is one:
                    then(v.scalar_tensor_tensor(out=rest[:], in0=one[:], scalar=-2.0, in1=rest[:],
                                                op0=ALU.mult, op1=ALU.add))
            then(v.tensor_tensor(sc[:, 6:7], sc[:, 3:4], sc[:, 4:5], ALU.add))
            then(v.reciprocal(sc[:, 7:8], sc[:, 6:7]))
            then(v.tensor_scalar(sc[:, 3:5], sc[:, 3:5], sc[:, 7:8], None, ALU.mult))
            then(v.tensor_scalar(eq[:], one[:], sc[:, 3:4], None, ALU.mult))
            v.scalar_tensor_tensor(out=sel[:], in0=two[:], scalar=sc[:, 4:5], in1=eq[:], op0=ALU.mult,
                                   op1=ALU.add).then_inc(chosen, 1)
            dve.wait_ge(turned, 1)
            v.tensor_copy(selt[:], ps[0:NPART, 1, 0:B]).then_inc(copied, 1)
            dve.wait_ge(spread, 1)
            then(v.tensor_copy(S.ew[:], ps[:, 2, 0:EXP * B]))
            then(v.scalar_tensor_tensor(out=S.ew[:], in0=S.ew[:], scalar=1e-6, in1=S.ew[:], op0=ALU.is_gt,
                                        op1=ALU.mult))
            then(v.tensor_scalar(S.eb[:], S.ew[:, 0:B], col(S, "moe_b2", 0), None, ALU.mult))
            for e in range(1, EXP):
                then(v.scalar_tensor_tensor(out=S.eb[:], in0=S.ew[:, e * B:(e + 1) * B], scalar=col(S, "moe_b2", e),
                                            in1=S.eb[:], op0=ALU.mult, op1=ALU.add))


def experts(nc, S, I):
    G = S.G
    N = EXP * EC
    HELD = 6
    LEAD = 4
    with ExitStack() as ctx:
        def sb(name, shape, dt=F32R):
            return ctx.enter_context(nc.sbuf_tensor(f"ex_{name}", shape, dt))

        w1h, w1l, w2h, w2l = (sb(x, [P, N * D]) for x in ("w1h", "w1l", "w2h", "w2l"))
        xh, xl = sb("xh", [P, 2, T]), sb("xl", [P, 2, T])
        g = sb("g", [P, HELD, T], F32)
        gh, gl = sb("gh", [P, HELD, T]), sb("gl", [P, HELD, T])
        up_ps = ctx.enter_context(nc.psum_tensor("ex_up_ps", [P, HELD, 512], F32))
        out_ps = ctx.enter_context(nc.psum_tensor("ex_out_ps", [P, 2, 512], F32))
        w_high = ctx.enter_context(nc.semaphore("ex_w_high"))
        w_low = ctx.enter_context(nc.semaphore("ex_w_low"))
        s = signals(ctx, nc, "ex", xh=1, xl=1, up=N, gelu=N, high=N, low01=2 * EXP, low2=EXP, down=N, biased=2,
                    added=2 * EXP)
        block = ctx.enter_context(nc.Block())

        def wait_low(eng, n, c):
            e, part = c // EC, c % EC
            if part < 2:
                eng.wait_ge(s.low01.sem, s.low01.at(n, 2 * e + part + 1))
            else:
                eng.wait_ge(s.low2.sem, s.low2.at(n, e + 1))

        def in_pairs(eng, group):
            with eng.Fori(0, G // 2 - 1) as i:
                for p in range(2):
                    group(2 * i + p, p, True)
            group(G - 2, 0, True)
            group(G - 1, 1, False)

        @block.tensor
        def _(pe):
            for sig in (s.up, s.down):
                sig.seed(pe)

            def three(out, high, low, rows_h, rows_l, first, last):
                nc.tensor.matmul(out, high, rows_h, start=first, stop=False)
                nc.tensor.matmul(out, high, rows_l, start=False, stop=False)
                return nc.tensor.matmul(out, low, rows_h, start=False, stop=last)

            def up(n, p, c):
                if c == 0:
                    pe.wait_ge(s.xh.sem, s.xh.at(n))
                    pe.wait_ge(s.xl.sem, s.xl.at(n))
                pe.wait_ge(s.gelu.sem, s.gelu.at(n, c + 1 - HELD))
                w = slice(c * D, (c + 1) * D)
                three(up_ps[:, c % HELD, 0:T], w1h[:, w], w1l[:, w], xh[:, p], xl[:, p], True, True)\
                    .then_inc(s.up.sem, 1)

            def down(n, c):
                e, part = c // EC, c % EC
                if part == 0:
                    pe.wait_ge(s.added.sem, s.added.at(n, 2 * (e + 1) - 4))
                pe.wait_ge(s.high.sem, s.high.at(n, c + 1))
                wait_low(pe, n, c)
                w = slice(c * D, (c + 1) * D)
                three(out_ps[:, e % 2, 0:T], w2h[:, w], w2l[:, w], gh[:, c % HELD], gl[:, c % HELD], part == 0,
                      part == EC - 1).then_inc(s.down.sem, 1)

            def group(n, p, first=False):
                for c in range(N):
                    up(n, p, c)
                    if c >= LEAD:
                        down(n, c - LEAD)
                    elif not first:
                        down(n - 1, N + c - LEAD)

            pe.wait_ge(w_high, 2)
            pe.wait_ge(w_low, 2)
            group(0, 0, first=True)
            group(1, 1)
            with pe.Fori(1, G // 2) as i:
                for p in range(2):
                    group(2 * i + p, p)
            for c in range(N - LEAD, N):
                down(G - 1, c)

        @block.scalar
        def _(act):
            s.gelu.seed(act)
            s.xh.seed(act)

            def split_x(n, p):
                act.wait_ge(s.up.sem, s.up.at(n - 2))
                xn = S.X[:, bass.ds(n * XP, XP)].rearrange("q (b t) -> q b t", b=PAIR)[:, :, 3:PADL]
                nc.scalar.activation(xh[:, p].rearrange("q (b t) -> q b t", b=PAIR), xn, ACT.Copy).then_inc(s.xh.sem, 1)

            def group(n, p, ahead):
                for c in range(N):
                    act.wait_ge(s.up.sem, s.up.at(n, c + 1))
                    wait_low(act, n, c - HELD)
                    nc.scalar.activation(g[:, c % HELD], up_ps[:, c % HELD, 0:T], ACT.Gelu, bias=col(S, "moe_b1", c))\
                        .then_inc(s.gelu.sem, 1)
                    if c == N // 2 and ahead:
                        split_x(n + 1, 1 - p)

            nc.scalar.activation(w1h[:], S.mw1[:], ACT.Copy).then_inc(w_high, 1)
            split_x(0, 0)
            nc.scalar.activation(w2h[:], S.mw2[:], ACT.Copy).then_inc(w_high, 1)
            in_pairs(act, group)

        @block.gpsimd
        def _(pool):
            for sig in (s.xl, s.low01):
                sig.seed(pool)

            def split_x(n, p):
                pool.wait_ge(s.xh.sem, s.xh.at(n))
                pool.wait_ge(s.up.sem, s.up.at(n - 2))
                halves = lambda ap: ap.rearrange("q (b t) -> q b t", b=PAIR)
                xn = halves(S.X[:, bass.ds(n * XP, XP)])[:, :, 3:PADL]
                nc.gpsimd.tensor_tensor(halves(xl[:, p]), xn, halves(xh[:, p]), ALU.subtract).then_inc(s.xl.sem, 1)

            def group(n, p, ahead):
                for c in range(N):
                    if c % EC < 2:
                        pool.wait_ge(s.high.sem, s.high.at(n, c + 1))
                        pool.wait_ge(s.down.sem, s.down.at(n, c + 1 - HELD))
                        nc.gpsimd.tensor_tensor(gl[:, c % HELD], g[:, c % HELD], gh[:, c % HELD], ALU.subtract)\
                            .then_inc(s.low01.sem, 1)
                    elif c == N // 2 + 2 and ahead:
                        split_x(n + 1, 1 - p)

            split_x(0, 0)
            in_pairs(pool, group)

        @block.vector
        def _(dve):
            for sig in (s.added, s.biased, s.high, s.low2):
                sig.seed(dve)

            def add(n, e):
                dve.wait_ge(s.down.sem, s.down.at(n, (e + 1) * EC))
                h_of = lambda b: S.h[:, bass.ds(n * T + b * L, L)]
                if e == 0:
                    for b in range(PAIR):
                        nc.vector.tensor_scalar(h_of(b), h_of(b), S.eb[:, bass.ds(n * PAIR + b, 1)], None, ALU.add)\
                            .then_inc(s.biased.sem, 1)
                    dve.wait_ge(s.biased.sem, s.biased.at(n))
                else:
                    dve.wait_ge(s.added.sem, s.added.at(n, 2 * e))
                for b in range(PAIR):
                    nc.vector.scalar_tensor_tensor(
                        out=h_of(b), in0=out_ps[:, e % 2, b * L:(b + 1) * L],
                        scalar=S.ew[:, bass.ds(n * PAIR + b + e * S.B, 1)], in1=h_of(b), op0=ALU.mult,
                        op1=ALU.add).then_inc(s.added.sem, 1)

            def group(n, p, ahead, first=False):
                for c in range(N):
                    dve.wait_ge(s.gelu.sem, s.gelu.at(n, c + 1))
                    dve.wait_ge(s.down.sem, s.down.at(n, c + 1 - HELD))
                    nc.vector.tensor_copy(gh[:, c % HELD], g[:, c % HELD]).then_inc(s.high.sem, 1)
                    if c % EC == 2:
                        dve.wait_ge(s.high.sem, s.high.at(n, c + 1))
                        nc.vector.tensor_tensor(gl[:, c % HELD], g[:, c % HELD], gh[:, c % HELD], ALU.subtract)\
                            .then_inc(s.low2.sem, 1)
                    k = c - LEAD - 1
                    if k % EC == EC - 1:
                        if k >= 0:
                            add(n, k // EC)
                        elif not first:
                            add(n - 1, EXP + k // EC)

            for w, (raw, high, low) in enumerate(((S.mw1, w1h, w1l), (S.mw2, w2h, w2l))):
                dve.wait_ge(w_high, w + 1)
                nc.vector.tensor_tensor(low[:], raw[:], high[:], ALU.subtract).then_inc(w_low, 1)
            group(0, 0, True, first=True)
            group(1, 1, True)
            with dve.Fori(1, G // 2) as i:
                for p in range(2):
                    group(2 * i + p, p, True)
            add(G - 1, EXP - 2)
            add(G - 1, EXP - 1)


def spectrum(nc, S, I):
    G, B = S.G, S.B
    L2 = L - P
    with ExitStack() as ctx:
        def sb(name, shape):
            return ctx.enter_context(nc.sbuf_tensor(f"sp_{name}", shape, F32))
        dft = sb("dft", [P, 2, 3 * MODES])
        sq, rec, y = (sb(x, [P, 2, T]) for x in ("sq", "rec", "y"))
        yt = sb("yt", [P, PAIR, 2, D])
        cen_ps, var_ps, t_ps, f_ps = (ctx.enter_context(nc.psum_tensor(f"sp_{x}", [P, 2, 512], F32))
                                      for x in ("cen_ps", "var_ps", "t_ps", "f_ps"))
        loaded = ctx.enter_context(nc.semaphore("sp_loaded"))
        s = signals(ctx, nc, "sp", cen=1, sq=1, var=1, log=1, rec=1, y=1, turn=2, yt=2, freq=2, q=2)
        block = ctx.enter_context(nc.Block())
        Qv = S.Q[:].rearrange("q (m c b) -> q c m b", m=MODES, c=3)

        @block.sync
        def _(sp):
            sp.dma_start(dft[:, 0], I.dft[0:P]).then_inc(loaded, 16)
            sp.dma_start(dft[0:L2, 1], I.dft[P:L]).then_inc(loaded, 16)

        @block.tensor
        def _(pe):
            for sig in (s.cen, s.var, s.turn, s.freq):
                sig.seed(pe)
            pe.wait_ge(loaded, 32)

            def center(n, p):
                pe.wait_ge(s.y.sem, s.y.at(n - 2))
                nc.tensor.matmul(cen_ps[:, p, 0:T], S.center[:], S.h[:, bass.ds(n * T, T)], start=True, stop=True)\
                    .then_inc(s.cen.sem, 1)

            def variance(n, p):
                pe.wait_ge(s.sq.sem, s.sq.at(n))
                pe.wait_ge(s.log.sem, s.log.at(n - 2))
                nc.tensor.matmul(var_ps[:, p, 0:T], S.mean[:], sq[:, p], start=True, stop=True).then_inc(s.var.sem, 1)

            def turn(n, p):
                pe.wait_ge(s.y.sem, s.y.at(n))
                for b in range(PAIR):
                    pe.wait_ge(s.yt.sem, s.yt.at(n - 1, b + 1))
                    nc.tensor.transpose(t_ps[:, b, 0:D], y[:, p, b * L:b * L + P], S.ident[:])
                    nc.tensor.transpose(t_ps[0:L2, b, D:2 * D], y[:, p, b * L + P:(b + 1) * L], S.ident[:])\
                        .then_inc(s.turn.sem, 1)

            def transform(n):
                for b in range(PAIR):
                    pe.wait_ge(s.yt.sem, s.yt.at(n, b + 1))
                    pe.wait_ge(s.q.sem, s.q.at(n - 1, b + 1))
                    nc.tensor.matmul(f_ps[:, b, 0:3 * MODES], yt[:, b, 0], dft[:, 0], start=True, stop=False)
                    nc.tensor.matmul(f_ps[:, b, 0:3 * MODES], yt[0:L2, b, 1], dft[0:L2, 1], start=False, stop=True)\
                        .then_inc(s.freq.sem, 1)

            center(0, 0)
            variance(0, 0)
            center(1, 1)

            with pe.Fori(0, G // 2 - 1) as i:
                for p in range(2):
                    n = 2 * i + p
                    turn(n, p)
                    variance(n + 1, 1 - p)
                    transform(n)
                    center(n + 2, p)
            for p in range(2):
                n = G - 2 + p
                turn(n, p)
                if p == 0:
                    variance(n + 1, 1)
                transform(n)

        @block.scalar
        def _(act):
            for sig in (s.sq, s.log, s.rec, s.q):
                sig.seed(act)
            act.preload_act_table_set(LOG_EXP)

            def squares(n, p):
                act.wait_ge(s.cen.sem, s.cen.at(n))
                act.wait_ge(s.var.sem, s.var.at(n - 2))
                nc.scalar.activation(sq[:, p], cen_ps[:, p, 0:T], ACT.Square).then_inc(s.sq.sem, 1)

            def inverse_root(n, p):
                act.wait_ge(s.var.sem, s.var.at(n))
                act.wait_ge(s.y.sem, s.y.at(n - 2))
                nc.scalar.activation(rec[:, p], var_ps[:, p, 0:T], ACT.Ln, bias=S.eps[:]).then_inc(s.log.sem, 1)
                act.wait_ge(s.log.sem, s.log.at(n))
                nc.scalar.activation(rec[:, p], rec[:, p], ACT.Exp, scale=-0.5).then_inc(s.rec.sem, 1)

            def store(n):
                for b in range(PAIR):
                    act.wait_ge(s.freq.sem, s.freq.at(n, b + 1))
                    nc.scalar.activation(Qv[:, :, :, bass.ds(n * PAIR + b, 1)],
                                         f_ps[:, b, 0:3 * MODES].rearrange("q (c m o) -> q c m o", c=3, o=1), ACT.Copy)\
                        .then_inc(s.q.sem, 1)

            squares(0, 0)
            inverse_root(0, 0)
            squares(1, 1)
            with act.Fori(0, G // 2 - 1) as i:
                for p in range(2):
                    n = 2 * i + p
                    inverse_root(n + 1, 1 - p)
                    squares(n + 2, p)
                    store(n)
            inverse_root(G - 1, 1)
            store(G - 2)
            store(G - 1)

        @block.vector
        def _(dve):
            for sig in (s.y, s.yt):
                sig.seed(dve)
            with dve.Fori(0, G // 2) as i:
                for p in range(2):
                    n = 2 * i + p
                    dve.wait_ge(s.rec.sem, s.rec.at(n))
                    dve.wait_ge(s.turn.sem, s.turn.at(n - 2))
                    nc.vector.tensor_tensor(y[:, p], cen_ps[:, p, 0:T], rec[:, p], ALU.mult).then_inc(s.y.sem, 1)
                    for b in range(PAIR):
                        dve.wait_ge(s.turn.sem, s.turn.at(n, b + 1))
                        dve.wait_ge(s.freq.sem, s.freq.at(n - 1, b + 1))
                        nc.vector.tensor_copy(yt[:, b, 0], t_ps[:, b, 0:D])
                        nc.vector.tensor_copy(yt[0:L2, b, 1], t_ps[0:L2, b, D:2 * D]).then_inc(s.yt.sem, 1)


def mix(nc, S, I):
    B = S.B
    NB = MODES // MB
    with ExitStack() as ctx:
        w = ctx.enter_context(nc.sbuf_tensor("mx_w", [P, 4, MB, 2, D], F32))
        ps = ctx.enter_context(nc.psum_tensor("mx_ps", [P, 4, 512], F32))
        wl = [Signal(ctx, nc, f"mx_wl{p}", 1, 16) for p in range(4)]
        s = signals(ctx, nc, "mx", mul=4, o=4)
        block = ctx.enter_context(nc.Block())
        Ov = S.O[:].rearrange("q (b c m) -> q m c b", c=2, m=MODES)

        @block.sync
        def _(sp):
            for p in range(4):
                wl[p].seed(sp)
            with sp.Fori(0, NB // 4) as i:
                for p in range(4):
                    sp.wait_ge(s.mul.sem, s.mul.at(i, p + 1 - 4))
                    sp.dma_start(w[:, p].rearrange("q m c e -> q (m c e)"),
                                   I.modes_w[bass.ds(4 * i + p, 1)].rearrange("o q t -> (o q) t"))\
                        .then_inc(wl[p].sem, 16)

        @block.tensor
        def _(pe):
            s.mul.seed(pe)
            with pe.Fori(0, NB // 4) as i:
                for p in range(4):
                    pe.wait_ge(wl[p].sem, wl[p].at(i))
                    pe.wait_ge(s.o.sem, s.o.at(i, p + 1 - 4))
                    for m in range(MB):
                        out = ps[:, p, m * 2 * B:(m + 1) * 2 * B]
                        at = ((4 * i + p) * MB + m) * 3 * B
                        nc.tensor.matmul(out, w[:, p, m, 0], S.Q[:, bass.ds(at + B, 2 * B)], start=True, stop=False,
                                         skip_group_check=True)
                        mm = nc.tensor.matmul(out, w[:, p, m, 1], S.Q[:, bass.ds(at, 2 * B)], start=False, stop=True,
                                              skip_group_check=True)
                    mm.then_inc(s.mul.sem, 1)

        @block.vector
        def _(dve):
            s.o.seed(dve)
            with dve.Fori(0, NB // 4) as i:
                for p in range(4):
                    dve.wait_ge(s.mul.sem, s.mul.at(i, p + 1))
                    nc.vector.tensor_copy(Ov[:, bass.ds((4 * i + p) * MB, MB)],
                                          ps[:, p, 0:MB * 2 * B].rearrange("q (m c b) -> q m c b", m=MB, c=2))\
                        .then_inc(s.o.sem, 1)


def finish(nc, S, I, out):
    G = S.G
    with ExitStack() as ctx:
        def sb(name, shape):
            return ctx.enter_context(nc.sbuf_tensor(f"fi_{name}", shape, F32))
        idft = sb("idft", [P, L])
        of = sb("of", [P, PAIR, P])
        ot = sb("ot", [P, PAIR, D])
        sq, rec, nrm, res = (sb(x, [P, 2, T]) for x in ("sq", "rec", "nrm", "res"))
        t_ps, i_ps, cen_ps, var_ps = (ctx.enter_context(nc.psum_tensor(f"fi_{x}", [P, 2, 512], F32))
                                      for x in ("t_ps", "i_ps", "cen_ps", "var_ps"))
        loaded = ctx.enter_context(nc.semaphore("fi_loaded"))
        s = signals(ctx, nc, "fi", of=1, turn=1, ot=1, inv=1, hv=1, cen=1, sq=1, var=1, log=1, rec=1, nrm=1, res=1)
        stored = [Signal(ctx, nc, f"fi_stored{p}", 1, 16) for p in range(2)]
        block = ctx.enter_context(nc.Block())

        @block.sync
        def _(sp):
            for p in range(2):
                stored[p].seed(sp)
            sp.dma_start(idft[:], I.idft).then_inc(loaded, 16)
            with sp.Fori(0, G // 2) as i:
                for p in range(2):
                    sp.wait_ge(s.res.sem, s.res.at(2 * i + p))
                    sp.dma_start(out[bass.ds(2 * i + p, 1)].rearrange("o q t -> (o q) t"), res[:, p])\
                        .then_inc(stored[p].sem, 16)
            for p in range(2):
                sp.wait_ge(stored[p].sem, stored[p].at(G // 2 - 1))

        def h_of(n):
            return S.h[:, bass.ds(n * T, T)]

        LEAD = 3

        @block.tensor
        def _(pe):
            for sig in (s.turn, s.inv, s.cen, s.var):
                sig.seed(pe)

            def step(n, i, p, live):
                if live(0):
                    pe.wait_ge(s.sq.sem, s.sq.at(n))
                    pe.wait_ge(s.log.sem, s.log.at(n - 2))
                    nc.tensor.matmul(var_ps[:, p, 0:T], S.mean[:], sq[:, p], start=True, stop=True)\
                        .then_inc(s.var.sem, 1)
                if live(2):
                    pe.wait_ge(s.ot.sem, s.ot.at(n + 2))
                    pe.wait_ge(s.hv.sem, s.hv.at(n))
                    for b in range(PAIR):
                        mm = nc.tensor.matmul(i_ps[:, p, b * L:(b + 1) * L], ot[:, b], idft[:], start=True, stop=True)
                    mm.then_inc(s.inv.sem, 1)
                if live(1):
                    pe.wait_ge(s.hv.sem, s.hv.at(n + 1))
                    pe.wait_ge(s.nrm.sem, s.nrm.at(n - 1))
                    nc.tensor.matmul(cen_ps[:, 1 - p, 0:T], S.center[:], h_of(n + 1), start=True, stop=True)\
                        .then_inc(s.cen.sem, 1)
                if live(3):
                    pe.wait_ge(s.of.sem, s.of.at(n + 3))
                    pe.wait_ge(s.ot.sem, s.ot.at(n + 1))
                    for b in range(PAIR):
                        mm = nc.tensor.transpose(t_ps[:, 1 - p, b * D:(b + 1) * D], of[:, b], S.ident[:])
                    mm.then_inc(s.turn.sem, 1)

            pe.wait_ge(loaded, 16)
            in_stages(pe, G, LEAD, step)

        @block.scalar
        def _(act):
            for sig in (s.ot, s.sq, s.log, s.rec):
                sig.seed(act)

            def step(n, i, p, live):
                if live(0):
                    act.wait_ge(s.var.sem, s.var.at(n))
                    act.wait_ge(s.nrm.sem, s.nrm.at(n - 2))
                    nc.scalar.activation(rec[:, p], var_ps[:, p, 0:T], ACT.Ln, bias=S.eps[:]).then_inc(s.log.sem, 1)
                    act.wait_ge(s.log.sem, s.log.at(n))
                    nc.scalar.activation(rec[:, p], rec[:, p], ACT.Exp, scale=-0.5).then_inc(s.rec.sem, 1)
                if live(1):
                    act.wait_ge(s.cen.sem, s.cen.at(n + 1))
                    act.wait_ge(s.var.sem, s.var.at(n - 1))
                    nc.scalar.activation(sq[:, 1 - p], cen_ps[:, 1 - p, 0:T], ACT.Square).then_inc(s.sq.sem, 1)
                if live(3):
                    act.wait_ge(s.turn.sem, s.turn.at(n + 3))
                    act.wait_ge(s.inv.sem, s.inv.at(n + 2))
                    nc.scalar.activation(ot[:], t_ps[:, 1 - p, 0:PAIR * D].rearrange("q (b e) -> q b e", b=PAIR),
                                         ACT.Copy).then_inc(s.ot.sem, 1)

            act.preload_act_table_set(LOG_EXP)
            in_stages(act, G, LEAD, step)

        @block.gpsimd
        def _(pool):
            for sig in (s.of, s.res):
                sig.seed(pool)

            def step(n, i, p, live):
                if live(3):
                    pool.wait_ge(s.turn.sem, s.turn.at(n + 2))
                    nc.gpsimd.tensor_copy(of[:].rearrange("q b m -> q (b m)"),
                                          S.O[:, bass.ds((n + 3) * PAIR * P, PAIR * P)]).then_inc(s.of.sem, 1)
                if live(0):
                    pool.wait_ge(s.nrm.sem, s.nrm.at(n))
                    pool.wait_ge(stored[p].sem, stored[p].at(i - 1))
                    nc.gpsimd.tensor_tensor(res[:, p], nrm[:, p], h_of(n), ALU.add).then_inc(s.res.sem, 1)

            in_stages(pool, G, LEAD, step)

        @block.vector
        def _(dve):
            for sig in (s.hv, s.nrm):
                sig.seed(dve)

            def step(n, i, p, live):
                if live(0):
                    dve.wait_ge(s.rec.sem, s.rec.at(n))
                    dve.wait_ge(s.res.sem, s.res.at(n - 2))
                    nc.vector.tensor_tensor(nrm[:, p], cen_ps[:, p, 0:T], rec[:, p], ALU.mult).then_inc(s.nrm.sem, 1)
                if live(2):
                    dve.wait_ge(s.inv.sem, s.inv.at(n + 2))
                    nc.vector.tensor_tensor(h_of(n + 2), h_of(n + 2), i_ps[:, p, 0:T], ALU.add).then_inc(s.hv.sem, 1)

            in_stages(dve, G, LEAD, step)


def vit_tower(nc, I, out):
    G = I.pixels.shape[0]
    B = G * PAIR
    with ExitStack() as ctx:
        def sb(name, shape, dt=F32):
            return ctx.enter_context(nc.sbuf_tensor(name, shape, dt))

        S = Shared()
        S.G, S.B = G, B
        S.center, S.mean, S.ident = sb("center", [P, D]), sb("mean", [P, D]), sb("ident", [P, D])
        S.cols, S.eps, S.past_edge = sb("cols", [P, NCOLS]), sb("eps", [P, 1]), sb("past_edge", [P, 1])
        S.h = sb("h", [P, B * L])
        S.sums = sb("sums", [P, B])
        S.tok_bias_c, S.ffn_b2_c, S.ffn_b2_cg = sb("tok_bias_c", [P, 1]), sb("ffn_b2_c", [P, 1]), sb("ffn_b2_cg", [P, 1])
        S.g_half, S.b_half = sb("g_half", [P, 2]), sb("b_half", [P, 1])
        S.conv_b_half, S.skip_half = sb("conv_b_half", [P, 2, 2]), sb("skip_half", [P, 2, 2])
        with ExitStack() as held:
            S.X = held.enter_context(nc.sbuf_tensor("X", [P, B * PADL], F32))
            with ExitStack() as weights:
                def wt(name, shape, dt=F32):
                    return weights.enter_context(nc.sbuf_tensor(name, shape, dt))
                S.neg_a = wt("neg_a", [P, 2, 2, NS])
                S.sel = wt("sel", [96, 2 * NS], BF16)
                S.convw, S.zw = wt("convw", [P, 2, TAPS, 2 * D]), wt("zw", [P, 2, 2 * D])
                S.xpw, S.dtw = wt("xpw", [P, 2, 2, 96 + R]), wt("dtw", [P, 2, 2 * D])
                S.woc, S.w1, S.w2c = wt("woc", [P, 4 * D]), wt("w1", [P, FF * D]), wt("w2c", [P, FF * D])
                setup(nc, S, I)
                tokens(nc, S, I)
                mamba(nc, S, I)
            with ExitStack() as weights:
                S.ew = weights.enter_context(nc.sbuf_tensor("ew", [P, EXP * B], F32))
                S.eb = weights.enter_context(nc.sbuf_tensor("eb", [P, B], F32))
                S.mw1 = weights.enter_context(nc.sbuf_tensor("mw1", [P, EXP * EC * D], F32))
                S.mw2 = weights.enter_context(nc.sbuf_tensor("mw2", [P, EXP * EC * D], F32))
                route(nc, S, I)
                experts(nc, S, I)
        S.O = sb("O", [P, B * 2 * MODES])
        with ExitStack() as held:
            S.Q = held.enter_context(nc.sbuf_tensor("Q", [P, MODES * 3 * B], F32))
            spectrum(nc, S, I)
            mix(nc, S, I)
        finish(nc, S, I, out)


def laid_out(x):
    f = lambda a: np.ascontiguousarray(np.asarray(a))
    B = x["x"].shape[0]
    G = B // PAIR
    m = {}
    m["pixels"] = x["x"].reshape(G, PAIR, 3, GRID, 2, 8, GRID, 2, 8).transpose(0, 7, 5, 8, 2, 4, 1, 3, 6)\
        .reshape(G, P, CH * TP)
    wm = x["L0_tok_W_main"].reshape(64, 3, 2, 8, 2, 8)
    wx = x["L0_tok_W_sx"].reshape(16, 3, 2, 8, 2, 8)
    wy = x["L0_tok_W_sy"].reshape(16, 3, 2, 8, 2, 8)
    w = np.zeros((3, D, 3, 2, 2, 8, 8), np.float32)
    at = lambda a: a.transpose(0, 1, 2, 4, 3, 5)
    w[0, 0:64] = at(wm)
    w[0, 64:80, :, :, 1] = at(wx)[:, :, :, 0]
    w[0, 80:96, :, :, 0] = at(wx)[:, :, :, 1]
    w[1, 64:80, :, :, 0] = at(wx)[:, :, :, 1]
    w[1, 80:96, :, :, 1] = at(wx)[:, :, :, 0]
    w[0, 96:112, :, 1] = at(wy)[:, :, 0]
    w[0, 112:128, :, 0] = at(wy)[:, :, 1]
    w[2, 96:112, :, 0] = at(wy)[:, :, 1]
    w[2, 112:128, :, 1] = at(wy)[:, :, 0]
    m["tok_w"] = w.transpose(1, 0, 2, 3, 4, 5, 6).reshape(D, 3 * CH, D)
    m["center"] = (np.eye(D) - 1.0 / D).astype(np.float32)
    m["mean"] = np.full((D, D), 1.0 / D, np.float32)
    m["ident"] = np.eye(D, dtype=np.float32)
    m["sel"] = np.tile(np.eye(2 * NS, dtype=np.float32), (3, 1))
    cols = {"tok_bias": np.concatenate([x["L0_tok_b_main"]] + [x["L0_tok_b_sx"]] * 2 + [x["L0_tok_b_sy"]] * 2),
            "tok_g": x["L0_tok_ln_g"], "tok_b": x["L0_tok_ln_b"], "cls": x["cls_tok"].reshape(D),
            "ff_g": x["L0_attn_ln_ff_g"], "ff_b": x["L0_attn_ln_ff_b"],
            "ffn_b1": x["L0_attn_ffn_b1"].reshape(FF, D).T, "ffn_b2": x["L0_attn_ffn_b2"],
            "moe_b2": x["L0_ffn_b2"].T}
    f1 = x["L0_ffn_W1"].shape[2]
    b1 = np.zeros((EXP, EC * D), np.float32)
    b1[:, :f1] = x["L0_ffn_b1"]
    cols["moe_b1"] = b1.reshape(EXP * EC, D).T
    for d, k in enumerate("fb"):
        a = lambda v: x[f"L0_attn_{k}_{v}"]
        cols[f"conv_b{d}"] = a("conv_b").reshape(2, D).T
        cols[f"skip{d}"] = a("D").reshape(2, D).T
        cols[f"dt_b{d}"] = a("dt_b").reshape(2, D).T
        cols[f"a_log{d}"] = a("A_log").reshape(2, D, NS).transpose(1, 0, 2).reshape(D, 2 * NS)
        cols[f"ln_g{d}"] = x[f"L0_attn_ln_{k}_g"]
        cols[f"ln_b{d}"] = x[f"L0_attn_ln_{k}_b"]
    m["cols"] = np.concatenate([np.asarray(cols[k]).reshape(D, wd) for k, (_, wd) in COLS.items()], axis=1)
    both = lambda g: np.stack([g(x, k) for k in "fb"], axis=1)
    m["out_w"] = both(lambda x, k: x[f"L0_attn_{k}_out_w"])
    m["ffn_w2"] = x["L0_attn_ffn_w2"]
    m["in_w_x"] = both(lambda x, k: x[f"L0_attn_{k}_in_w"].T[:, :2 * D])
    m["in_w_z"] = both(lambda x, k: x[f"L0_attn_{k}_in_w"].T[:, 2 * D:])
    m["taps"] = np.broadcast_to(both(lambda x, k: x[f"L0_attn_{k}_conv_w"].T[None])[0], (P, 2, TAPS, 2 * D))

    def xproj(x, k):
        v = x[f"L0_attn_{k}_xproj_w"]
        v = np.concatenate([v[R:]] * 3 + [v[:R]], axis=0)
        return v.T.reshape(2, D, 96 + R).transpose(1, 0, 2)
    m["xproj"] = both(xproj)
    m["dt_w"] = both(lambda x, k: x[f"L0_attn_{k}_dt_w"].T)
    m["ffn_w1"] = x["L0_attn_ffn_w1"].T
    w1 = np.zeros((EXP, D, EC * D), np.float32)
    w1[:, :, :f1] = x["L0_ffn_W1"]
    m["moe_w1"] = w1.transpose(1, 0, 2).reshape(D, EXP * EC * D)
    w2 = np.zeros((EXP, EC * D, D), np.float32)
    w2[:, :f1] = x["L0_ffn_W2"]
    m["moe_w2"] = w2.reshape(EXP * EC, D, D).transpose(1, 0, 2).reshape(D, EXP * EC * D)
    m["router_w"] = x["L0_ffn_router_w"].T
    m["keys"] = np.broadcast_to(np.arange(NPART, 0, -1, dtype=np.float32), (P, NPART))
    parts = [(6,), (5, 1), (4, 2), (4, 1, 1), (3, 3), (3, 2, 1), (3, 1, 1, 1), (2, 2, 2), (2, 2, 1, 1),
             (2, 1, 1, 1, 1), (1, 1, 1, 1, 1, 1)]
    pw = np.zeros((NPART, EXP), np.float32)
    for i, part in enumerate(parts):
        pw[i, :len(part)] = [v / 6 for v in part]
    m["part_w"] = np.broadcast_to(pw[:, :, None], (NPART, EXP, D)).reshape(NPART, EXP * D)
    angle = 2 * np.pi * (np.outer(np.arange(L), np.arange(MODES)) % L) / L
    m["dft"] = np.concatenate([np.sin(angle), np.cos(angle), -np.sin(angle)], axis=1).astype(np.float32)
    twice = np.where(np.arange(MODES) == 0, 1.0, 2.0)[:, None] / L
    m["idft"] = np.concatenate([np.cos(angle).T * twice, -np.sin(angle).T * twice]).astype(np.float32)
    wr, wi = x["L1_attn_weights_real"], x["L1_attn_weights_imag"]
    m["modes_w"] = np.stack([wr, wi]).transpose(3, 1, 0, 2).reshape(MODES // MB, MB, D, 2, D)\
        .transpose(0, 2, 1, 3, 4).reshape(MODES // MB, D, MB * 2 * D)
    return {k: f(v) for k, v in m.items()}


def kernel(**inputs):
    import concourse.bacc as bacc
    from concourse.bass_utils import run_bass_kernel_spmd as run

    arrays = {f"in_{k}": v for k, v in laid_out({k: np.asarray(v) for k, v in inputs.items()}).items()}
    nc = bacc.Bacc("TRN2", target_bir_lowering=False, num_devices=1)
    given = [nc.dram_tensor(k, v.shape, mybir.dt.from_np(v.dtype), kind="ExternalInput").ap() for k, v in arrays.items()]
    I = namedtuple("Inputs", [k[3:] for k in arrays])(*given)
    G = arrays["in_pixels"].shape[0]
    out = nc.dram_tensor("out_0", (G, P, T), F32, kind="ExternalOutput").ap()
    vit_tower(nc, I, out)
    got = run(nc, [arrays], core_ids=[0]).results[0]["out_0"]
    return got.reshape(G, D, PAIR, L).transpose(0, 2, 3, 1).reshape(G * PAIR, L, D)
```
